# Optimizing a Trainium2 kernel written in Bass

```python
import numpy as np
import jax
import jax.numpy as jnp

def _softmax(x, axis=-1):
    return jax.nn.softmax(x, axis=axis)

def _gelu(x):
    return jax.nn.gelu(x, approximate=True)

def _silu(x):
    return jax.nn.silu(x)

def _sigmoid(x):
    return jax.nn.sigmoid(x)

def _layernorm(x, axis=-1, eps=1e-05):
    m = jnp.mean(x, axis=axis, keepdims=True)
    v = jnp.var(x, axis=axis, keepdims=True)
    return (x - m) / jnp.sqrt(v + eps)

def _scatter_add(tgt, idx, src, axis=0):
    return tgt.at[idx].add(src)

def _segment_sum(src, seg, n):
    return jax.ops.segment_sum(src, seg, n)
kernel_name = 'mk_adj_ffn_d2_adj_r2_3b0c02'

def setup_inputs(seed: int=0):
    np.random.seed(seed)
    _w = jnp.asarray

    def _rec_inputs():
        import jax
        import jax.numpy as jnp
        _gk = jax.random.key(seed)
        x = -0.0002928 + 1 * jax.random.normal(jax.random.fold_in(_gk, 1), (8, 1024, 128), jnp.float32)
        _w = (1.0 + jnp.arange(1024, dtype=jnp.float32)) ** (-0.5)
        _w = _w / _w.mean()
        _pij = jnp.clip(0.00195312 * _w[:, None] * _w[None, :], 0.0, 1.0)
        _a = jax.random.uniform(jax.random.fold_in(_gk, 2), (8, 1024, 1024)) < _pij
        adj = _a.astype(jnp.int32)
        return (x, adj)
    x, adj = _rec_inputs()

    def _L0_gnn_setup():
        import jax, jax.numpy as jnp
        import numpy as np
        B, N, DIN, DOUT = (16, 512, 128, 128)
        NEG_SLOPE = 0.2
        key = jax.random.key(seed)
        k1, k2, k3, k4 = jax.random.split(key, 4)
        h = jax.random.normal(k1, (B, N, DIN), dtype=jnp.float32)
        adj_mask = jax.random.randint(k2, (B, N, N), 0, 2, dtype=jnp.int32)
        W = jax.random.normal(k3, (DOUT, DIN), dtype=jnp.float32) * (1.0 / np.sqrt(DIN))
        a = jax.random.normal(k4, (2 * DOUT,), dtype=jnp.float32) * (1.0 / np.sqrt(2 * DOUT))
        return {'h': h, 'adj_mask': adj_mask, 'W': W, 'a': a}
    _L0_gnn_all = _L0_gnn_setup()
    _L0_gnn_in = {k: v for k, v in _L0_gnn_all.items() if k in ('W', 'a')}
    del _L0_gnn_all

    def _L0_ffn_setup():
        import jax, jax.numpy as jnp
        import numpy as np
        B, S, D, F, E, K = (8, 1024, 128, 512, 8, 2)
        key = jax.random.key(seed)
        ks = jax.random.split(key, 10)
        s = 0.02
        return {'x': jax.random.normal(ks[0], (B, S, D), dtype=jnp.float32), 'Wr': jax.random.normal(ks[1], (D, E), dtype=jnp.float32) * s, 'W1s': jax.random.normal(ks[2], (D, F), dtype=jnp.float32) * s, 'b1s': jnp.zeros((F,), dtype=jnp.float32), 'W2s': jax.random.normal(ks[3], (F, D), dtype=jnp.float32) * s, 'b2s': jnp.zeros((D,), dtype=jnp.float32), 'W1p': jax.random.normal(ks[4], (E, D, F), dtype=jnp.float32) * s, 'b1p': jnp.zeros((E, F), dtype=jnp.float32), 'W2p': jax.random.normal(ks[5], (E, F, D), dtype=jnp.float32) * s, 'b2p': jnp.zeros((E, D), dtype=jnp.float32)}
    _L0_ffn_all = _L0_ffn_setup()
    _L0_ffn_in = {k: v for k, v in _L0_ffn_all.items() if k in ('Wr', 'W1s', 'b1s', 'W2s', 'b2s', 'W1p', 'b1p', 'W2p', 'b2p')}
    del _L0_ffn_all

    def _L1_gnn_setup():
        import jax, jax.numpy as jnp
        import numpy as np
        B, S, D = (64, 256, 128)

        def _leaky(x):
            return jnp.where(x >= 0, x, 0.2 * x)
        key = jax.random.key(seed)
        k = jax.random.split(key, 6)
        stdv = 1.0 / np.sqrt(D)
        return {'hidden': jax.random.normal(k[0], (B, S, D), dtype=jnp.float32), 'adj': jax.random.randint(k[1], (B, S, S), 0, 5, dtype=jnp.int32), 'a0': jax.random.uniform(k[2], (D, 1), jnp.float32, -stdv, stdv), 'a1': jax.random.uniform(k[3], (D, 1), jnp.float32, -stdv, stdv), 'a2': jax.random.uniform(k[4], (D, 1), jnp.float32, -stdv, stdv), 'a3': jax.random.uniform(k[5], (D, 1), jnp.float32, -stdv, stdv), 'bias': jnp.zeros((D,), dtype=jnp.float32)}
    _L1_gnn_all = _L1_gnn_setup()
    _L1_gnn_in = {k: v for k, v in _L1_gnn_all.items() if k in ('a0', 'a1', 'a2', 'a3', 'bias')}
    del _L1_gnn_all

    def _L1_ffn_setup():
        import jax, jax.numpy as jnp
        import numpy as np
        D_MODEL = 128
        EXPERT_DIM = 256
        NUM_EXPERTS = 8
        TOP_K = 2
        SEQ_LEN = 1024
        BATCH = 2
        key = jax.random.key(seed)
        ks = jax.random.split(key, 8)
        s = 0.02
        x = jax.random.normal(ks[0], (SEQ_LEN, BATCH, D_MODEL), dtype=jnp.float32)
        Wg = jax.random.normal(ks[1], (D_MODEL, NUM_EXPERTS), dtype=jnp.float32) * s
        bg = jax.random.normal(ks[2], (NUM_EXPERTS,), dtype=jnp.float32) * s
        bias = jnp.zeros((NUM_EXPERTS,), dtype=jnp.float32)
        W1 = jax.random.normal(ks[3], (NUM_EXPERTS, D_MODEL, EXPERT_DIM), dtype=jnp.float32) * s
        b1 = jax.random.normal(ks[4], (NUM_EXPERTS, EXPERT_DIM), dtype=jnp.float32) * s
        W2 = jax.random.normal(ks[5], (NUM_EXPERTS, EXPERT_DIM, D_MODEL), dtype=jnp.float32) * s
        b2 = jax.random.normal(ks[6], (NUM_EXPERTS, D_MODEL), dtype=jnp.float32) * s
        return {'x': x, 'Wg': Wg, 'bg': bg, 'bias': bias, 'W1': W1, 'b1': b1, 'W2': W2, 'b2': b2}
    _L1_ffn_all = _L1_ffn_setup()
    _L1_ffn_in = {k: v for k, v in _L1_ffn_all.items() if k in ('Wg', 'bg', 'bias', 'W1', 'b1', 'W2', 'b2')}
    del _L1_ffn_all
    return {'x': x, 'adj': adj, 'L0_gnn_W': _L0_gnn_in['W'], 'L0_gnn_a': _L0_gnn_in['a'], 'L0_ffn_Wr': _L0_ffn_in['Wr'], 'L0_ffn_W1s': _L0_ffn_in['W1s'], 'L0_ffn_b1s': _L0_ffn_in['b1s'], 'L0_ffn_W2s': _L0_ffn_in['W2s'], 'L0_ffn_b2s': _L0_ffn_in['b2s'], 'L0_ffn_W1p': _L0_ffn_in['W1p'], 'L0_ffn_b1p': _L0_ffn_in['b1p'], 'L0_ffn_W2p': _L0_ffn_in['W2p'], 'L0_ffn_b2p': _L0_ffn_in['b2p'], 'L1_gnn_a0': _L1_gnn_in['a0'], 'L1_gnn_a1': _L1_gnn_in['a1'], 'L1_gnn_a2': _L1_gnn_in['a2'], 'L1_gnn_a3': _L1_gnn_in['a3'], 'L1_gnn_bias': _L1_gnn_in['bias'], 'L1_ffn_Wg': _L1_ffn_in['Wg'], 'L1_ffn_bg': _L1_ffn_in['bg'], 'L1_ffn_bias': _L1_ffn_in['bias'], 'L1_ffn_W1': _L1_ffn_in['W1'], 'L1_ffn_b1': _L1_ffn_in['b1'], 'L1_ffn_W2': _L1_ffn_in['W2'], 'L1_ffn_b2': _L1_ffn_in['b2']}

def reference(x, adj, L0_gnn_W, L0_gnn_a, L0_ffn_Wr, L0_ffn_W1s, L0_ffn_b1s, L0_ffn_W2s, L0_ffn_b2s, L0_ffn_W1p, L0_ffn_b1p, L0_ffn_W2p, L0_ffn_b2p, L1_gnn_a0, L1_gnn_a1, L1_gnn_a2, L1_gnn_a3, L1_gnn_bias, L1_ffn_Wg, L1_ffn_bg, L1_ffn_bias, L1_ffn_W1, L1_ffn_b1, L1_ffn_W2, L1_ffn_b2):
    import jax
    import jax.numpy as jnp

    def _L0_gnn_ref(h, adj_mask, W, a):
        import jax, jax.numpy as jnp
        import numpy as np
        B, N, DIN, DOUT = (16, 512, 128, 128)
        NEG_SLOPE = 0.2
        Wh = jnp.einsum('bnd,od->bno', h, W)
        d = Wh.shape[-1]
        a1, a2 = (a[:d], a[d:])
        ei = Wh @ a1
        ej = Wh @ a2
        e = ei[:, :, None] + ej[:, None, :]
        e = jnp.where(e > 0, e, NEG_SLOPE * e)
        e = jnp.where(adj_mask == 0, -jnp.inf, e)
        alpha = jax.nn.softmax(e, axis=-1)
        alpha = jnp.where(jnp.isnan(alpha), 0.0, alpha)
        h_out = jnp.einsum('bij,bjo->bio', alpha, Wh)
        return h_out

    def _L0_ffn_ref(x, Wr, W1s, b1s, W2s, b2s, W1p, b1p, W2p, b2p):
        import jax, jax.numpy as jnp
        import numpy as np
        B, S, D, F, E, K = (8, 1024, 128, 512, 8, 2)
        gelu = lambda t: jax.nn.gelu(t, approximate=False)
        shared = gelu(x @ W1s + b1s) @ W2s + b2s
        rw = jax.nn.softmax(x @ Wr, axis=-1)
        topw, topi = jax.lax.top_k(rw, K)
        topw = topw / jnp.sum(topw, axis=-1, keepdims=True)
        mask = jnp.sum(jax.nn.one_hot(topi, E, dtype=topw.dtype) * topw[..., None], axis=-2)
        h = gelu(jnp.einsum('bsd,edf->bsef', x, W1p) + b1p)
        priv = jnp.einsum('bsef,efd->bsed', h, W2p) + b2p
        routed = jnp.einsum('bsed,bse->bsd', priv, mask)
        return shared + routed

    def _L1_gnn_ref(hidden, adj, a0, a1, a2, a3, bias):
        import jax, jax.numpy as jnp
        import numpy as np
        B, S, D = (64, 256, 128)

        def _leaky(x):
            return jnp.where(x >= 0, x, 0.2 * x)
        h = hidden

        def e_of(a):
            return _leaky(jnp.einsum('bid,bjd->bij', h * a[:, 0], h))
        e0, e1, e2, e3 = (e_of(a0), e_of(a1), e_of(a2), e_of(a3))
        neg_inf = jnp.float32(-jnp.finfo(e0.dtype).max)
        alpha = jnp.where(adj == 1, e0, neg_inf)
        alpha = jnp.where(adj == 2, e1, alpha)
        alpha = jnp.where(adj == 3, e2, alpha)
        alpha = jnp.where(adj == 4, e3, alpha)
        alpha = jax.nn.sigmoid(alpha)
        return jnp.einsum('bij,bjd->bid', alpha, h) + bias

    def _L1_ffn_ref(x, Wg, bg, bias, W1, b1, W2, b2):
        import jax, jax.numpy as jnp
        import numpy as np
        D_MODEL = 128
        EXPERT_DIM = 256
        NUM_EXPERTS = 8
        TOP_K = 2
        SEQ_LEN = 1024
        BATCH = 2
        x_flat = x.reshape(-1, D_MODEL)
        gate_logits = x_flat @ Wg + bg + bias
        topk_vals, topk_idx = jax.lax.top_k(gate_logits, TOP_K)
        topk_w = jax.nn.softmax(topk_vals, axis=-1)
        combine = (jax.nn.one_hot(topk_idx, NUM_EXPERTS, dtype=x.dtype) * topk_w[..., None]).sum(axis=1)
        h = jax.nn.relu(jnp.einsum('td,edh->teh', x_flat, W1) + b1)
        y = jnp.einsum('teh,ehd->ted', h, W2) + b2
        out = jnp.einsum('ted,te->td', y, combine)
        return out.reshape(x.shape)
    x = x + _L0_gnn_ref(_layernorm(x, axis=-1), adj, L0_gnn_W, L0_gnn_a)
    x = x + _L0_ffn_ref(_layernorm(x, axis=-1), L0_ffn_Wr, L0_ffn_W1s, L0_ffn_b1s, L0_ffn_W2s, L0_ffn_b2s, L0_ffn_W1p, L0_ffn_b1p, L0_ffn_W2p, L0_ffn_b2p)
    x = x + _L1_gnn_ref(_layernorm(x, axis=-1), adj, L1_gnn_a0, L1_gnn_a1, L1_gnn_a2, L1_gnn_a3, L1_gnn_bias)
    x = x + _L1_ffn_ref(_layernorm(x, axis=-1), L1_ffn_Wg, L1_ffn_bg, L1_ffn_bias, L1_ffn_W1, L1_ffn_b1, L1_ffn_W2, L1_ffn_b2)
    return x

_drawn_inputs = setup_inputs


def setup_inputs(seed=0):
    import zlib

    import numpy as np

    out = dict(_drawn_inputs(seed))
    spreads = {'L0_ffn_b1s': (0.0, 0.1),
     'L0_ffn_b2s': (0.0, 0.1),
     'L0_ffn_b1p': (0.0, 0.433),
     'L0_ffn_b2p': (0.0, 0.1),
     'L1_gnn_bias': (0.0, 0.1),
     'L1_ffn_bias': (0.0, 0.578)}
    factors = {'L1_ffn_bg': 8.0, 'L1_ffn_W1': 2.805, 'L1_ffn_b1': 28.132, 'L1_ffn_b2': 5.797}
    for name, (base, spread) in spreads.items():
        noise = np.random.default_rng([zlib.crc32(name.encode()), seed]).standard_normal(out[name].shape)
        drawn = base * np.exp(spread * noise) if base else spread * noise
        out[name] = jnp.asarray(drawn.astype(out[name].dtype))
    for name, factor in factors.items():
        out[name] = (out[name] * factor).astype(out[name].dtype)
    return out
```

```python
import concourse.bass as bass
from concourse import mybir
from contextlib import ExitStack


def bass_two_layers_of_gnn_and_moe(
    nc: bass.Bass, x_in, adj_in, gnn_w, gnn_a, wr0, w1s, b1s, w2s, b2s, w1p, b1p, w2p, b2p,
    a0, a1, a2, a3, gbias, wg1, bg1, bias1, w1e, b1e, w2e, b2e, out,
):
    f32, f16, i32, u32 = mybir.dt.float32, mybir.dt.float16, mybir.dt.int32, mybir.dt.uint32
    ALU = mybir.AluOpType
    ACT = mybir.ActivationFunctionType
    AX = mybir.AxisListType
    ds = bass.ds

    P = 128
    B, N, D = x_in.shape
    TB = N // P
    T = B * TB
    NG = 2
    BG = B // NG
    TG = BG * TB
    E = wr0.shape[1]
    F = [w1s.shape[1], w1e.shape[2]]
    C = [f // P for f in F]
    SH = E
    NE = [E + 1, E]
    SPAN = 256
    ST = SPAN // P
    US = TG // ST
    NB = (2 * TG * P - E) // SPAN + E
    ROWS = NB * SPAN
    H = NB // 2
    NPAR = [H + 1, H]
    QG = TG // 4
    LEAK = 0.2
    NEG = -1e30
    FLOOR = -1e20
    EPS = 1e-5
    assert NB % 2 == 1 and US % 2 == 0
    NA = 4
    NCONST = 8
    NC = 17
    NPIECES = 2 * sum(NE)
    CR = NA

    ctx = ExitStack()
    with ctx:
        def sb(name, shape, dt):
            return ctx.enter_context(nc.sbuf_tensor(name, shape, dt))

        def sem(name):
            return ctx.enter_context(nc.semaphore(name))

        xn_d = nc.dram_tensor("xn_rows", (NG * TG * P, 2 * D), f16, kind="Internal").ap()
        xs_d = [nc.dram_tensor(f"block_in{g}", (ROWS, 2 * D), f16, kind="Internal").ap() for g in range(NG)]
        ys_d = [nc.dram_tensor(f"block_out{g}", (ROWS, D), f32, kind="Internal").ap() for g in range(NG)]
        slot_d = nc.dram_tensor("slots", (NG * P, TG * 2), i32, kind="Internal").ap()

        x = sb("x", [P, T * D], f32)
        ident = sb("ident", [P, P], f32)
        ident16 = sb("ident16", [P, P], f16)
        before = sb("before", [P, P], f16)
        ones16 = sb("ones16", [P, P], f16)
        ones_row = sb("ones_row", [1, P], f32)
        zero16 = sb("zero16", [P, 256], f16)
        rank = sb("rank", [P, E], f32)
        blockno = sb("blockno", [P, NB], f32)
        wcat = sb("wcat", [P, D], f32)
        wa = sb("wa", [P, 2], f32)
        wa2b = sb("wa2b", [P, P], f32)
        gacol = sb("gacol", [P, 2], f32)
        akcol = sb("akcol", [P, 4], f32)
        gbrow = sb("gbrow", [1, D], f32)
        wrf = sb("wrf", [P, 2, E], f32)
        wrs = sb("wrs", [P, 2, 2, E], f16)
        gateb = sb("gateb", [P, 2, ST, E], f32)
        gtmp = sb("gtmp", [P, 2, E], f32)
        w1sp = [sb(f"w1sp{l}", [P, NE[l] * 2 * F[l]], f16) for l in range(2)]
        w2sp = [sb(f"w2sp{l}", [P, NE[l] * C[l] * 2 * D], f16) for l in range(2)]
        b1 = [sb(f"b1_{l}", [P, NE[l] * C[l]], f32) for l in range(2)]
        b2b = [sb(f"b2b{l}", [P, NE[l] * D], f32) for l in range(2)]
        adjb = [sb(f"adjb{i}", [P, N], i32) for i in range(NA)]
        stats = sb("stats", [P, 8, 6], f32)
        mv8 = sb("mv8", [P, 16], f32)
        mv = sb("mv", [P, TG * 2], f32)
        std = sb("std", [P, TG], f32)
        rstd = sb("rstd", [P, TG], f32)
        stage = [sb(f"stage{i}", [P, TB * 2 * D], f16) for i in range(2)]
        idx = [sb(f"idx{i}", [P, TB * 2], i32) for i in range(2)]
        got = [sb(f"got{i}", [P, TB * D], f32) for i in range(2)]

        KB = 256
        arena = sb("arena", [P, 75 * KB], f32)

        def at(kb, n, dt=f32):
            a = arena[:, int(kb * KB):int(kb * KB) + (n if dt == f32 else n // 2)]
            return a if dt == f32 else a.bitcast(dt)

        vals = at(0, TG * D)
        ejb = at(16, BG * N)
        kT = at(16, 2 * TG * P, f16)
        qT = at(32, 2 * TG * P, f16)
        ejc = at(32, N)
        zt = [at(48 + 4 * i, N) for i in range(2)]
        pr = [at(56 + 4 * i, N) for i in range(2)]
        pT = [at(64 + 4 * i, N) for i in range(2)]
        xn4 = [at(48 + 2 * i, 4 * D) for i in range(2)]
        xT4 = [at(52 + 2 * i, 4 * P) for i in range(2)]
        qf = [at(56 + 2 * i, 4 * P) for i in range(2)]
        ei = at(72, TG)
        mrow = at(72.5, 2)
        t1 = at(72.75, 1)
        t2 = at(73, 1)
        nmax = at(73.25, 1)
        shift1 = at(74, 2)
        shift2 = at(74.25, 2)
        rsum = at(73.5, 4)
        rcp = at(73.75, 2)
        junk = at(36, N)
        gw = at(64, D)
        b1rows = [at(65 + l, P)[0:NE[l] * C[l], :] for l in range(2)]
        xf = [at(0 + i, ST * D) for i in range(2)]
        xb = [at(2 + i, ST * 2 * D, f16) for i in range(2)]
        xt = [at(4 + i, 2 * SPAN, f16) for i in range(2)]
        hf = [at(6 + 4 * i, 4 * SPAN) for i in range(2)]
        hs = [at(14 + 4 * i, 2 * 4 * SPAN, f16) for i in range(2)]
        ysb = [at(22 + i, ST * D) for i in range(2)]
        lg = at(24, TG * E)
        oh = [at(25 + i, TG * E) for i in range(2)]
        tm = [at(27 + i, TG * E) for i in range(3)]
        oh16 = at(30, TG * E, f16)
        cum = [at(31 + i, TG * E) for i in range(2)]
        mx = [at(33 + 0.25 * i, TG) for i in range(4)]
        small = at(34, 64)
        slf = at(35, 2 * TG)
        cmpb = at(36, NB * E)
        bef = at(38, NB)

        squares = sb("squares", [P, T], f32)
        worst = sb("worst", [P, 1], f32)
        other16 = sb("other16", [P, 1], f16)
        others = [sb(f"others{g}", [1, 1], i32) for g in range(NG)]
        minus_half = sb("minus_half", [P, 1], f32)
        codes = sb("codes", [P, 4], f32)
        wgt = sb("wgt", [P, NG * TG * 2], f32)
        sl = sb("sl", [P, TG * 2], i32)
        be = [sb(f"be{g}", [1, NB], i32) for g in range(NG)]
        nb_i = sb("nb_i", [P, E], i32)

        ps = [ctx.enter_context(nc.psum_tensor(f"ps{i}", [P, 1024], f32)) for i in range(4)]
        eP = ps[0]
        tP = [ps[1], ps[2]]
        vP = [ps[3][:, 0:P], ps[3][:, 512:512 + P]]
        xtP = [ps[0][:, 512 * i:512 * i + SPAN].bitcast(f16) for i in range(2)]
        lgP = [ps[0][:, 512 * i + 384:512 * i + 384 + ST * E] for i in range(2)]
        hP = [ps[1], ps[2]]
        yP = [ps[3][:, 512 * i:512 * i + ST * D] for i in range(2)]

        x_ld = [sem(f"x_ld{i}") for i in range(NG)]
        c_ld = sem("c_ld")
        w_ld = [sem(f"w_ld{i}") for i in range(2)]
        adj_ld = [sem(f"adj_ld{i}") for i in range(NA)]
        xs_zero = sem("xs_zero")
        xb_ld = [sem(f"xb_ld{i}") for i in range(2)]
        xb_st = [sem(f"xb_st{i}") for i in range(2)]
        ys_st = [sem(f"ys_st{i}") for i in range(2)]
        slot_st = sem("slot_st")
        st_ld = [sem(f"st_ld{i}") for i in range(2)]
        scat = [sem(f"scat{i}") for i in range(2)]
        gi_ld = [sem(f"gi_ld{i}") for i in range(2)]
        gath = [[sem(f"gath{i}{k}") for k in range(2)] for i in range(2)]
        o_st = sem("o_st")
        w_used, consts, pchain, chain = sem("w_used"), sem("consts"), sem("pchain"), sem("chain")
        prep_pe, prep_act, prep_dve = sem("prep_pe"), sem("prep_act"), sem("prep_dve")
        over, scat_all, blocks_out = sem("over"), sem("scat_all"), sem("blocks_out")
        var_rdy, std_rdy = sem("var_rdy"), sem("std_rdy")
        route_rdy, pos_rdy, w2_rdy, w2e_rdy, tbl_rdy = (sem("route_rdy"), sem("pos_rdy"), sem("w2_rdy"),
                                                        sem("w2e_rdy"), sem("tbl_rdy"))

        counted = []

        def unit(name):
            counted.append(sem(name))
            return counted[-1]

        xn4_rdy, xTp_rdy, xT_rdy, ebP_rdy, eb_used = (unit("xn4_rdy"), unit("xTp_rdy"), unit("xT_rdy"),
                                                      unit("ebP_rdy"), unit("eb_used"))
        whP_rdy, wh_used, qf_rdy, khi_rdy, kq_rdy, h_rdy = (unit("whP_rdy"), unit("wh_used"), unit("qf_rdy"),
                                                            unit("khi_rdy"), unit("kq_rdy"), unit("h_rdy"))
        ejc_rdy, mask_rdy, z_rdy, nm_step, nmax_rdy = (unit("ejc_rdy"), unit("mask_rdy"), unit("z_rdy"),
                                                       unit("nm_step"), unit("nmax_rdy"))
        e_rdy, y_rdy, s_rdy, p_rdy, t_rdy = (unit("e_rdy"), unit("y_rdy"), unit("s_rdy"), unit("p_rdy"),
                                             unit("t_rdy"))
        tA_used, tV_used, v_rdy, rc_step, v_used = (unit("tA_used"), unit("tV_used"), unit("v_rdy"),
                                                    unit("rc_step"), unit("v_used"))
        xb_made, xtp_rdy, xt_rdy, lgp_rdy, lg_rdy = (unit("xb_made"), unit("xtp_rdy"), unit("xt_rdy"),
                                                     unit("lgp_rdy"), unit("lg_rdy"))
        hp_rdy, hf_rdy, hhi_rdy, hs_rdy, yp_rdy = (unit("hp_rdy"), unit("hf_rdy"), unit("hhi_rdy"),
                                                   unit("hs_rdy"), unit("yp_rdy"))
        r_step, r_used, y_out, comb = unit("r_step"), unit("r_used"), unit("y_out"), unit("comb")

        sq_rdy, oth_rdy, othP_rdy, flag_rdy = unit("sq_rdy"), sem("oth_rdy"), sem("othP_rdy"), sem("flag_rdy")
        o_ld = [sem(f"o_ld{g}") for g in range(NG)]
        o_half, o_q, o_e, o_s, o_max, o_p, o_t, o_c, o_v, o_x = (
            [unit(f"{n}{g}") for g in range(NG)]
            for n in ("o_half", "o_q", "o_e", "o_s", "o_max", "o_p", "o_t", "o_c", "o_v", "o_x"))

        def after(eng, semaphore, count):
            eng.wait_ge(semaphore, count + CR)

        ENGINES = 3

        def order(project, gnn, relations, dense, blocks, combine):
            for l in range(2):
                for g in range(NG):
                    if l == 1:
                        combine(0, g)
                    project(l, g)
                    gnn(l, g)
                    if l == 1:
                        relations(l, g)
                    dense(l, g)
                for g in range(NG):
                    blocks(l, g)
            for g in range(NG):
                combine(1, g)

        MEET = {}

        def note(kind):
            def f(l, g):
                MEET[kind, l, g] = len(MEET) + 1
            return f
        order(note("project"), note("gnn"), lambda l, g: None, note("dense"), note("blocks"), lambda l, g: None)

        def meet(eng, kind, l, g):
            eng.drain().then_inc(over, 1)
            eng.wait_ge(over, ENGINES * MEET[kind, l, g])

        def q_of(l, g):
            return l * NG + g

        U0, M0, BL0 = {}, {}, {}
        u = m = bl = 0
        for l in range(2):
            for g in range(NG):
                U0["dense", l, g], M0["dense", l, g], BL0["dense", l, g] = u, m, bl
                u += US
                m += US if l == 0 else 0
            for g in range(NG):
                U0["blocks", l, g], M0["blocks", l, g], BL0["blocks", l, g] = u, m, bl
                u += NB
                m += NB
                bl += NB

        block = ctx.enter_context(nc.Block())

        @block.sync
        def _(sp):
            for c in counted:
                sp.sem_inc(c, CR)
            for c in (*xb_st, *ys_st):
                sp.sem_inc(c, 16)
            xv = x_in.rearrange("b (t p) d -> p (b t) d", p=P)
            ov = out.rearrange("b (t p) d -> p (b t) d", p=P)
            sp.dma_start(x[:, 0:TG * D].rearrange("p (t d) -> p t d", d=D), xv[:, 0:TG, :]).then_inc(x_ld[0], 16)
            small_loads = [
                (gw, gnn_w), (gacol[:], gnn_a.rearrange("(k p) -> p k", p=P)),
                (gbrow[:], gbias.rearrange("(o d) -> o d", o=1)),
                (wrf[:, 0, :], wr0), (wrf[:, 1, :], wg1),
                (b1rows[0][0:E * C[0], :], b1p.rearrange("e (c p) -> (e c) p", p=P)),
                (b1rows[0][E * C[0]:NE[0] * C[0], :], b1s.rearrange("(c p) -> c p", p=P)),
                (b1rows[1], b1e.rearrange("e (c p) -> (e c) p", p=P)),
                (b2b[0][:, 0:E * D], b2p.rearrange("e d -> (e d)").partition_broadcast(P)),
                (b2b[0][:, E * D:NE[0] * D], b2s.partition_broadcast(P)),
                (b2b[1][:, :], b2e.rearrange("e d -> (e d)").partition_broadcast(P)),
                (gtmp[:, 0, :], bg1.partition_broadcast(P)), (gtmp[:, 1, :], bias1.partition_broadcast(P)),
            ] + [(akcol[:, k:k + 1], a) for k, a in enumerate([a0, a1, a2, a3])]
            assert len(small_loads) == NC
            with nc.allow_non_contiguous_dma(reason="a few small vectors"):
                for dst, src in small_loads:
                    sp.dma_start(dst, src).then_inc(c_ld, 16)
            sp.dma_start(x[:, TG * D:T * D].rearrange("p (t d) -> p t d", d=D), xv[:, TG:T, :]).then_inc(x_ld[1], 16)

            def project(l, g):
                pass

            def gnn(l, g):
                with sp.Fori(0, BG) as bb:
                    for k in range(TB):
                        after(sp, p_rdy, (q_of(l, g) * BG + bb) * TB + k - NA + 1)
                        sp.dma_start(adjb[k % NA][:], adj_in[ds(g * BG + bb, 1), k * P:(k + 1) * P, :]
                                     .rearrange("o p n -> (o p) n")).then_inc(adj_ld[k % NA], 16)
                if l == 0 and g == 0:
                    sp.wait_ge(consts, NCONST)
                    for gg in range(NG):
                        sp.dma_start(xs_d[gg].rearrange("(p r) c -> p (r c)", p=P)
                                     .rearrange("p (r c) -> p r c", c=256),
                                     zero16[:].rearrange("p (o c) -> p o c", o=1)
                                     .to_broadcast([P, ROWS * 2 * D // (P * 256), 256])).then_inc(xs_zero, 16)

            def relations(l, g):
                sp.wait_ge(flag_rdy, g + 1)
                flag = sp.value_load(others[g][0:1, 0:1], min_val=0, max_val=P)
                with sp.If(flag > 0):
                    after(sp, p_rdy, (q_of(l, g) + 1) * TG)
                    with sp.Fori(1, 4) as r:
                        with sp.Fori(0, BG) as bb:
                            with sp.Fori(0, TB) as k:
                                after(sp, o_p[g], ((r - 1) * BG + bb) * TB + k)
                                sp.dma_start(adjb[0][:], adj_in[ds(g * BG + bb, 1), ds(k * P, P), :]
                                             .rearrange("o p n -> (o p) n")).then_inc(o_ld[g], 16)

            def dense(l, g):
                q = q_of(l, g)
                if l == 1:
                    sp.wait_ge(scat_all, g + 1)

                def store(j, par):
                    u = 2 * j + par
                    after(sp, xb_made, q * US + u + 1)
                    sp.dma_start(xn_d[ds(g * TG * P + u * SPAN, SPAN), :].rearrange("(s p) c -> p s c", p=P),
                                 xb[par].rearrange("p (s c) -> p s c", s=ST)).then_inc(xb_st[par], 16)
                with sp.Fori(0, US // 2) as j:
                    store(j, 0)
                    store(j, 1)
                sp.wait_ge(tbl_rdy, 2 * q + 1)
                if l == 1:
                    after(sp, comb, 2 * BG * (g + 1))
                sp.dma_start(slot_d[g * P:(g + 1) * P, :], sl[:]).then_inc(slot_st, 16)

            def blocks(l, g):
                q = q_of(l, g)
                sp.wait_ge(over, ENGINES * MEET["blocks", l, g])
                sp.wait_ge(scat_all, q + 1)
                if l == 1:
                    after(sp, comb, 2 * BG * (g + 1))

                def load(j, par):
                    u = 2 * j + par
                    after(sp, xtp_rdy, U0["blocks", l, g] + u - 1)
                    sp.dma_start(xb[par].rearrange("p (s c) -> p s c", s=ST),
                                 xs_d[g][ds(u * SPAN, SPAN), :].rearrange("(s p) c -> p s c", p=P)
                                 ).then_inc(xb_ld[par], 16)

                def store(j, par):
                    u = 2 * j + par
                    after(sp, y_out, BL0["blocks", l, g] + u + 1)
                    sp.dma_start(ys_d[g][ds(u * SPAN, SPAN), :].rearrange("(s p) d -> p s d", p=P),
                                 ysb[par].rearrange("p (s d) -> p s d", s=ST)).then_inc(ys_st[par], 16)
                load(0, 0)
                load(0, 1)
                with sp.Fori(0, H - 1) as j:
                    load(j + 1, 0)
                    store(j, 0)
                    load(j + 1, 1)
                    store(j, 1)
                load(H, 0)
                store(H - 1, 0)
                store(H - 1, 1)
                store(H, 0)
                for par in range(2):
                    sp.wait_ge(ys_st[par], 16 * (1 + NPAR[par] * (q + 1)))
                sp.sem_inc(blocks_out, 1)

            def combine(l, g):
                if l == 1:
                    for bb in range(BG):
                        t = (g * BG + bb) * TB
                        after(sp, comb, 2 * (q_of(l, g) * BG + bb + 1))
                        sp.dma_start(ov[:, t:t + TB, :],
                                     x[:, t * D:(t + TB) * D].rearrange("p (t d) -> p t d", d=D)).then_inc(o_st, 16)
            order(project, gnn, relations, dense, blocks, combine)
            sp.wait_ge(o_st, 16 * B)

        @block.gpsimd
        def _(pool):
            n_link = [0]

            def link(ins):
                n_link[0] += 1
                ins.then_inc(pchain, 1)
                pool.wait_ge(pchain, n_link[0])

            g_ = nc.gpsimd
            link(g_.memset(ident[:], 0.0))
            link(g_.affine_select(out=ident[:], in_=ident[:], compare_op=ALU.not_equal, fill=1.0, base=0,
                                  pattern=[[-1, P]], channel_multiplier=1))
            g_.memset(ones_row[:], 1.0).then_inc(consts, 1)
            g_.memset(zero16[:], 0.0).then_inc(consts, 1)
            g_.memset(ones16[:], 1.0).then_inc(consts, 1)
            link(g_.memset(before[:], 1.0))
            g_.affine_select(out=before[:], in_=before[:], compare_op=ALU.is_gt, fill=0.0, base=0,
                             pattern=[[1, P]], channel_multiplier=-1).then_inc(consts, 1)
            g_.iota(rank[:], pattern=[[-1, E]], base=E, channel_multiplier=0,
                    allow_small_or_imprecise_dtypes=True).then_inc(consts, 1)
            g_.iota(blockno[:], pattern=[[1, NB]], base=0, channel_multiplier=0,
                    allow_small_or_imprecise_dtypes=True).then_inc(consts, 1)
            g_.iota(codes[:], pattern=[[1, 4]], base=1, channel_multiplier=0,
                    allow_small_or_imprecise_dtypes=True).then_inc(consts, 1)
            g_.tensor_copy(ident16[:], ident[:]).then_inc(consts, 1)

            pieces = []
            for l in range(2):
                f, c = F[l], C[l]
                for e in range(NE[l]):
                    w1 = (w1s if e == SH else w1p[e]) if l == 0 else w1e[e]
                    w2 = (w2s if e == SH else w2p[e]) if l == 0 else w2e[e]
                    to1 = w1sp[l][:, e * 2 * f:(e + 1) * 2 * f].rearrange("p (h f) -> p h f", h=2)
                    to2 = (w2sp[l][:, e * c * 2 * D:(e + 1) * c * 2 * D]
                           .rearrange("p (c h d) -> p h c d", c=c, h=2))
                    pieces.append((w1, 0, to1[:, 0, :], to1[:, 1, :], f))
                    pieces.append((w2.rearrange("(c p) d -> p c d", p=P), c, to2[:, 0], to2[:, 1], f))
            assert len(pieces) == NPIECES

            def staged(i):
                c, f = pieces[i][1], pieces[i][4]
                w = stage[i % 2].bitcast(f32)[:, 0:f]
                return w.rearrange("p (c d) -> p c d", c=c) if c else w

            def fetch(i):
                if i >= 2:
                    pool.wait_ge(w_used, i - 1)
                pool.dma_start(staged(i), pieces[i][0]).then_inc(w_ld[i % 2], 16)

            fetch(0)
            for i, (_, _, hi, lo, _) in enumerate(pieces):
                if i + 1 < len(pieces):
                    fetch(i + 1)
                pool.wait_ge(w_ld[i % 2], 16 * (i // 2 + 1))
                link(g_.tensor_copy(hi, staged(i)))
                g_.tensor_tensor(lo, staged(i), hi, ALU.subtract).then_inc(w_used, 1)

            h = BG // 2

            def slots_of(g, bb):
                return slot_d[g * P:(g + 1) * P, ds(bb * 2 * TB, 2 * TB)]

            def scatter(l, g):
                q = q_of(l, g)
                pool.wait_ge(slot_st, 16 * (q + 1))
                if q == 0:
                    pool.wait_ge(xs_zero, 16 * NG)
                if l == 1:
                    pool.wait_ge(blocks_out, g + 1)
                for par in range(2):
                    pool.wait_ge(xb_st[par], 16 * (1 + (q + 1) * US // 2))

                def load(j, par):
                    pool.dma_start(idx[par][:], slots_of(g, 2 * j + par)).then_inc(st_ld[par], 16)
                    pool.dma_start(stage[par][:].rearrange("p (t c) -> p t c", t=TB),
                                   xn_d[ds((g * TG + (2 * j + par) * TB) * P, TB * P), :]
                                   .rearrange("(t p) c -> p t c", p=P)).then_inc(st_ld[par], 16)

                def rows_out(j, par):
                    pool.wait_ge(st_ld[par], 32 * (h * q + j + 1))
                    pool.nop(nofuse=True)
                    for k in range(TB):
                        for c in range(2):
                            pool.indirect_dma_start(
                                out=xs_d[g][:, :],
                                out_offset=bass.IndirectOffsetOnAxis(ap=idx[par][:, 2 * k + c:2 * k + c + 1], axis=0),
                                in_=stage[par][:, k * 2 * D:(k + 1) * 2 * D], in_offset=None).then_inc(scat[par], 16)

                def all_out(j, par):
                    pool.wait_ge(scat[par], 16 * 2 * TB * (h * q + j + 1))
                load(0, 0)
                load(0, 1)
                with pool.Fori(0, h - 1) as j:
                    rows_out(j, 0)
                    rows_out(j, 1)
                    for par in range(2):
                        all_out(j, par)
                        load(j + 1, par)
                rows_out(h - 1, 0)
                rows_out(h - 1, 1)
                all_out(h - 1, 0)
                all_out(h - 1, 1)
                pool.sem_inc(scat_all, 1)

            def gather(l, g):
                q = q_of(l, g)
                pool.wait_ge(blocks_out, q + 1)

                def load(j, par):
                    pool.dma_start(idx[par][:], slots_of(g, 2 * j + par)).then_inc(gi_ld[par], 16)

                def rows_in(j, par):
                    bb = 2 * j + par
                    pool.wait_ge(gi_ld[par], 16 * (h * q + j + 1))
                    for half in range(2):
                        after(pool, comb, 2 * (BG * q + bb) + half - 1)
                        pool.nop(nofuse=True)
                        for i in range(TB):
                            k = half * TB + i
                            pool.indirect_dma_start(
                                out=got[half][:, i * D:(i + 1) * D], out_offset=None, in_=ys_d[g][:, :],
                                in_offset=bass.IndirectOffsetOnAxis(ap=idx[par][:, k:k + 1], axis=0),
                            ).then_inc(gath[par][half], 16)

                def all_in(j, par):
                    for half in range(2):
                        pool.wait_ge(gath[par][half], 16 * TB * (h * q + j + 1))
                load(0, 0)
                load(0, 1)
                with pool.Fori(0, h - 1) as j:
                    rows_in(j, 0)
                    rows_in(j, 1)
                    for par in range(2):
                        all_in(j, par)
                        load(j + 1, par)
                rows_in(h - 1, 0)
                rows_in(h - 1, 1)
                all_in(h - 1, 0)
                all_in(h - 1, 1)

            for l in range(2):
                for g in range(NG):
                    scatter(l, g)
                for g in range(NG):
                    gather(l, g)

        @block.scalar
        def _(act):
            s_ = nc.scalar
            act.wait_ge(prep_pe, 1)
            act.wait_ge(prep_dve, 1)
            for l in range(2):
                s_.copy(b1[l][:], ps[0][:, 512 * l:512 * l + NE[l] * C[l]]).then_inc(prep_act, 1)
            s_.copy(wcat[:], ps[1][:, 0:D]).then_inc(prep_act, 1)
            s_.copy(wa[:], ps[2][:, 0:2]).then_inc(prep_act, 1)

            def deviation(n):
                act.wait_ge(var_rdy, n)
                s_.activation(std[:], std[:], ACT.Sqrt).then_inc(std_rdy, 1)

            def project(l, g):
                meet(act, "project", l, g)
                q = q_of(l, g)
                deviation(2 * q + 1)

                def quad(i, par):
                    n = q * QG + i
                    after(act, xTp_rdy, n + 1)
                    if l == 0:
                        after(act, whP_rdy, n - 1)
                        s_.copy(xT4[par], eP[:, 512 * par:512 * par + 512]).then_inc(xT_rdy, 1)
                        after(act, ebP_rdy, n + 1)
                        s_.copy(ejb[:, ds(i * 512, 512)], tP[par][:, 0:512]).then_inc(eb_used, 1)
                    else:
                        m = n - NG * QG
                        after(act, kq_rdy, m - 1)
                        s_.copy(xT4[par], eP[:, 512 * par:512 * par + 512]).then_inc(xT_rdy, 1)
                        after(act, xT_rdy, n + 1)
                        s_.activation(qf[par], xT4[par], ACT.Copy, scale=akcol[:, 0:1]).then_inc(qf_rdy, 1)
                        s_.copy(vals[:, ds(i * 4 * D, 4 * D)], xn4[par]).then_inc(h_rdy, 1)
                with act.Fori(0, QG // 2) as i:
                    quad(2 * i, 0)
                    quad(2 * i + 1, 1)

            def gnn(l, g):
                meet(act, "gnn", l, g)
                q = q_of(l, g)

                def weights(n, k, bb):
                    par = k % 2
                    after(act, t_rdy, n - 1)
                    if l == 0:
                        act.wait_ge(adj_ld[k % NA], 16 * ((q * BG + bb) * (TB // NA) + k // NA + 1))
                        after(act, sq_rdy, n)
                        s_.activation(junk, adjb[k % NA][:], ACT.Square, bias=minus_half[:, 0:1],
                                      accum_out=squares[:, ds(g * TG + bb * TB + k, 1)]).then_inc(sq_rdy, 1)
                        after(act, nmax_rdy, n + 1)
                        s_.activation(pr[par], zt[par], ACT.Exp, scale=LEAK, bias=shift2[:, par:par + 1])
                        s_.activation(zt[par], zt[par], ACT.Exp, bias=shift1[:, par:par + 1]).then_inc(y_rdy, 1)
                    else:
                        after(act, e_rdy, n - NG * TG + 1)
                        after(act, p_rdy, n - 1)
                        s_.activation(pr[par], eP[:, :], ACT.Sigmoid, scale=LEAK)
                        s_.activation(zt[par], eP[:, :], ACT.Sigmoid).then_inc(y_rdy, 1)

                def evacuate(n, k):
                    par = k % 2
                    after(act, t_rdy, n + 1)
                    after(act, v_rdy, n - 1)
                    s_.copy(pT[par][:, 512:1024], tP[par][:, 512:1024]).then_inc(tA_used, 1)

                with act.Fori(0, BG) as bb:
                    n0 = (q * BG + bb) * TB
                    if l == 0:
                        after(act, z_rdy, n0)
                        s_.copy(ejc, ejb[:, ds(bb * N, N)]).then_inc(ejc_rdy, 1)
                    for k in range(TB):
                        weights(n0 + k, k, bb)
                        if k >= 1:
                            evacuate(n0 + k - 1, k - 1)
                    evacuate(n0 + TB - 1, TB - 1)

            def relations(l, g):
                act.wait_ge(flag_rdy, g + 1)
                flag = act.value_load(others[g][0:1, 0:1], min_val=0, max_val=P)
                with act.If(flag > 0):
                    with act.Fori(1, 4) as r:
                        with act.Fori(0, BG) as bb:
                            with act.Fori(0, TB) as k:
                                n = ((r - 1) * BG + bb) * TB + k
                                after(act, o_e[g], n + 1)
                                after(act, o_p[g], n)
                                after(act, o_t[g], n)
                                s_.activation(pr[0], eP[:, :], ACT.Sigmoid, scale=LEAK)
                                s_.activation(zt[0], eP[:, :], ACT.Sigmoid).then_inc(o_s[g], 1)

            def to_sbuf(j, par, kind, l, g):
                u = 2 * j + par
                after(act, xtp_rdy, U0[kind, l, g] + u + 1)
                if kind == "dense" and l == 1:
                    after(act, lgp_rdy, q_of(l, g) * US + u - 1)
                else:
                    after(act, hp_rdy, M0[kind, l, g] + u - 1)
                s_.copy(xt[par], xtP[par]).then_inc(xt_rdy, 1)

            def hidden(j, par, kind, l, g, e):
                m = M0[kind, l, g] + 2 * j + par
                after(act, hp_rdy, m + 1)
                after(act, hs_rdy, m - 1)
                for c in range(C[l]):
                    last = s_.activation(hf[par][:, c * SPAN:(c + 1) * SPAN], hP[par][:, c * SPAN:(c + 1) * SPAN],
                                         ACT.Gelu if l == 0 else ACT.Relu, bias=b1[l][:, ds(e * C[l] + c, 1)])
                last.then_inc(hf_rdy, 1)

            def dense(l, g):
                meet(act, "dense", l, g)
                deviation(2 * q_of(l, g) + 2)
                k = "dense"
                if l == 0:
                    to_sbuf(0, 0, k, l, g)
                    with act.Fori(0, US // 2 - 1) as j:
                        to_sbuf(j, 1, k, l, g)
                        hidden(j, 0, k, l, g, SH)
                        to_sbuf(j + 1, 0, k, l, g)
                        hidden(j, 1, k, l, g, SH)
                    to_sbuf(US // 2 - 1, 1, k, l, g)
                    hidden(US // 2 - 1, 0, k, l, g, SH)
                    hidden(US // 2 - 1, 1, k, l, g, SH)
                else:
                    with act.Fori(0, US // 2) as j:
                        to_sbuf(j, 0, k, l, g)
                        to_sbuf(j, 1, k, l, g)
                act.wait_ge(w2_rdy, q_of(l, g) + 1)
                s_.activation(mx[2], mx[2], ACT.Exp).then_inc(w2e_rdy, 1)

            def blocks(l, g):
                meet(act, "blocks", l, g)
                k = "blocks"

                def expert(u):
                    return act.value_load(be[g][0:1, ds(u, 1)], min_val=0, max_val=E - 1)
                act.wait_ge(tbl_rdy, 2 * q_of(l, g) + 2)
                to_sbuf(0, 0, k, l, g)
                with act.Fori(0, H) as j:
                    to_sbuf(j, 1, k, l, g)
                    hidden(j, 0, k, l, g, expert(2 * j))
                    to_sbuf(j + 1, 0, k, l, g)
                    hidden(j, 1, k, l, g, expert(2 * j + 1))
                hidden(H, 0, k, l, g, expert(2 * H))

            order(project, gnn, relations, dense, blocks, lambda l, g: None)

        @block.vector
        def _(dve):
            v_ = nc.vector
            n_link = [0]

            def link(ins):
                n_link[0] += 1
                ins.then_inc(chain, 1)
                dve.wait_ge(chain, n_link[0])

            dve.wait_ge(c_ld, 16 * NC)
            dve.wait_ge(consts, NCONST)
            link(v_.tensor_copy(wrs[:, :, 0, :], wrf[:]))
            v_.memset(gateb[:, 0], 0.0)
            v_.memset(minus_half[:], -0.5)
            for s in range(ST):
                v_.tensor_tensor(gateb[:, 1, s], gtmp[:, 0, :], gtmp[:, 1, :], ALU.add)
            v_.tensor_tensor(wrs[:, :, 1, :], wrf[:], wrs[:, :, 0, :], ALU.subtract).then_inc(prep_dve, 1)
            dve.wait_ge(prep_act, 4)
            v_.tensor_copy(wa2b[:], wa[:, 1:2].to_broadcast([P, P])).then_inc(prep_dve, 1)

            def statistics(n, g):
                base = n_link[0]
                with dve.Fori(0, TG // 8) as i:
                    for s in range(8):
                        v_.bn_stats(stats[:, s, :], x[:, ds((g * TG + 8 * i + s) * D, D)]).then_inc(chain, 1)
                    dve.wait_ge(chain, base + 17 * i + 8)
                    dve.nop(nofuse=True)
                    for s in range(8):
                        v_.bn_aggr(mv8[:, 2 * s:2 * s + 2], stats[:, s, :]).then_inc(chain, 1)
                    dve.wait_ge(chain, base + 17 * i + 16)
                    v_.tensor_copy(mv[:, ds(16 * i, 16)], mv8[:]).then_inc(chain, 1)
                    dve.wait_ge(chain, base + 17 * i + 17)
                n_link[0] += 17 * (TG // 8)
                v_.tensor_scalar(std[:], mv[:].rearrange("p (t k) -> p t k", k=2)[:, :, 1], EPS, None,
                                 ALU.add).then_inc(var_rdy, 1)
                dve.wait_ge(std_rdy, n)
                link(v_.reciprocal(rstd[:], std[:]))

            def project(l, g):
                meet(dve, "project", l, g)
                q = q_of(l, g)
                if l == 0:
                    dve.wait_ge(x_ld[g], 16)
                statistics(2 * q + 1, g)

                def normal(i, par):
                    n = q * QG + i
                    after(dve, xTp_rdy, n - 1)
                    if l == 1:
                        after(dve, h_rdy, n - NG * QG - 1)
                    for s in range(4):
                        t = 4 * i + s
                        last = v_.tensor_scalar(xn4[par][:, s * D:(s + 1) * D], x[:, ds((g * TG + t) * D, D)],
                                                mv[:, ds(2 * t, 1)], rstd[:, ds(t, 1)], ALU.subtract, ALU.mult)
                    last.then_inc(xn4_rdy, 1)

                def collect(i, par):
                    n = q * QG + i
                    if l == 0:
                        after(dve, whP_rdy, n + 1)
                        v_.tensor_copy(vals[:, ds(i * 4 * D, 4 * D)], ps[3][:, 512 * par:512 * par + 512])
                        v_.tensor_copy(ei[:, ds(i * 4, 4)], tP[par][:, 512:516]).then_inc(wh_used, 1)
                    else:
                        m = n - NG * QG
                        after(dve, xT_rdy, n + 1)
                        v_.tensor_copy(kT[:, ds(i * 512, 512)], xT4[par]).then_inc(khi_rdy, 1)
                        after(dve, qf_rdy, m + 1)
                        v_.tensor_copy(qT[:, ds(i * 512, 512)], qf[par]).then_inc(khi_rdy, 1)
                        after(dve, khi_rdy, 2 * m + 1)
                        v_.tensor_tensor(kT[:, ds(TG * P + i * 512, 512)], xT4[par], kT[:, ds(i * 512, 512)],
                                         ALU.subtract)
                        after(dve, khi_rdy, 2 * m + 2)
                        v_.tensor_tensor(qT[:, ds(TG * P + i * 512, 512)], qf[par], qT[:, ds(i * 512, 512)],
                                         ALU.subtract).then_inc(kq_rdy, 1)
                normal(0, 0)
                with dve.Fori(0, QG // 2 - 1) as i:
                    normal(2 * i + 1, 1)
                    collect(2 * i, 0)
                    normal(2 * i + 2, 0)
                    collect(2 * i + 1, 1)
                normal(QG - 1, 1)
                collect(QG - 2, 0)
                collect(QG - 1, 1)

            def gnn(l, g):
                meet(dve, "gnn", l, g)
                q = q_of(l, g)

                def front(n, k, bb):
                    par = k % 2
                    dve.wait_ge(adj_ld[k % NA], 16 * ((q * BG + bb) * (TB // NA) + k // NA + 1))
                    after(dve, p_rdy, n - 1)
                    v_.tensor_scalar(zt[par], adjb[k % NA][:], 0.0, NEG, ALU.is_equal,
                                     ALU.mult).then_inc(mask_rdy, 1)
                    after(dve, mask_rdy, n + 1)
                    dve.nop(nofuse=True)
                    v_.tensor_tensor_reduce(out=zt[par], in0=zt[par], in1=ejc, scale=1.0, scalar=2 * NEG,
                                            op0=ALU.add, op1=ALU.max,
                                            accum_out=mrow[:, par:par + 1]).then_inc(z_rdy, 1)
                    after(dve, z_rdy, n + 1)
                    v_.tensor_scalar(t1, mrow[:, par:par + 1], ei[:, ds(bb * TB + k, 1)], FLOOR,
                                     ALU.add, ALU.max).then_inc(nm_step, 1)
                    after(dve, nm_step, 3 * n + 1)
                    v_.tensor_scalar(t2, t1, -LEAK, None, ALU.mult).then_inc(nm_step, 1)
                    after(dve, nm_step, 3 * n + 2)
                    v_.scalar_tensor_tensor(nmax, t1, -1.0, t2, ALU.mult, ALU.min).then_inc(nm_step, 1)
                    after(dve, nm_step, 3 * n + 3)
                    eik = ei[:, ds(bb * TB + k, 1)]
                    v_.tensor_tensor(shift1[:, par:par + 1], eik, nmax, ALU.add)
                    v_.scalar_tensor_tensor(shift2[:, par:par + 1], eik, LEAK, nmax, ALU.mult,
                                            ALU.add).then_inc(nmax_rdy, 1)

                def merge(n, k, bb_):
                    par = k % 2
                    after(dve, y_rdy, n + 1)
                    if l == 0:
                        v_.scalar_tensor_tensor(pr[par], zt[par], 1.0, pr[par], ALU.mult, ALU.max,
                                                accum_out=rsum[:, k % 4:k % 4 + 1]).then_inc(p_rdy, 1)
                    else:
                        m = n - NG * TG
                        v_.tensor_tensor(zt[par], zt[par], pr[par], ALU.max).then_inc(s_rdy, 1)
                        after(dve, s_rdy, m + 1)
                        dve.wait_ge(adj_ld[k % NA], 16 * ((q * BG + bb_) * (TB // NA) + k // NA + 1))
                        v_.scalar_tensor_tensor(pr[par], adjb[k % NA][:], 1.0, zt[par], ALU.is_equal,
                                                ALU.mult).then_inc(p_rdy, 1)

                def evacuate(n, k):
                    par = k % 2
                    after(dve, t_rdy, n + 1)
                    after(dve, v_rdy, n - 1)
                    v_.tensor_copy(pT[par][:, 0:512], tP[par][:, 0:512]).then_inc(tV_used, 1)

                def finish(n, k, bb):
                    par = k % 2
                    xt_ = x[:, ds((g * TG + bb * TB + k) * D, D)]
                    after(dve, v_rdy, n + 1)
                    if l == 0:
                        v_.tensor_scalar(rcp[:, par:par + 1], rsum[:, k % 4:k % 4 + 1], 1e-30, None,
                                         ALU.max).then_inc(rc_step, 1)
                        after(dve, rc_step, 2 * n + 1)
                        v_.reciprocal(rcp[:, par:par + 1], rcp[:, par:par + 1]).then_inc(rc_step, 1)
                        after(dve, rc_step, 2 * n + 2)
                    v_.scalar_tensor_tensor(xt_, vP[par], rcp[:, par:par + 1] if l == 0 else 1.0, xt_,
                                            ALU.mult, ALU.add).then_inc(v_used, 1)

                with dve.Fori(0, BG) as bb:
                    n0 = (q * BG + bb) * TB
                    if l == 0:
                        after(dve, ejc_rdy, q * BG + bb + 1)
                    for k in range(TB):
                        if l == 0:
                            front(n0 + k, k, bb)
                            if k >= 1:
                                merge(n0 + k - 1, k - 1, bb)
                        else:
                            merge(n0 + k, k, bb)
                        if k >= 2 - l:
                            evacuate(n0 + k - 2 + l, k - 2 + l)
                        if k >= 3 - l:
                            finish(n0 + k - 3 + l, k - 3 + l, bb)
                    if l == 0:
                        merge(n0 + TB - 1, TB - 1, bb)
                        evacuate(n0 + TB - 2, TB - 2)
                        finish(n0 + TB - 3, TB - 3, bb)
                    evacuate(n0 + TB - 1, TB - 1)
                    finish(n0 + TB - 2, TB - 2, bb)
                    finish(n0 + TB - 1, TB - 1, bb)

            def relations(l, g):
                q = q_of(l, g)
                dve.wait_ge(flag_rdy, g + 1)
                flag = dve.value_load(others[g][0:1, 0:1], min_val=0, max_val=P)
                with dve.If(flag > 0):
                    after(dve, v_rdy, (q + 1) * TG)
                    after(dve, v_used, (q + 1) * TG)
                    with dve.Fori(1, 4) as r:
                        with dve.Fori(0, BG) as bb:
                            b = (r - 1) * BG + bb
                            after(dve, o_v[g], b * TB)
                            hi_k, lo_k = kT[:, ds(bb * N, N)], kT[:, ds(TG * P + bb * N, N)]
                            hi_q, lo_q = qT[:, ds(bb * N, N)], qT[:, ds(TG * P + bb * N, N)]
                            v_.tensor_tensor(zt[0], hi_k, lo_k, ALU.add).then_inc(o_half[g], 1)
                            after(dve, o_half[g], 3 * b + 1)
                            v_.tensor_scalar(zt[0], zt[0], akcol[:, ds(r, 1)], None, ALU.mult).then_inc(o_half[g], 1)
                            after(dve, o_half[g], 3 * b + 2)
                            v_.tensor_copy(hi_q, zt[0]).then_inc(o_half[g], 1)
                            after(dve, o_half[g], 3 * b + 3)
                            v_.tensor_tensor(lo_q, zt[0], hi_q, ALU.subtract).then_inc(o_q[g], 1)
                            with dve.Fori(0, TB) as k:
                                n = b * TB + k
                                after(dve, o_s[g], n + 1)
                                v_.tensor_tensor(zt[0], zt[0], pr[0], ALU.max).then_inc(o_max[g], 1)
                                after(dve, o_max[g], n + 1)
                                dve.wait_ge(o_ld[g], 16 * (n + 1))
                                v_.scalar_tensor_tensor(pr[0], adjb[0][:], codes[:, ds(r, 1)], zt[0],
                                                        ALU.is_equal, ALU.mult).then_inc(o_p[g], 1)
                                after(dve, o_t[g], n + 1)
                                after(dve, o_v[g], n)
                                v_.tensor_copy(pT[0], tP[0][:, :]).then_inc(o_c[g], 1)
                                after(dve, o_v[g], n + 1)
                                xt_ = x[:, ds((g * TG + bb * TB + k) * D, D)]
                                v_.tensor_tensor(xt_, vP[0], xt_, ALU.add).then_inc(o_x[g], 1)

            def split(j, par, kind, l, g):
                m = M0[kind, l, g] + 2 * j + par
                w = C[l] * SPAN
                after(dve, hf_rdy, m + 1)
                after(dve, yp_rdy, m - 1)
                v_.tensor_copy(hs[par][:, 0:w], hf[par][:, 0:w]).then_inc(hhi_rdy, 1)
                after(dve, hhi_rdy, m + 1)
                v_.tensor_tensor(hs[par][:, 4 * SPAN:4 * SPAN + w], hf[par][:, 0:w], hs[par][:, 0:w],
                                 ALU.subtract).then_inc(hs_rdy, 1)

            def dense(l, g):
                meet(dve, "dense", l, g)
                q = q_of(l, g)
                statistics(2 * q + 2, g)
                c0 = n_link[0]

                def rows(j, par):
                    u = 2 * j + par
                    for s in range(ST):
                        t = ST * u + s
                        v_.tensor_scalar(xf[par][:, s * D:(s + 1) * D], x[:, ds((g * TG + t) * D, D)],
                                         mv[:, ds(2 * t, 1)], rstd[:, ds(t, 1)], ALU.subtract,
                                         ALU.mult).then_inc(chain, 1)
                    dve.wait_ge(chain, c0 + 3 * u + 2)
                    after(dve, xtp_rdy, U0["dense", l, g] + u - 1)
                    dve.wait_ge(xb_st[par], 16 * (1 + q * US // 2 + j))
                    f3 = xf[par].rearrange("p (s d) -> p s d", s=ST)
                    b3 = xb[par].rearrange("p (s c) -> p s c", s=ST)
                    v_.tensor_copy(b3[:, :, 0:D], f3).then_inc(chain, 1)
                    dve.wait_ge(chain, c0 + 3 * u + 3)
                    v_.tensor_tensor(b3[:, :, D:2 * D], f3, b3[:, :, 0:D], ALU.subtract).then_inc(xb_made, 1)

                def scores(j, par):
                    u = 2 * j + par
                    after(dve, lgp_rdy, q * US + u + 1)
                    v_.tensor_tensor(lg[:, ds(u * ST * E, ST * E)], lgP[par],
                                     gateb[:, l].rearrange("p s e -> p (s e)"), ALU.add).then_inc(lg_rdy, 1)

                def residual(j, par):
                    u = 2 * j + par
                    r = g * US + u
                    after(dve, yp_rdy, M0["dense", l, g] + u + 1)
                    for s in range(ST):
                        last = v_.tensor_tensor(ysb[par][:, s * D:(s + 1) * D], yP[par][:, s * D:(s + 1) * D],
                                                b2b[0][:, SH * D:(SH + 1) * D], ALU.add)
                    last.then_inc(r_step, 1)
                    after(dve, r_step, r + 1)
                    xu = x[:, ds((g * TG + ST * u) * D, ST * D)]
                    v_.tensor_tensor(xu, xu, ysb[par], ALU.add).then_inc(r_used, 1)

                J = US // 2
                rows(0, 0)
                rows(0, 1)
                if l == 0:
                    scores(0, 0)
                    split(0, 0, "dense", l, g)
                    with dve.Fori(0, J - 1) as j:
                        rows(j + 1, 0)
                        scores(j, 1)
                        split(j, 1, "dense", l, g)
                        residual(j, 0)
                        rows(j + 1, 1)
                        scores(j + 1, 0)
                        split(j + 1, 0, "dense", l, g)
                        residual(j, 1)
                    scores(J - 1, 1)
                    split(J - 1, 1, "dense", l, g)
                    residual(J - 1, 0)
                    residual(J - 1, 1)
                else:
                    with dve.Fori(0, J - 1) as j:
                        scores(j, 0)
                        rows(j + 1, 0)
                        scores(j, 1)
                        rows(j + 1, 1)
                    scores(J - 1, 0)
                    scores(J - 1, 1)
                n_link[0] += 3 * US
                after(dve, lg_rdy, US * (q + 1))
                route(l, g)
                for par in range(2):
                    dve.wait_ge(xb_st[par], 16 * (1 + (q + 1) * US // 2))

            def route(l, g):
                q = q_of(l, g)
                W = TG * E

                def te(a):
                    return a.rearrange("p (t e) -> p t e", e=E)

                def bc(a):
                    return a.rearrange("p (t o) -> p t o", o=1).to_broadcast([P, TG, E])
                rk = rank[:].rearrange("p (o e) -> p o e", o=1).to_broadcast([P, TG, E])
                src = lg
                for c in range(2):
                    link(v_.tensor_reduce(mx[c], te(src), AX.X, ALU.max))
                    link(v_.tensor_tensor(te(tm[0]), te(src), bc(mx[c]), ALU.is_equal))
                    link(v_.tensor_tensor(te(tm[0]), te(tm[0]), rk, ALU.mult))
                    link(v_.tensor_reduce(mx[3], te(tm[0]), AX.X, ALU.max))
                    link(v_.tensor_tensor(te(oh[c]), te(tm[0]), bc(mx[3]), ALU.is_equal))
                    if c == 0:
                        link(v_.scalar_tensor_tensor(tm[1], oh[0], NEG, lg, ALU.mult, ALU.add))
                        src = tm[1]
                v_.tensor_tensor(oh16, oh[0], oh[1], ALU.add).then_inc(route_rdy, 1)
                v_.tensor_tensor(mx[2], mx[1], mx[0], ALU.subtract).then_inc(w2_rdy, 1)
                if l == 0:
                    after(dve, sq_rdy, (g + 1) * TG)
                    link(v_.tensor_reduce(worst[:], squares[:, g * TG:(g + 1) * TG], AX.X, ALU.max))
                    v_.tensor_scalar(other16[:], worst[:], N / 4, None, ALU.is_gt).then_inc(oth_rdy, 1)
                    dve.wait_ge(othP_rdy, g + 1)
                    v_.tensor_copy(others[g][:], tP[0][0:1, 512:513]).then_inc(flag_rdy, 1)
                dve.wait_ge(pos_rdy, q + 1)
                link(v_.tensor_copy(cum[0], tP[1][:, 0:W]))
                a, b, d = 0, 1, 1
                while d < TG:
                    link(v_.tensor_copy(cum[b][:, 0:d * E], cum[a][:, 0:d * E]))
                    link(v_.tensor_tensor(cum[b][:, d * E:W], cum[a][:, d * E:W], cum[a][:, 0:W - d * E], ALU.add))
                    a, b, d = b, a, 2 * d
                tot = cum[a][:, W - E:W]
                link(v_.tensor_scalar(nb_i[:], tot, float(SPAN - 1), None, ALU.add))
                link(v_.tensor_scalar(nb_i[:], nb_i[:], SPAN.bit_length() - 1, None, ALU.arith_shift_right))
                blk = [small[:, 0:E], small[:, E:2 * E]]
                link(v_.tensor_copy(blk[0], nb_i[:]))
                s, r, d = 0, 1, 1
                while d < E:
                    link(v_.tensor_copy(blk[r][:, 0:d], blk[s][:, 0:d]))
                    link(v_.tensor_tensor(blk[r][:, d:E], blk[s][:, d:E], blk[s][:, 0:E - d], ALU.add))
                    s, r, d = r, s, 2 * d
                first = small[:, 2 * E:3 * E]
                link(v_.memset(first, 0.0))
                link(v_.tensor_scalar(first[:, 1:E], blk[s][:, 0:E - 1], float(SPAN), None, ALU.mult))
                link(v_.tensor_tensor(te(tm[0]), te(tP[0][:, 0:W]),
                                      first.rearrange("p (o e) -> p o e", o=1).to_broadcast([P, TG, E]), ALU.add))
                link(v_.tensor_tensor(tm[0][:, E:W], tm[0][:, E:W], cum[a][:, 0:W - E], ALU.add))
                slv = slf.rearrange("p (t c) -> p t c", c=2)
                for c in range(2):
                    link(v_.tensor_tensor(tm[1], tm[0], oh[c], ALU.mult))
                    link(v_.tensor_reduce(slv[:, :, c], te(tm[1]), AX.X, ALU.add))
                if q >= 1:
                    dve.wait_ge(slot_st, 16 * q)
                v_.tensor_copy(sl[:], slf).then_inc(tbl_rdy, 1)
                nbv = blockno[:].rearrange("p (n o) -> p n o", o=1).to_broadcast([P, NB, E])
                bv = blk[s].rearrange("p (o e) -> p o e", o=1).to_broadcast([P, NB, E])
                cv = cmpb.rearrange("p (n e) -> p n e", e=E)
                link(v_.tensor_tensor(cv, nbv, bv, ALU.is_ge))
                link(v_.tensor_reduce(bef, cv, AX.X, ALU.add))
                v_.tensor_scalar(be[g][:], bef[0:1, :], float(E - 1), None, ALU.min).then_inc(tbl_rdy, 1)
                dve.wait_ge(w2e_rdy, q + 1)
                wv = wgt[:, g * TG * 2:(g + 1) * TG * 2].rearrange("p (t c) -> p t c", c=2)
                link(v_.tensor_scalar(mx[0], mx[2], 1.0, None, ALU.add))
                link(v_.reciprocal(mx[1], mx[0]))
                link(v_.tensor_copy(wv[:, :, 0], mx[1]))
                link(v_.tensor_tensor(wv[:, :, 1], mx[1], mx[2], ALU.mult))

            def blocks(l, g):
                meet(dve, "blocks", l, g)
                q = q_of(l, g)
                dve.wait_ge(tbl_rdy, 2 * q + 2)

                def result(j, par):
                    u = 2 * j + par
                    e = dve.value_load(be[g][0:1, ds(u, 1)], min_val=0, max_val=E - 1)
                    after(dve, yp_rdy, M0["blocks", l, g] + u + 1)
                    dve.wait_ge(ys_st[par], 16 * (1 + NPAR[par] * q + j))
                    for s in range(ST):
                        last = v_.tensor_tensor(ysb[par][:, s * D:(s + 1) * D], yP[par][:, s * D:(s + 1) * D],
                                                b2b[l][:, ds(e * D, D)], ALU.add)
                    last.then_inc(y_out, 1)
                split(0, 0, "blocks", l, g)
                with dve.Fori(0, H) as j:
                    split(j, 1, "blocks", l, g)
                    result(j, 0)
                    split(j + 1, 0, "blocks", l, g)
                    result(j, 1)
                result(H, 0)
                for par in range(2):
                    dve.wait_ge(ys_st[par], 16 * (1 + NPAR[par] * (q + 1)))

            def combine(l, g):
                q = q_of(l, g)
                base = n_link[0]
                h = BG // 2

                def add(j, par):
                    bb = 2 * j + par
                    for half in range(2):
                        dve.wait_ge(gath[par][half], 16 * TB * (h * q + j + 1))
                        for c in range(2):
                            for i in range(TB // 2):
                                t = g * TG + bb * TB + half * (TB // 2) + i
                                xt_ = x[:, ds(t * D, D)]
                                end = c == 1 and i == TB // 2 - 1
                                v_.scalar_tensor_tensor(xt_, got[half][:, (2 * i + c) * D:(2 * i + c + 1) * D],
                                                        wgt[:, ds(t * 2 + c, 1)], xt_, ALU.mult,
                                                        ALU.add).then_inc(comb if end else chain, 1)
                            if c == 0:
                                dve.wait_ge(chain, base + (TB - 1) * (2 * bb + half) + TB // 2)
                with dve.Fori(0, h) as j:
                    add(j, 0)
                    add(j, 1)
                n_link[0] += (TB - 1) * 2 * BG
                dve.wait_ge(chain, n_link[0])
                after(dve, comb, 2 * BG * (q + 1))

            order(project, gnn, relations, dense, blocks, combine)

        @block.tensor
        def _(pe):
            t_ = nc.tensor
            pe.wait_ge(c_ld, 16 * NC)
            pe.wait_ge(consts, NCONST)
            for l in range(2):
                n = NE[l] * C[l]
                t_.transpose(ps[0][:, 512 * l:512 * l + n], b1rows[l], ident[0:n, 0:n])
            t_.transpose(ps[1][:, 0:D], gw, ident[:])
            t_.matmul(ps[2][:, 0:2], gw, gacol[:], start=True, stop=True).then_inc(prep_pe, 1)

            def project(l, g):
                meet(pe, "project", l, g)
                q = q_of(l, g)
                if q == 0:
                    pe.wait_ge(prep_act, 4)
                    pe.wait_ge(prep_dve, 2)

                def turn(i, par):
                    n = q * QG + i
                    after(pe, xn4_rdy, n + 1)
                    after(pe, xT_rdy, n - 1)
                    for s in range(4):
                        last = t_.transpose(eP[:, 512 * par + s * P:512 * par + (s + 1) * P],
                                            xn4[par][:, s * D:(s + 1) * D], ident[:])
                    last.then_inc(xTp_rdy, 1)

                def multiply(i, par):
                    n = q * QG + i
                    after(pe, xT_rdy, n + 1)
                    after(pe, eb_used, n - 1)
                    after(pe, wh_used, n - 1)
                    t_.matmul(tP[par][:, 0:512], wa2b[:], xT4[par], start=True, stop=True).then_inc(ebP_rdy, 1)
                    for s in range(4):
                        t_.matmul(ps[3][:, 512 * par + s * D:512 * par + (s + 1) * D], xT4[par][:, s * P:(s + 1) * P],
                                  wcat[:], start=True, stop=True)
                        last = t_.matmul(tP[par][:, 512 + s:513 + s], xT4[par][:, s * P:(s + 1) * P],
                                         wa[:, 0:1], start=True, stop=True)
                    last.then_inc(whP_rdy, 1)
                with pe.Fori(0, QG // 2) as i:
                    turn(2 * i, 0)
                    turn(2 * i + 1, 1)
                    if l == 0:
                        multiply(2 * i, 0)
                        multiply(2 * i + 1, 1)

            def scores_of(bb, k):
                i0 = (bb * TB + k) * P
                for c in range(N // 512):
                    j0 = bb * N + c * 512
                    o = eP[:, c * 512:(c + 1) * 512]
                    hi_q, lo_q = qT[:, ds(i0, P)], qT[:, ds(TG * P + i0, P)]
                    hi_k, lo_k = kT[:, ds(j0, 512)], kT[:, ds(TG * P + j0, 512)]
                    t_.matmul(o, hi_q, hi_k, start=True, stop=False)
                    t_.matmul(o, hi_q, lo_k, start=False, stop=False)
                    last = t_.matmul(o, lo_q, hi_k, start=False, stop=True)
                return last

            def turn_of(par):
                for j in range(TB):
                    last = t_.transpose(tP[par][:, j * P:(j + 1) * P], pr[par][:, j * P:(j + 1) * P], ident[:])
                return last

            def sum_of(par, bb, bias):
                for j in range(TB):
                    last = t_.matmul(vP[par], pT[par][:, j * P:(j + 1) * P], vals[:, ds((bb * TB + j) * D, D)],
                                     start=(j == 0), stop=(j == TB - 1 and not bias))
                if bias:
                    last = t_.matmul(vP[par], ones_row[:], gbrow[:], start=False, stop=True)
                return last

            def gnn(l, g):
                meet(pe, "gnn", l, g)
                q = q_of(l, g)

                def similar(n, k, bb):
                    after(pe, y_rdy, n)
                    scores_of(bb, k).then_inc(e_rdy, 1)

                def turn(n, k):
                    after(pe, p_rdy, n + 1)
                    after(pe, tA_used, n - 1)
                    after(pe, tV_used, n - 1)
                    turn_of(k % 2).then_inc(t_rdy, 1)

                def sum_up(n, k, bb):
                    after(pe, tA_used, n + 1)
                    after(pe, tV_used, n + 1)
                    after(pe, v_used, n - 1)
                    sum_of(k % 2, bb, l == 1).then_inc(v_rdy, 1)

                with pe.Fori(0, BG) as bb:
                    n0 = (q * BG + bb) * TB
                    if l == 1:
                        similar(n0, 0, bb)
                    for k in range(TB):
                        if l == 1 and k + 1 < TB:
                            similar(n0 + k + 1, k + 1, bb)
                        turn(n0 + k, k)
                        if k >= 1:
                            sum_up(n0 + k - 1, k - 1, bb)
                    sum_up(n0 + TB - 1, TB - 1, bb)

            def relations(l, g):
                pe.wait_ge(flag_rdy, g + 1)
                flag = pe.value_load(others[g][0:1, 0:1], min_val=0, max_val=P)
                with pe.If(flag > 0):
                    with pe.Fori(1, 4) as r:
                        with pe.Fori(0, BG) as bb:
                            b = (r - 1) * BG + bb
                            with pe.Fori(0, TB) as k:
                                n = b * TB + k
                                after(pe, o_q[g], b + 1)
                                after(pe, o_s[g], n)
                                scores_of(bb, k).then_inc(o_e[g], 1)
                                after(pe, o_p[g], n + 1)
                                after(pe, o_c[g], n)
                                turn_of(0).then_inc(o_t[g], 1)
                                after(pe, o_c[g], n + 1)
                                after(pe, o_x[g], n)
                                sum_of(0, bb, False).then_inc(o_v[g], 1)

            def turn_unit(j, par, kind, l, g):
                q, u = q_of(l, g), 2 * j + par
                after(pe, xt_rdy, U0[kind, l, g] + u - 1)
                if kind == "dense":
                    after(pe, lg_rdy, q * US + u - 1)
                    after(pe, xb_made, q * US + u + 1)
                else:
                    pe.wait_ge(xb_ld[par], 16 * (NPAR[par] * q + j + 1))
                xp = xtP[par].rearrange("p (h s q) -> p h s q", h=2, s=ST)
                for s in range(ST):
                    for h in range(2):
                        last = t_.transpose(xp[:, h, s, :], xb[par][:, (2 * s + h) * D:(2 * s + h + 1) * D],
                                            ident16[:])
                last.then_inc(xtp_rdy, 1)

            def route_unit(j, par, l, g):
                u = 2 * j + par
                after(pe, xt_rdy, U0["dense", l, g] + u + 1)
                for s in range(ST):
                    hi, lo = xt[par][:, s * P:(s + 1) * P], xt[par][:, SPAN + s * P:SPAN + (s + 1) * P]
                    o = lgP[par][:, s * E:(s + 1) * E]
                    t_.matmul(o, hi, wrs[:, l, 0, :], start=True, stop=False)
                    t_.matmul(o, hi, wrs[:, l, 1, :], start=False, stop=False)
                    last = t_.matmul(o, lo, wrs[:, l, 0, :], start=False, stop=True)
                last.then_inc(lgp_rdy, 1)

            def up(j, par, kind, l, g, e):
                u = 2 * j + par
                after(pe, xt_rdy, U0[kind, l, g] + u + 1)
                after(pe, hf_rdy, M0[kind, l, g] + u - 1)
                f = F[l]
                for c in range(C[l]):
                    o = hP[par][:, c * SPAN:(c + 1) * SPAN]
                    hi = w1sp[l][:, ds(e * 2 * f + c * P, P)]
                    lo = w1sp[l][:, ds(e * 2 * f + f + c * P, P)]
                    t_.matmul(o, hi, xt[par][:, 0:SPAN], start=True, stop=False)
                    t_.matmul(o, hi, xt[par][:, SPAN:2 * SPAN], start=False, stop=False)
                    last = t_.matmul(o, lo, xt[par][:, 0:SPAN], start=False, stop=True)
                last.then_inc(hp_rdy, 1)

            def down(j, par, kind, l, g, e):
                u = 2 * j + par
                after(pe, hs_rdy, M0[kind, l, g] + u + 1)
                if kind == "dense":
                    after(pe, r_used, g * US + u - 1)
                else:
                    after(pe, y_out, BL0[kind, l, g] + u - 1)
                for s in range(ST):
                    o = yP[par][:, s * D:(s + 1) * D]
                    for c in range(C[l]):
                        w = e * C[l] * 2 * D + c * 2 * D
                        hi = hs[par][:, c * SPAN + s * P:c * SPAN + (s + 1) * P]
                        lo = hs[par][:, (4 + c) * SPAN + s * P:(4 + c) * SPAN + (s + 1) * P]
                        whi, wlo = w2sp[l][:, ds(w, D)], w2sp[l][:, ds(w + D, D)]
                        t_.matmul(o, hi, whi, start=(c == 0), stop=False)
                        t_.matmul(o, hi, wlo, start=False, stop=False)
                        last = t_.matmul(o, lo, whi, start=False, stop=(c == C[l] - 1))
                last.then_inc(yp_rdy, 1)

            def dense(l, g):
                meet(pe, "dense", l, g)
                q = q_of(l, g)
                if q == 0:
                    pe.wait_ge(w_used, NPIECES)
                k, J = "dense", US // 2
                if l == 0:
                    turn_unit(0, 0, k, l, g)
                    turn_unit(0, 1, k, l, g)
                    route_unit(0, 0, l, g)
                    up(0, 0, k, l, g, SH)
                    with pe.Fori(0, J - 1) as j:
                        turn_unit(j + 1, 0, k, l, g)
                        route_unit(j, 1, l, g)
                        up(j, 1, k, l, g, SH)
                        down(j, 0, k, l, g, SH)
                        turn_unit(j + 1, 1, k, l, g)
                        route_unit(j + 1, 0, l, g)
                        up(j + 1, 0, k, l, g, SH)
                        down(j, 1, k, l, g, SH)
                    route_unit(J - 1, 1, l, g)
                    up(J - 1, 1, k, l, g, SH)
                    down(J - 1, 0, k, l, g, SH)
                    down(J - 1, 1, k, l, g, SH)
                else:
                    with pe.Fori(0, J) as j:
                        turn_unit(j, 0, k, l, g)
                        turn_unit(j, 1, k, l, g)
                        route_unit(j, 0, l, g)
                        route_unit(j, 1, l, g)
                if l == 0:
                    pe.wait_ge(oth_rdy, g + 1)
                    t_.matmul(tP[0][0:1, 512:513], other16[:], ones16[:, 0:1], start=True,
                              stop=True).then_inc(othP_rdy, 1)
                pe.wait_ge(route_rdy, q + 1)
                t_.matmul(tP[0][:, 0:TG * E], before[:], oh16, start=True, stop=True)
                t_.matmul(tP[1][:, 0:TG * E], ones16[:], oh16, start=True, stop=True).then_inc(pos_rdy, 1)

            def blocks(l, g):
                meet(pe, "blocks", l, g)
                k = "blocks"
                pe.wait_ge(tbl_rdy, 2 * q_of(l, g) + 2)

                def expert(u):
                    return pe.value_load(be[g][0:1, ds(u, 1)], min_val=0, max_val=E - 1)
                turn_unit(0, 0, k, l, g)
                turn_unit(0, 1, k, l, g)
                up(0, 0, k, l, g, expert(0))
                with pe.Fori(0, H - 1) as j:
                    turn_unit(j + 1, 0, k, l, g)
                    up(j, 1, k, l, g, expert(2 * j + 1))
                    down(j, 0, k, l, g, expert(2 * j))
                    turn_unit(j + 1, 1, k, l, g)
                    up(j + 1, 0, k, l, g, expert(2 * j + 2))
                    down(j, 1, k, l, g, expert(2 * j + 1))
                turn_unit(H, 0, k, l, g)
                up(H - 1, 1, k, l, g, expert(2 * H - 1))
                down(H - 1, 0, k, l, g, expert(2 * H - 2))
                up(H, 0, k, l, g, expert(2 * H))
                down(H - 1, 1, k, l, g, expert(2 * H - 1))
                down(H, 0, k, l, g, expert(2 * H))

            order(project, gnn, relations, dense, blocks, lambda l, g: None)


_INS = ["x", "adj", "L0_gnn_W", "L0_gnn_a", "L0_ffn_Wr", "L0_ffn_W1s", "L0_ffn_b1s", "L0_ffn_W2s", "L0_ffn_b2s",
        "L0_ffn_W1p", "L0_ffn_b1p", "L0_ffn_W2p", "L0_ffn_b2p", "L1_gnn_a0", "L1_gnn_a1", "L1_gnn_a2", "L1_gnn_a3",
        "L1_gnn_bias", "L1_ffn_Wg", "L1_ffn_bg", "L1_ffn_bias", "L1_ffn_W1", "L1_ffn_b1", "L1_ffn_W2", "L1_ffn_b2"]


def kernel(**inputs):
    import numpy as _np
    import concourse.bacc as _bacc
    from concourse import mybir as _mybir
    from concourse.bass_utils import run_bass_kernel_spmd as _run

    nc = _bacc.Bacc("TRN2", target_bir_lowering=False, num_devices=1)
    arrays, args = {}, []
    for name in _INS:
        a = _np.ascontiguousarray(inputs[name])
        arrays[f"in_{name}_dram"] = a
        args.append(nc.dram_tensor(f"in_{name}_dram", a.shape, _mybir.dt.from_np(a.dtype), kind="ExternalInput").ap())
    args.append(nc.dram_tensor("out_0_dram", inputs["x"].shape, _mybir.dt.float32, kind="ExternalOutput").ap())
    bass_two_layers_of_gnn_and_moe(nc, *args)
    r = _run(nc, [arrays], core_ids=[0])
    return r.results[0]["out_0_dram"]
```

```python
import concourse.bass as bass
from concourse import mybir
from contextlib import ExitStack


def bass_two_layers_of_gnn_and_moe(
    nc: bass.Bass, x_in, adj_in, gnn_w, gnn_a, wr0, w1s, b1s, w2s, b2s, w1p, b1p, w2p, b2p,
    a0, a1, a2, a3, gbias, wg1, bg1, bias1, w1e, b1e, w2e, b2e, out,
):
    f32, f16, i32, u32 = mybir.dt.float32, mybir.dt.float16, mybir.dt.int32, mybir.dt.uint32
    ALU = mybir.AluOpType
    ACT = mybir.ActivationFunctionType
    AX = mybir.AxisListType
    ds = bass.ds

    P = 128
    B, N, D = x_in.shape
    TB = N // P
    T = B * TB
    NG = 2
    BG = B // NG
    TG = BG * TB
    E = wr0.shape[1]
    F = [w1s.shape[1], w1e.shape[2]]
    C = [f // P for f in F]
    SH = E
    NE = [E + 1, E]
    SPAN = 256
    ST = SPAN // P
    US = TG // ST
    NB = (2 * TG * P - E) // SPAN + E
    ROWS = NB * SPAN
    R = 4
    NRING = [(NB - i + R - 1) // R for i in range(R)]
    QG = TG // 4
    LEAK = 0.2
    NEG = -1e30
    FLOOR = -1e20
    EPS = 1e-5
    assert US % R == 0
    NA = 4
    NCONST = 8
    NC = 17
    NPIECES = 2 * sum(NE)
    CR = NA

    ctx = ExitStack()
    with ctx:
        def sb(name, shape, dt):
            return ctx.enter_context(nc.sbuf_tensor(name, shape, dt))

        def sem(name):
            return ctx.enter_context(nc.semaphore(name))

        xn_d = nc.dram_tensor("xn_rows", (NG * TG * P, 2 * D), f16, kind="Internal").ap()
        xs_d = [nc.dram_tensor(f"block_in{g}", (ROWS, 2 * D), f16, kind="Internal").ap() for g in range(NG)]
        ys_d = [nc.dram_tensor(f"block_out{g}", (ROWS, D), f32, kind="Internal").ap() for g in range(NG)]
        slot_d = nc.dram_tensor("slots", (NG * P, TG * 2), i32, kind="Internal").ap()

        x = sb("x", [P, T * D], f32)
        ident = sb("ident", [P, P], f32)
        ident16 = sb("ident16", [P, P], f16)
        before = sb("before", [P, P], f16)
        ones16 = sb("ones16", [P, P], f16)
        ones_row = sb("ones_row", [1, P], f32)
        zero16 = sb("zero16", [P, 256], f16)
        rank = sb("rank", [P, E], f32)
        blockno = sb("blockno", [P, NB], f32)
        wcat = sb("wcat", [P, D], f32)
        wa = sb("wa", [P, 2], f32)
        wa2b = sb("wa2b", [P, P], f32)
        gacol = sb("gacol", [P, 2], f32)
        akcol = sb("akcol", [P, 4], f32)
        gbrow = sb("gbrow", [1, D], f32)
        wrf = sb("wrf", [P, 2, E], f32)
        wrs = sb("wrs", [P, 2, 2, E], f16)
        gateb = sb("gateb", [P, 2, ST, E], f32)
        gtmp = sb("gtmp", [P, 2, E], f32)
        w1sp = [sb(f"w1sp{l}", [P, NE[l] * 2 * F[l]], f16) for l in range(2)]
        w2sp = [sb(f"w2sp{l}", [P, NE[l] * C[l] * 2 * D], f16) for l in range(2)]
        b1 = [sb(f"b1_{l}", [P, NE[l] * C[l]], f32) for l in range(2)]
        b2b = [sb(f"b2b{l}", [P, NE[l] * D], f32) for l in range(2)]
        adjb = [sb(f"adjb{i}", [P, N], i32) for i in range(NA)]
        stats = sb("stats", [P, 8, 6], f32)
        mv8 = sb("mv8", [P, 16], f32)
        mv = sb("mv", [P, TG * 2], f32)
        std = sb("std", [P, TG], f32)
        rstd = sb("rstd", [P, TG], f32)
        stage = [sb(f"stage{i}", [P, TB * 2 * D], f16) for i in range(2)]
        idx = [sb(f"idx{i}", [P, TB * 2], i32) for i in range(2)]
        got = [sb(f"got{i}", [P, 2 * D], f32) for i in range(R)]
        squares = sb("squares", [P, TG], f32)
        junk = sb("junk", [P, N], f32)

        KB = 256
        arena = sb("arena", [P, 75 * KB], f32)

        def at(kb, n, dt=f32):
            a = arena[:, int(kb * KB):int(kb * KB) + (n if dt == f32 else n // 2)]
            return a if dt == f32 else a.bitcast(dt)

        vals = at(0, TG * D)
        ejb = at(16, BG * N)
        kT = at(16, 2 * TG * P, f16)
        qT = at(32, 2 * TG * P, f16)
        ejc = at(32, N)
        zt = [at(48 + 4 * i, N) for i in range(2)]
        pr = [at(56 + 4 * i, N) for i in range(2)]
        pT = [at(64 + 4 * i, N) for i in range(2)]
        xn4 = [at(48 + 2 * i, 4 * D) for i in range(2)]
        xT4 = [at(52 + 2 * i, 4 * P) for i in range(2)]
        qf = [at(56 + 2 * i, 4 * P) for i in range(2)]
        ei = at(72, TG)
        mrow = at(72.5, 2)
        t1 = at(72.75, 1)
        t2 = at(73, 1)
        nmax = at(73.25, 1)
        shift1 = at(74, 2)
        shift2 = at(74.25, 2)
        rsum = at(73.5, 4)
        rcp = at(73.75, 2)
        gw = at(64, D)
        b1rows = [at(65 + l, P)[0:NE[l] * C[l], :] for l in range(2)]
        xf = [at(0 + i, ST * D) for i in range(2)]
        xb = [at(2 + i, ST * 2 * D, f16) for i in range(R)]
        xt = [at(6 + i, 2 * SPAN, f16) for i in range(R)]
        ysb = [at(10 + i, ST * D) for i in range(R)]
        hf = [at(14 + 4 * i, 4 * SPAN) for i in range(2)]
        hs = [at(22 + 4 * i, 2 * 4 * SPAN, f16) for i in range(R)]
        lg = at(38, TG * E)
        oh = [at(39 + i, TG * E) for i in range(2)]
        tm = [at(41 + i, TG * E) for i in range(3)]
        oh16 = at(44, TG * E, f16)
        cum = [at(45 + i, TG * E) for i in range(2)]
        mx = [at(47 + 0.25 * i, TG) for i in range(4)]
        small = at(48, 64)
        slf = at(49, 2 * TG)
        cmpb = at(50, NB * E)
        bef = at(52, NB)

        worst = sb("worst", [P, 1], f32)
        other16 = sb("other16", [P, 1], f16)
        others = [sb(f"others{g}", [1, 1], i32) for g in range(NG)]
        minus_half = sb("minus_half", [P, 1], f32)
        codes = sb("codes", [P, 4], f32)
        wgt = sb("wgt", [P, NG * TG * 2], f32)
        sl = sb("sl", [P, TG * 2], i32)
        be = [sb(f"be{g}", [1, NB], i32) for g in range(NG)]
        nb_i = sb("nb_i", [P, E], i32)

        ps = [ctx.enter_context(nc.psum_tensor(f"ps{i}", [P, 1024], f32)) for i in range(4)]
        eP = ps[0]
        tP = [ps[1], ps[2]]
        vP = [ps[3][:, 0:P], ps[3][:, 512:512 + P]]
        xtP = [ps[0][:, 512 * i:512 * i + SPAN].bitcast(f16) for i in range(2)]
        lgP = [ps[0][:, 512 * i + 384:512 * i + 384 + ST * E] for i in range(2)]
        hP = [ps[1], ps[2]]
        yP = [ps[3][:, 512 * i:512 * i + ST * D] for i in range(2)]

        x_ld = [sem(f"x_ld{i}") for i in range(NG)]
        c_ld = sem("c_ld")
        w_ld = [sem(f"w_ld{i}") for i in range(2)]
        adj_ld = [sem(f"adj_ld{i}") for i in range(NA)]
        xs_zero = sem("xs_zero")
        xb_ld = [sem(f"xb_ld{i}") for i in range(R)]
        xb_st = [sem(f"xb_st{i}") for i in range(R)]
        ys_st = [sem(f"ys_st{i}") for i in range(R)]
        slot_st = sem("slot_st")
        st_ld = [sem(f"st_ld{i}") for i in range(2)]
        scat = [sem(f"scat{i}") for i in range(2)]
        gi_ld = [sem(f"gi_ld{i}") for i in range(2)]
        gath = [sem(f"gath{i}") for i in range(R)]
        o_st = sem("o_st")
        w_used, consts, pchain, chain = sem("w_used"), sem("consts"), sem("pchain"), sem("chain")
        prep_pe, prep_act, prep_dve = sem("prep_pe"), sem("prep_act"), sem("prep_dve")
        over, scat_all, blocks_out = sem("over"), sem("scat_all"), sem("blocks_out")
        var_rdy, std_rdy = sem("var_rdy"), sem("std_rdy")
        route_rdy, pos_rdy, w2_rdy, w2e_rdy, tbl_rdy = (sem("route_rdy"), sem("pos_rdy"), sem("w2_rdy"),
                                                        sem("w2e_rdy"), sem("tbl_rdy"))

        counted = []

        def unit(name):
            counted.append(sem(name))
            return counted[-1]

        xn4_rdy, xTp_rdy, xT_rdy, ebP_rdy, eb_used = (unit("xn4_rdy"), unit("xTp_rdy"), unit("xT_rdy"),
                                                      unit("ebP_rdy"), unit("eb_used"))
        whP_rdy, wh_used, qf_rdy, khi_rdy, kq_rdy, h_rdy = (unit("whP_rdy"), unit("wh_used"), unit("qf_rdy"),
                                                            unit("khi_rdy"), unit("kq_rdy"), unit("h_rdy"))
        ejc_rdy, mask_rdy, z_rdy, nm_step, nmax_rdy = (unit("ejc_rdy"), unit("mask_rdy"), unit("z_rdy"),
                                                       unit("nm_step"), unit("nmax_rdy"))
        e_rdy, y_rdy, s_rdy, p_rdy, t_rdy = (unit("e_rdy"), unit("y_rdy"), unit("s_rdy"), unit("p_rdy"),
                                             unit("t_rdy"))
        t_used, v_rdy, rc_step, v_used = unit("t_used"), unit("v_rdy"), unit("rc_step"), unit("v_used")
        xb_made, xtp_rdy, xt_rdy, lgp_rdy, lg_rdy = (unit("xb_made"), unit("xtp_rdy"), unit("xt_rdy"),
                                                     unit("lgp_rdy"), unit("lg_rdy"))
        hp_rdy, hf_rdy, hhi_rdy, hs_rdy, yp_rdy = (unit("hp_rdy"), unit("hf_rdy"), unit("hhi_rdy"),
                                                   unit("hs_rdy"), unit("yp_rdy"))
        r_step, r_used, y_out = unit("r_step"), unit("r_used"), unit("y_out")
        first_in, comb = unit("first_in"), unit("comb")

        seen, oth_rdy, othP_rdy, flag_rdy = unit("seen"), sem("oth_rdy"), sem("othP_rdy"), sem("flag_rdy")
        o_ld = [sem(f"o_ld{g}") for g in range(NG)]
        o_half, o_q, o_e, o_s, o_max, o_p, o_t, o_c, o_v, o_x = (
            [unit(f"{n}{g}") for g in range(NG)]
            for n in ("o_half", "o_q", "o_e", "o_s", "o_max", "o_p", "o_t", "o_c", "o_v", "o_x"))

        def after(eng, semaphore, count):
            eng.wait_ge(semaphore, count + CR)

        ENGINES = 3

        def order(project, gnn, relations, dense, blocks, combine):
            for l in range(2):
                for g in range(NG):
                    project(l, g)
                    gnn(l, g)
                    if l == 1:
                        relations(l, g)
                    dense(l, g)
                for g in range(NG):
                    blocks(l, g)
            for g in range(NG):
                combine(1, g)

        COMBINED_IN = {("blocks", 0, 1): (0, 0), ("gnn", 1, 0): (0, 1), ("blocks", 1, 1): (1, 0)}

        MEET = {}

        def note(kind):
            def f(l, g):
                MEET[kind, l, g] = len(MEET) + 1
            return f
        order(note("project"), note("gnn"), lambda l, g: None, note("dense"), note("blocks"), lambda l, g: None)

        def meet(eng, kind, l, g):
            eng.drain().then_inc(over, 1)
            eng.wait_ge(over, ENGINES * MEET[kind, l, g])

        def q_of(l, g):
            return l * NG + g

        U0, M0, BL0 = {}, {}, {}
        u = m = bl = 0
        for l in range(2):
            for g in range(NG):
                U0["dense", l, g], M0["dense", l, g], BL0["dense", l, g] = u, m, bl
                u += US
                m += US if l == 0 else 0
            for g in range(NG):
                U0["blocks", l, g], M0["blocks", l, g], BL0["blocks", l, g] = u, m, bl
                u += NB
                m += NB
                bl += NB

        def shifted(w, i, by, ring=R):
            return w + (i + by) // ring, (i + by) % ring

        def each_unit(eng, n, step, ahead, lag, ring=R):
            rounds = (n - ring - ahead) // ring
            assert lag <= ring and rounds > 0

            def peeled(u):
                step(u // ring, u % ring, lambda by: 0 <= u + by < n)
            for u in range(ring):
                peeled(u)
            with eng.Fori(1, 1 + rounds) as w:
                for i in range(ring):
                    step(w, i, lambda by: True)
            for u in range(ring * (1 + rounds), n + lag):
                peeled(u)

        def expert_of(eng, g, u):
            return nc.values_load(be[g][0:1, ds(u, 1)], engines=[eng.engine], min_val=0, max_val=E - 1,
                                  skip_runtime_bounds_check_because="route() clamps it to E - 1, and it is a count")

        block = ctx.enter_context(nc.Block())

        @block.sync
        def _(sp):
            for c in counted:
                sp.sem_inc(c, CR)
            for c in (*xb_st, *ys_st):
                sp.sem_inc(c, 16)
            xv = x_in.rearrange("b (t p) d -> p (b t) d", p=P)
            ov = out.rearrange("b (t p) d -> p (b t) d", p=P)
            sp.dma_start(x[:, 0:TG * D].rearrange("p (t d) -> p t d", d=D), xv[:, 0:TG, :]).then_inc(x_ld[0], 16)
            small_loads = [
                (gw, gnn_w), (gacol[:], gnn_a.rearrange("(k p) -> p k", p=P)),
                (gbrow[:], gbias.rearrange("(o d) -> o d", o=1)),
                (wrf[:, 0, :], wr0), (wrf[:, 1, :], wg1),
                (b1rows[0][0:E * C[0], :], b1p.rearrange("e (c p) -> (e c) p", p=P)),
                (b1rows[0][E * C[0]:NE[0] * C[0], :], b1s.rearrange("(c p) -> c p", p=P)),
                (b1rows[1], b1e.rearrange("e (c p) -> (e c) p", p=P)),
                (b2b[0][:, 0:E * D], b2p.rearrange("e d -> (e d)").partition_broadcast(P)),
                (b2b[0][:, E * D:NE[0] * D], b2s.partition_broadcast(P)),
                (b2b[1][:, :], b2e.rearrange("e d -> (e d)").partition_broadcast(P)),
                (gtmp[:, 0, :], bg1.partition_broadcast(P)), (gtmp[:, 1, :], bias1.partition_broadcast(P)),
            ] + [(akcol[:, k:k + 1], a) for k, a in enumerate([a0, a1, a2, a3])]
            assert len(small_loads) == NC
            with nc.allow_non_contiguous_dma(reason="a few small vectors"):
                for dst, src in small_loads:
                    sp.dma_start(dst, src).then_inc(c_ld, 16)
            sp.dma_start(x[:, TG * D:T * D].rearrange("p (t d) -> p t d", d=D), xv[:, TG:T, :]).then_inc(x_ld[1], 16)

            def project(l, g):
                pass

            def gnn(l, g):
                with sp.Fori(0, BG) as bb:
                    for k in range(TB):
                        n = (q_of(l, g) * BG + bb) * TB + k
                        if l == 0:
                            after(sp, mask_rdy, n - NA + 1)
                        else:
                            after(sp, p_rdy, n - NA + 1)
                            sp.nop(nofuse=True)
                            after(sp, seen, n - NG * TG - NA + 1)
                        sp.nop(nofuse=True)
                        sp.dma_start(adjb[k % NA][:], adj_in[ds(g * BG + bb, 1), k * P:(k + 1) * P, :]
                                     .rearrange("o p n -> (o p) n")).then_inc(adj_ld[k % NA], 16)
                if l == 0 and g == 0:
                    sp.wait_ge(consts, NCONST)
                    for gg in range(NG):
                        sp.dma_start(xs_d[gg].rearrange("(p r) c -> p (r c)", p=P)
                                     .rearrange("p (r c) -> p r c", c=256),
                                     zero16[:].rearrange("p (o c) -> p o c", o=1)
                                     .to_broadcast([P, ROWS * 2 * D // (P * 256), 256])).then_inc(xs_zero, 16)

            def relations(l, g):
                sp.wait_ge(flag_rdy, g + 1)
                flag = sp.value_load(others[g][0:1, 0:1], min_val=0, max_val=P)
                with sp.If(flag > 0):
                    after(sp, p_rdy, (q_of(l, g) + 1) * TG)
                    with sp.Fori(1, 4) as r:
                        with sp.Fori(0, BG) as bb:
                            with sp.Fori(0, TB) as k:
                                after(sp, o_p[g], ((r - 1) * BG + bb) * TB + k)
                                sp.dma_start(adjb[0][:], adj_in[ds(g * BG + bb, 1), ds(k * P, P), :]
                                             .rearrange("o p n -> (o p) n")).then_inc(o_ld[g], 16)

            def dense(l, g):
                q = q_of(l, g)
                if l == 1:
                    sp.wait_ge(scat_all, g + 1)

                with sp.Fori(0, US // R) as w:
                    for i in range(R):
                        u = R * w + i
                        after(sp, xb_made, q * US + u + 1)
                        sp.dma_start(xn_d[ds(g * TG * P + u * SPAN, SPAN), :].rearrange("(s p) c -> p s c", p=P),
                                     xb[i].rearrange("p (s c) -> p s c", s=ST)).then_inc(xb_st[i], 16)
                sp.wait_ge(tbl_rdy, 2 * q + 1)
                if l == 1:
                    after(sp, comb, TG * (g + 1))
                sp.dma_start(slot_d[g * P:(g + 1) * P, :], sl[:]).then_inc(slot_st, 16)

            def blocks(l, g):
                q = q_of(l, g)
                sp.wait_ge(over, ENGINES * MEET["blocks", l, g])
                sp.wait_ge(scat_all, q + 1)
                if l == 1:
                    after(sp, comb, TG * (g + 1))

                def load(w, i):
                    u = R * w + i
                    after(sp, xtp_rdy, U0["blocks", l, g] + u - R + 1)
                    sp.dma_start(xb[i].rearrange("p (s c) -> p s c", s=ST),
                                 xs_d[g][ds(u * SPAN, SPAN), :].rearrange("(s p) c -> p s c", p=P)
                                 ).then_inc(xb_ld[i], 16)

                def store(w, i):
                    u = R * w + i
                    after(sp, y_out, BL0["blocks", l, g] + u + 1)
                    sp.dma_start(ys_d[g][ds(u * SPAN, SPAN), :].rearrange("(s p) d -> p s d", p=P),
                                 ysb[i].rearrange("p (s d) -> p s d", s=ST)).then_inc(ys_st[i], 16)

                def step(w, i, has):
                    if has(R):
                        load(w + 1, i)
                    if has(-R):
                        store(w - 1, i)
                for i in range(R):
                    load(0, i)
                each_unit(sp, NB, step, R, R)
                for i in range(R):
                    sp.wait_ge(ys_st[i], 16 * (1 + NRING[i] * (q + 1)))
                sp.sem_inc(blocks_out, 1)

            def combine(l, g):
                if l == 1:
                    for bb in range(BG):
                        t = (g * BG + bb) * TB
                        after(sp, comb, (q_of(l, g) * BG + bb + 1) * TB)
                        sp.dma_start(ov[:, t:t + TB, :],
                                     x[:, t * D:(t + TB) * D].rearrange("p (t d) -> p t d", d=D)).then_inc(o_st, 16)
            order(project, gnn, relations, dense, blocks, combine)
            sp.wait_ge(o_st, 16 * B)

        @block.gpsimd
        def _(pool):
            n_link = [0]

            def link(ins):
                n_link[0] += 1
                ins.then_inc(pchain, 1)
                pool.wait_ge(pchain, n_link[0])

            g_ = nc.gpsimd
            link(g_.memset(ident[:], 0.0))
            link(g_.affine_select(out=ident[:], in_=ident[:], compare_op=ALU.not_equal, fill=1.0, base=0,
                                  pattern=[[-1, P]], channel_multiplier=1))
            g_.memset(ones_row[:], 1.0).then_inc(consts, 1)
            g_.memset(zero16[:], 0.0).then_inc(consts, 1)
            g_.memset(ones16[:], 1.0).then_inc(consts, 1)
            link(g_.memset(before[:], 1.0))
            g_.affine_select(out=before[:], in_=before[:], compare_op=ALU.is_gt, fill=0.0, base=0,
                             pattern=[[1, P]], channel_multiplier=-1).then_inc(consts, 1)
            g_.iota(rank[:], pattern=[[-1, E]], base=E, channel_multiplier=0,
                    allow_small_or_imprecise_dtypes=True).then_inc(consts, 1)
            g_.iota(blockno[:], pattern=[[1, NB]], base=0, channel_multiplier=0,
                    allow_small_or_imprecise_dtypes=True).then_inc(consts, 1)
            g_.iota(codes[:], pattern=[[1, 4]], base=1, channel_multiplier=0,
                    allow_small_or_imprecise_dtypes=True).then_inc(consts, 1)
            g_.tensor_copy(ident16[:], ident[:]).then_inc(consts, 1)

            pieces = []
            for l in range(2):
                f, c = F[l], C[l]
                for e in range(NE[l]):
                    w1 = (w1s if e == SH else w1p[e]) if l == 0 else w1e[e]
                    w2 = (w2s if e == SH else w2p[e]) if l == 0 else w2e[e]
                    to1 = w1sp[l][:, e * 2 * f:(e + 1) * 2 * f].rearrange("p (h f) -> p h f", h=2)
                    to2 = (w2sp[l][:, e * c * 2 * D:(e + 1) * c * 2 * D]
                           .rearrange("p (c h d) -> p h c d", c=c, h=2))
                    pieces.append((w1, 0, to1[:, 0, :], to1[:, 1, :], f))
                    pieces.append((w2.rearrange("(c p) d -> p c d", p=P), c, to2[:, 0], to2[:, 1], f))
            assert len(pieces) == NPIECES

            def staged(i):
                c, f = pieces[i][1], pieces[i][4]
                w = stage[i % 2].bitcast(f32)[:, 0:f]
                return w.rearrange("p (c d) -> p c d", c=c) if c else w

            def fetch(i):
                if i >= 2:
                    pool.wait_ge(w_used, i - 1)
                pool.dma_start(staged(i), pieces[i][0]).then_inc(w_ld[i % 2], 16)

            def split_piece(i):
                _, _, hi, lo, _ = pieces[i]
                if i + 1 < len(pieces):
                    fetch(i + 1)
                pool.wait_ge(w_ld[i % 2], 16 * (i // 2 + 1))
                link(g_.tensor_copy(hi, staged(i)))
                g_.tensor_tensor(lo, staged(i), hi, ALU.subtract).then_inc(w_used, 1)

            fetch(0)
            for i in range(NPIECES):
                split_piece(i)

            h = BG // 2

            def slots_of(g, bb):
                return slot_d[g * P:(g + 1) * P, ds(bb * 2 * TB, 2 * TB)]

            def scatter(l, g):
                q = q_of(l, g)
                pool.wait_ge(slot_st, 16 * (q + 1))
                if q == 0:
                    pool.wait_ge(xs_zero, 16 * NG)
                if l == 1:
                    pool.wait_ge(blocks_out, g + 1)
                for i in range(R):
                    pool.wait_ge(xb_st[i], 16 * (1 + (q + 1) * US // R))

                def load(j, par):
                    pool.dma_start(idx[par][:], slots_of(g, 2 * j + par)).then_inc(st_ld[par], 16)
                    pool.dma_start(stage[par][:].rearrange("p (t c) -> p t c", t=TB),
                                   xn_d[ds((g * TG + (2 * j + par) * TB) * P, TB * P), :]
                                   .rearrange("(t p) c -> p t c", p=P)).then_inc(st_ld[par], 16)

                def rows_out(j, par):
                    pool.wait_ge(st_ld[par], 32 * (h * q + j + 1))
                    pool.nop(nofuse=True)
                    for k in range(TB):
                        for c in range(2):
                            pool.indirect_dma_start(
                                out=xs_d[g][:, :],
                                out_offset=bass.IndirectOffsetOnAxis(ap=idx[par][:, 2 * k + c:2 * k + c + 1], axis=0),
                                in_=stage[par][:, k * 2 * D:(k + 1) * 2 * D], in_offset=None).then_inc(scat[par], 16)

                def all_out(j, par):
                    pool.wait_ge(scat[par], 16 * 2 * TB * (h * q + j + 1))
                load(0, 0)
                load(0, 1)
                with pool.Fori(0, h - 1) as j:
                    rows_out(j, 0)
                    rows_out(j, 1)
                    for par in range(2):
                        all_out(j, par)
                        load(j + 1, par)
                rows_out(h - 1, 0)
                rows_out(h - 1, 1)
                all_out(h - 1, 0)
                all_out(h - 1, 1)
                pool.sem_inc(scat_all, 1)

            def gather(l, g):
                q = q_of(l, g)
                pool.wait_ge(blocks_out, q + 1)

                def load(j, par):
                    pool.dma_start(idx[par][:], slots_of(g, 2 * j + par)).then_inc(gi_ld[par], 16)

                def rows_in(j, par):
                    pool.wait_ge(gi_ld[par], 16 * (h * q + j + 1))
                    for k in range(TB):
                        after(pool, comb, (BG * q + 2 * j + par) * TB + k - R + 1)
                        pool.nop(nofuse=True)
                        for c in range(2):
                            pool.indirect_dma_start(
                                out=got[k % R][:, c * D:(c + 1) * D], out_offset=None, in_=ys_d[g][:, :],
                                in_offset=bass.IndirectOffsetOnAxis(ap=idx[par][:, 2 * k + c:2 * k + c + 1], axis=0),
                            ).then_inc(gath[k % R], 16)

                def all_in(j, par):
                    for i in range(R):
                        pool.wait_ge(gath[i], 32 * (BG * q + 2 * j + par + 1) * (TB // R))
                load(0, 0)
                load(0, 1)
                with pool.Fori(0, h - 1) as j:
                    rows_in(j, 0)
                    rows_in(j, 1)
                    for par in range(2):
                        all_in(j, par)
                        load(j + 1, par)
                rows_in(h - 1, 0)
                rows_in(h - 1, 1)
                all_in(h - 1, 0)
                all_in(h - 1, 1)

            for l in range(2):
                for g in range(NG):
                    scatter(l, g)
                for g in range(NG):
                    gather(l, g)

        @block.scalar
        def _(act):
            s_ = nc.scalar
            act.wait_ge(prep_pe, 1)
            act.wait_ge(prep_dve, 1)
            for l in range(2):
                s_.copy(b1[l][:], ps[0][:, 512 * l:512 * l + NE[l] * C[l]]).then_inc(prep_act, 1)
            s_.copy(wcat[:], ps[1][:, 0:D]).then_inc(prep_act, 1)
            s_.copy(wa[:], ps[2][:, 0:2]).then_inc(prep_act, 1)

            def deviation(n):
                act.wait_ge(var_rdy, n)
                s_.activation(std[:], std[:], ACT.Sqrt).then_inc(std_rdy, 1)

            def project(l, g):
                meet(act, "project", l, g)
                q = q_of(l, g)
                deviation(2 * q + 1)

                def quad(i, par):
                    n = q * QG + i
                    after(act, xTp_rdy, n + 1)
                    if l == 0:
                        after(act, whP_rdy, n - 1)
                        s_.copy(xT4[par], eP[:, 512 * par:512 * par + 512]).then_inc(xT_rdy, 1)
                        after(act, ebP_rdy, n + 1)
                        s_.copy(ejb[:, ds(i * 512, 512)], tP[par][:, 0:512]).then_inc(eb_used, 1)
                    else:
                        m = n - NG * QG
                        after(act, kq_rdy, m - 1)
                        s_.copy(xT4[par], eP[:, 512 * par:512 * par + 512]).then_inc(xT_rdy, 1)
                        after(act, xT_rdy, n + 1)
                        s_.activation(qf[par], xT4[par], ACT.Copy, scale=akcol[:, 0:1]).then_inc(qf_rdy, 1)
                        s_.copy(vals[:, ds(i * 4 * D, 4 * D)], xn4[par]).then_inc(h_rdy, 1)
                with act.Fori(0, QG // 2) as i:
                    quad(2 * i, 0)
                    quad(2 * i + 1, 1)

            def gnn(l, g):
                meet(act, "gnn", l, g)
                q = q_of(l, g)

                def weights(n, k):
                    par = k % 2
                    after(act, t_rdy, n - 1)
                    if l == 0:
                        after(act, nmax_rdy, n + 1)
                        s_.activation(pr[par], zt[par], ACT.Exp, scale=LEAK, bias=shift2[:, par:par + 1])
                        s_.activation(zt[par], zt[par], ACT.Exp, bias=shift1[:, par:par + 1]).then_inc(y_rdy, 1)
                    else:
                        after(act, e_rdy, n - NG * TG + 1)
                        after(act, p_rdy, n - 1)
                        s_.activation(pr[par], eP[:, :], ACT.Sigmoid, scale=LEAK)
                        s_.activation(zt[par], eP[:, :], ACT.Sigmoid).then_inc(y_rdy, 1)

                def evacuate(n, k):
                    par = k % 2
                    after(act, t_rdy, n + 1)
                    after(act, v_rdy, n - 1)
                    s_.copy(pT[par], tP[par][:, :]).then_inc(t_used, 1)

                def look(n, bb, k):
                    act.wait_ge(adj_ld[k % NA], 16 * ((q * BG + bb) * (TB // NA) + k // NA + 1))
                    after(act, seen, n - NG * TG)
                    s_.activation(junk[:], adjb[k % NA][:], ACT.Square, bias=minus_half[:, 0:1],
                                  accum_out=squares[:, ds(bb * TB + k, 1)]).then_inc(seen, 1)

                def step(bb, k, has):
                    n = (q * BG + bb) * TB + k
                    if l == 0:
                        if has(0):
                            weights(n, k)
                        if has(-1):
                            evacuate(n - 1, (k - 1) % TB)
                    else:
                        if has(-1):
                            evacuate(n - 1, (k - 1) % TB)
                        if has(1):
                            weights(n + 1, (k + 1) % TB)
                        if has(0):
                            look(n, bb, k)
                if l == 1:
                    weights(q * TG, 0)
                each_unit(act, TG, step, l, 1, TB)

            def relations(l, g):
                act.wait_ge(flag_rdy, g + 1)
                flag = act.value_load(others[g][0:1, 0:1], min_val=0, max_val=P)
                with act.If(flag > 0):
                    with act.Fori(1, 4) as r:
                        with act.Fori(0, BG) as bb:
                            with act.Fori(0, TB) as k:
                                n = ((r - 1) * BG + bb) * TB + k
                                after(act, o_e[g], n + 1)
                                after(act, o_p[g], n)
                                after(act, o_t[g], n)
                                s_.activation(pr[0], eP[:, :], ACT.Sigmoid, scale=LEAK)
                                s_.activation(zt[0], eP[:, :], ACT.Sigmoid).then_inc(o_s[g], 1)

            def to_sbuf(w, i, kind, l, g):
                u = R * w + i
                after(act, xtp_rdy, U0[kind, l, g] + u + 1)
                if kind == "dense" and l == 1:
                    after(act, lgp_rdy, q_of(l, g) * US + u - R + 1)
                else:
                    after(act, hp_rdy, M0[kind, l, g] + u - R + 1)
                s_.copy(xt[i], xtP[i % 2]).then_inc(xt_rdy, 1)

            def hidden(w, i, kind, l, g, e):
                m = M0[kind, l, g] + R * w + i
                par = i % 2
                after(act, hp_rdy, m + 1)
                after(act, hs_rdy, m - 1)
                for c in range(C[l]):
                    last = s_.activation(hf[par][:, c * SPAN:(c + 1) * SPAN], hP[par][:, c * SPAN:(c + 1) * SPAN],
                                         ACT.Gelu if l == 0 else ACT.Relu, bias=b1[l][:, ds(e * C[l] + c, 1)])
                last.then_inc(hf_rdy, 1)

            def through_experts(kind, l, g, n, expert):
                def step(w, i, has):
                    if has(0):
                        hidden(w, i, kind, l, g, expert(R * w + i))
                    if has(2):
                        to_sbuf(*shifted(w, i, 2), kind, l, g)
                to_sbuf(0, 0, kind, l, g)
                to_sbuf(0, 1, kind, l, g)
                each_unit(act, n, step, 2, 0)

            def dense(l, g):
                meet(act, "dense", l, g)
                deviation(2 * q_of(l, g) + 2)
                if l == 0:
                    through_experts("dense", l, g, US, lambda u: SH)
                else:
                    with act.Fori(0, US // R) as w:
                        for i in range(R):
                            to_sbuf(w, i, "dense", l, g)
                act.wait_ge(w2_rdy, q_of(l, g) + 1)
                s_.activation(mx[2], mx[2], ACT.Exp).then_inc(w2e_rdy, 1)

            def blocks(l, g):
                meet(act, "blocks", l, g)
                act.wait_ge(tbl_rdy, 2 * q_of(l, g) + 2)
                through_experts("blocks", l, g, NB,
                                lambda u: expert_of(act, g, u))

            order(project, gnn, relations, dense, blocks, lambda l, g: None)

        @block.vector
        def _(dve):
            v_ = nc.vector
            n_link = [0]

            def link(ins):
                n_link[0] += 1
                ins.then_inc(chain, 1)
                dve.wait_ge(chain, n_link[0])

            dve.wait_ge(c_ld, 16 * NC)
            dve.wait_ge(consts, NCONST)
            link(v_.tensor_copy(wrs[:, :, 0, :], wrf[:]))
            v_.memset(gateb[:, 0], 0.0)
            v_.memset(minus_half[:], -0.5)
            for s in range(ST):
                v_.tensor_tensor(gateb[:, 1, s], gtmp[:, 0, :], gtmp[:, 1, :], ALU.add)
            v_.tensor_tensor(wrs[:, :, 1, :], wrf[:], wrs[:, :, 0, :], ALU.subtract).then_inc(prep_dve, 1)
            dve.wait_ge(prep_act, 4)
            v_.tensor_copy(wa2b[:], wa[:, 1:2].to_broadcast([P, P])).then_inc(prep_dve, 1)

            def add_tile(l, g, w, i):
                n = q_of(l, g) * TG + R * w + i
                t = g * TG + R * w + i
                xt_ = x[:, ds(t * D, D)]
                dve.wait_ge(gath[i], 32 * (q_of(l, g) * (TG // R) + w + 1))
                v_.scalar_tensor_tensor(xt_, got[i][:, 0:D], wgt[:, ds(t * 2, 1)], xt_, ALU.mult,
                                        ALU.add).then_inc(first_in, 1)
                after(dve, first_in, n + 1)
                v_.scalar_tensor_tensor(xt_, got[i][:, D:2 * D], wgt[:, ds(t * 2 + 1, 1)], xt_, ALU.mult,
                                        ALU.add).then_inc(comb, 1)

            def statistics(n, g):
                base = n_link[0]
                with dve.Fori(0, TG // 8) as i:
                    for s in range(8):
                        v_.bn_stats(stats[:, s, :], x[:, ds((g * TG + 8 * i + s) * D, D)]).then_inc(chain, 1)
                    dve.wait_ge(chain, base + 17 * i + 8)
                    dve.nop(nofuse=True)
                    for s in range(8):
                        v_.bn_aggr(mv8[:, 2 * s:2 * s + 2], stats[:, s, :]).then_inc(chain, 1)
                    dve.wait_ge(chain, base + 17 * i + 16)
                    v_.tensor_copy(mv[:, ds(16 * i, 16)], mv8[:]).then_inc(chain, 1)
                    dve.wait_ge(chain, base + 17 * i + 17)
                n_link[0] += 17 * (TG // 8)
                v_.tensor_scalar(std[:], mv[:].rearrange("p (t k) -> p t k", k=2)[:, :, 1], EPS, None,
                                 ALU.add).then_inc(var_rdy, 1)
                dve.wait_ge(std_rdy, n)
                link(v_.reciprocal(rstd[:], std[:]))

            def project(l, g):
                meet(dve, "project", l, g)
                q = q_of(l, g)
                if l == 0:
                    dve.wait_ge(x_ld[g], 16)
                statistics(2 * q + 1, g)

                def normal(i, par):
                    n = q * QG + i
                    after(dve, xTp_rdy, n - 1)
                    if l == 1:
                        after(dve, h_rdy, n - NG * QG - 1)
                    for s in range(4):
                        t = 4 * i + s
                        last = v_.tensor_scalar(xn4[par][:, s * D:(s + 1) * D], x[:, ds((g * TG + t) * D, D)],
                                                mv[:, ds(2 * t, 1)], rstd[:, ds(t, 1)], ALU.subtract, ALU.mult)
                    last.then_inc(xn4_rdy, 1)

                def collect(i, par):
                    n = q * QG + i
                    if l == 0:
                        after(dve, whP_rdy, n + 1)
                        v_.tensor_copy(vals[:, ds(i * 4 * D, 4 * D)], ps[3][:, 512 * par:512 * par + 512])
                        v_.tensor_copy(ei[:, ds(i * 4, 4)], tP[par][:, 512:516]).then_inc(wh_used, 1)
                    else:
                        m = n - NG * QG
                        after(dve, xT_rdy, n + 1)
                        v_.tensor_copy(kT[:, ds(i * 512, 512)], xT4[par]).then_inc(khi_rdy, 1)
                        after(dve, qf_rdy, m + 1)
                        v_.tensor_copy(qT[:, ds(i * 512, 512)], qf[par]).then_inc(khi_rdy, 1)
                        after(dve, khi_rdy, 2 * m + 1)
                        v_.tensor_tensor(kT[:, ds(TG * P + i * 512, 512)], xT4[par], kT[:, ds(i * 512, 512)],
                                         ALU.subtract)
                        after(dve, khi_rdy, 2 * m + 2)
                        v_.tensor_tensor(qT[:, ds(TG * P + i * 512, 512)], qf[par], qT[:, ds(i * 512, 512)],
                                         ALU.subtract).then_inc(kq_rdy, 1)
                normal(0, 0)
                with dve.Fori(0, QG // 2 - 1) as i:
                    normal(2 * i + 1, 1)
                    collect(2 * i, 0)
                    normal(2 * i + 2, 0)
                    collect(2 * i + 1, 1)
                normal(QG - 1, 1)
                collect(QG - 2, 0)
                collect(QG - 1, 1)

            def gnn(l, g):
                meet(dve, "gnn", l, g)
                q = q_of(l, g)

                def adj_in_sbuf(bb, k):
                    dve.wait_ge(adj_ld[k % NA], 16 * ((q * BG + bb) * (TB // NA) + k // NA + 1))

                def own_batch(n, bb):
                    after(dve, z_rdy, n)
                    v_.tensor_copy(ejc, ejb[:, ds(bb * N, N)]).then_inc(ejc_rdy, 1)

                def masks(n, k, bb):
                    par = k % 2
                    adj_in_sbuf(bb, k)
                    after(dve, p_rdy, n - 1)
                    v_.tensor_scalar(zt[par], adjb[k % NA][:], 0.0, NEG, ALU.is_equal,
                                     ALU.mult).then_inc(mask_rdy, 1)

                def maximum(n, k, bb):
                    par = k % 2
                    after(dve, mask_rdy, n + 1)
                    after(dve, ejc_rdy, q * BG + bb + 1)
                    dve.nop(nofuse=True)
                    v_.tensor_tensor_reduce(out=zt[par], in0=zt[par], in1=ejc, scale=1.0, scalar=2 * NEG,
                                            op0=ALU.add, op1=ALU.max,
                                            accum_out=mrow[:, par:par + 1]).then_inc(z_rdy, 1)

                def shift_a(n, k, bb):
                    after(dve, z_rdy, n + 1)
                    v_.tensor_scalar(t1, mrow[:, k % 2:k % 2 + 1], ei[:, ds(bb * TB + k, 1)], FLOOR,
                                     ALU.add, ALU.max).then_inc(nm_step, 1)

                def shift_b(n):
                    after(dve, nm_step, 3 * n + 1)
                    v_.tensor_scalar(t2, t1, -LEAK, None, ALU.mult).then_inc(nm_step, 1)

                def shift_c(n):
                    after(dve, nm_step, 3 * n + 2)
                    v_.scalar_tensor_tensor(nmax, t1, -1.0, t2, ALU.mult, ALU.min).then_inc(nm_step, 1)

                def shift_d(n, k, bb):
                    par = k % 2
                    eik = ei[:, ds(bb * TB + k, 1)]
                    after(dve, nm_step, 3 * n + 3)
                    v_.tensor_tensor(shift1[:, par:par + 1], eik, nmax, ALU.add)
                    v_.scalar_tensor_tensor(shift2[:, par:par + 1], eik, LEAK, nmax, ALU.mult,
                                            ALU.add).then_inc(nmax_rdy, 1)

                def larger(n, k):
                    par = k % 2
                    after(dve, y_rdy, n + 1)
                    v_.scalar_tensor_tensor(pr[par], zt[par], 1.0, pr[par], ALU.mult, ALU.max,
                                            accum_out=rsum[:, k % 4:k % 4 + 1]).then_inc(p_rdy, 1)

                def larger_and_masked(n, k, bb):
                    par, m = k % 2, n - NG * TG
                    after(dve, y_rdy, n + 1)
                    v_.tensor_tensor(zt[par], zt[par], pr[par], ALU.max).then_inc(s_rdy, 1)
                    after(dve, s_rdy, m + 1)
                    adj_in_sbuf(bb, k)
                    v_.scalar_tensor_tensor(pr[par], adjb[k % NA][:], 1.0, zt[par], ALU.is_equal,
                                            ALU.mult).then_inc(p_rdy, 1)

                def inverse_a(n, k):
                    after(dve, p_rdy, n + 1)
                    v_.tensor_scalar(rcp[:, k % 2:k % 2 + 1], rsum[:, k % 4:k % 4 + 1], 1e-30, None,
                                     ALU.max).then_inc(rc_step, 1)

                def inverse_b(n, k):
                    after(dve, rc_step, 2 * n + 1)
                    v_.reciprocal(rcp[:, k % 2:k % 2 + 1], rcp[:, k % 2:k % 2 + 1]).then_inc(rc_step, 1)

                def finish(n, k, bb):
                    xt_ = x[:, ds((g * TG + bb * TB + k) * D, D)]
                    after(dve, v_rdy, n + 1)
                    if l == 0:
                        after(dve, rc_step, 2 * n + 2)
                    v_.scalar_tensor_tensor(xt_, vP[k % 2], rcp[:, k % 2:k % 2 + 1] if l == 0 else 1.0, xt_,
                                            ALU.mult, ALU.add).then_inc(v_used, 1)

                def step(bb, k, has):
                    n = (q * BG + bb) * TB + k
                    if l == 0:
                        b3, k3 = shifted(bb, k, -3, TB)
                        if has(0):
                            if k == 0:
                                own_batch(n, bb)
                            masks(n, k, bb)
                        if has(-3):
                            inverse_a(n - 3, k3)
                        if has(0):
                            maximum(n, k, bb)
                        if has(-3):
                            inverse_b(n - 3, k3)
                        if has(0):
                            shift_a(n, k, bb)
                        if has(-3):
                            finish(n - 3, k3, b3)
                        if has(0):
                            shift_b(n)
                            shift_c(n)
                            shift_d(n, k, bb)
                        if has(-1):
                            larger(n - 1, (k - 1) % TB)
                    else:
                        if has(0):
                            larger_and_masked(n, k, bb)
                        if has(-2):
                            b2, k2 = shifted(bb, k, -2, TB)
                            finish(n - 2, k2, b2)
                        if has(0) and combined:
                            add_tile(*combined, bb * (TB // R) + k // R, k % R)
                combined = COMBINED_IN.get(("gnn", l, g))
                each_unit(dve, TG, step, 0, 3 - l, TB)
                if combined:
                    after(dve, comb, TG * (q_of(*combined) + 1))

            def relations(l, g):
                q = q_of(l, g)
                after(dve, seen, (g + 1) * TG)
                link(v_.tensor_reduce(worst[:], squares[:], AX.X, ALU.max))
                v_.tensor_scalar(other16[:], worst[:], N / 4, None, ALU.is_gt).then_inc(oth_rdy, 1)
                dve.wait_ge(othP_rdy, g + 1)
                v_.tensor_copy(others[g][:], tP[0][0:1, 512:513]).then_inc(flag_rdy, 1)
                dve.wait_ge(flag_rdy, g + 1)
                flag = dve.value_load(others[g][0:1, 0:1], min_val=0, max_val=P)
                with dve.If(flag > 0):
                    after(dve, v_rdy, (q + 1) * TG)
                    after(dve, v_used, (q + 1) * TG)
                    with dve.Fori(1, 4) as r:
                        with dve.Fori(0, BG) as bb:
                            b = (r - 1) * BG + bb
                            after(dve, o_v[g], b * TB)
                            hi_k, lo_k = kT[:, ds(bb * N, N)], kT[:, ds(TG * P + bb * N, N)]
                            hi_q, lo_q = qT[:, ds(bb * N, N)], qT[:, ds(TG * P + bb * N, N)]
                            v_.tensor_tensor(zt[0], hi_k, lo_k, ALU.add).then_inc(o_half[g], 1)
                            after(dve, o_half[g], 3 * b + 1)
                            v_.tensor_scalar(zt[0], zt[0], akcol[:, ds(r, 1)], None, ALU.mult).then_inc(o_half[g], 1)
                            after(dve, o_half[g], 3 * b + 2)
                            v_.tensor_copy(hi_q, zt[0]).then_inc(o_half[g], 1)
                            after(dve, o_half[g], 3 * b + 3)
                            v_.tensor_tensor(lo_q, zt[0], hi_q, ALU.subtract).then_inc(o_q[g], 1)
                            with dve.Fori(0, TB) as k:
                                n = b * TB + k
                                after(dve, o_s[g], n + 1)
                                v_.tensor_tensor(zt[0], zt[0], pr[0], ALU.max).then_inc(o_max[g], 1)
                                after(dve, o_max[g], n + 1)
                                dve.wait_ge(o_ld[g], 16 * (n + 1))
                                v_.scalar_tensor_tensor(pr[0], adjb[0][:], codes[:, ds(r, 1)], zt[0],
                                                        ALU.is_equal, ALU.mult).then_inc(o_p[g], 1)
                                after(dve, o_t[g], n + 1)
                                after(dve, o_v[g], n)
                                v_.tensor_copy(pT[0], tP[0][:, :]).then_inc(o_c[g], 1)
                                after(dve, o_v[g], n + 1)
                                xt_ = x[:, ds((g * TG + bb * TB + k) * D, D)]
                                v_.tensor_tensor(xt_, vP[0], xt_, ALU.add).then_inc(o_x[g], 1)

            def split(w, i, kind, l, g):
                m = M0[kind, l, g] + R * w + i
                n, f = C[l] * SPAN, hf[i % 2]
                after(dve, hf_rdy, m + 1)
                after(dve, yp_rdy, m - R + 1)
                v_.tensor_copy(hs[i][:, 0:n], f[:, 0:n]).then_inc(hhi_rdy, 1)
                after(dve, hhi_rdy, m + 1)
                v_.tensor_tensor(hs[i][:, 4 * SPAN:4 * SPAN + n], f[:, 0:n], hs[i][:, 0:n],
                                 ALU.subtract).then_inc(hs_rdy, 1)

            def biased(i, bias):
                return v_.tensor_tensor(ysb[i].rearrange("p (s d) -> p s d", s=ST),
                                        yP[i % 2].rearrange("p (s d) -> p s d", s=ST),
                                        bias.rearrange("p (o d) -> p o d", o=1).to_broadcast([P, ST, D]), ALU.add)

            def dense(l, g):
                meet(dve, "dense", l, g)
                q = q_of(l, g)
                statistics(2 * q + 2, g)
                c0 = n_link[0]

                def rows(w, i):
                    u, f = R * w + i, xf[i % 2]
                    for s in range(ST):
                        t = ST * u + s
                        v_.tensor_scalar(f[:, s * D:(s + 1) * D], x[:, ds((g * TG + t) * D, D)],
                                         mv[:, ds(2 * t, 1)], rstd[:, ds(t, 1)], ALU.subtract,
                                         ALU.mult).then_inc(chain, 1)
                    dve.wait_ge(chain, c0 + 3 * u + 2)
                    after(dve, xtp_rdy, U0["dense", l, g] + u - R + 1)
                    dve.wait_ge(xb_st[i], 16 * (1 + q * US // R + w))
                    f3 = f.rearrange("p (s d) -> p s d", s=ST)
                    b3 = xb[i].rearrange("p (s c) -> p s c", s=ST)
                    v_.tensor_copy(b3[:, :, 0:D], f3).then_inc(chain, 1)
                    dve.wait_ge(chain, c0 + 3 * u + 3)
                    v_.tensor_tensor(b3[:, :, D:2 * D], f3, b3[:, :, 0:D], ALU.subtract).then_inc(xb_made, 1)

                def scores(w, i):
                    u = R * w + i
                    after(dve, lgp_rdy, q * US + u + 1)
                    v_.tensor_tensor(lg[:, ds(u * ST * E, ST * E)], lgP[i % 2],
                                     gateb[:, l].rearrange("p s e -> p (s e)"), ALU.add).then_inc(lg_rdy, 1)

                def residual(w, i):
                    u = R * w + i
                    r = g * US + u
                    after(dve, yp_rdy, M0["dense", l, g] + u + 1)
                    biased(i, b2b[0][:, SH * D:(SH + 1) * D]).then_inc(r_step, 1)
                    after(dve, r_step, r + 1)
                    xu = x[:, ds((g * TG + ST * u) * D, ST * D)]
                    v_.tensor_tensor(xu, xu, ysb[i], ALU.add).then_inc(r_used, 1)

                def step(w, i, has):
                    if has(0):
                        scores(w, i)
                    if has(3):
                        rows(*shifted(w, i, 3))
                    if l == 0 and has(0):
                        split(w, i, "dense", l, g)
                    if l == 0 and has(-2):
                        residual(*shifted(w, i, -2))
                for i in range(3):
                    rows(0, i)
                each_unit(dve, US, step, 3, 2 if l == 0 else 0)
                n_link[0] += 3 * US
                after(dve, lg_rdy, US * (q + 1))
                route(l, g)
                for i in range(R):
                    dve.wait_ge(xb_st[i], 16 * (1 + (q + 1) * US // R))

            def route(l, g):
                q = q_of(l, g)
                W = TG * E

                def te(a):
                    return a.rearrange("p (t e) -> p t e", e=E)

                def bc(a):
                    return a.rearrange("p (t o) -> p t o", o=1).to_broadcast([P, TG, E])
                rk = rank[:].rearrange("p (o e) -> p o e", o=1).to_broadcast([P, TG, E])
                src = lg
                for c in range(2):
                    link(v_.tensor_reduce(mx[c], te(src), AX.X, ALU.max))
                    link(v_.tensor_tensor(te(tm[0]), te(src), bc(mx[c]), ALU.is_equal))
                    link(v_.tensor_tensor(te(tm[0]), te(tm[0]), rk, ALU.mult))
                    link(v_.tensor_reduce(mx[3], te(tm[0]), AX.X, ALU.max))
                    link(v_.tensor_tensor(te(oh[c]), te(tm[0]), bc(mx[3]), ALU.is_equal))
                    if c == 0:
                        link(v_.scalar_tensor_tensor(tm[1], oh[0], NEG, lg, ALU.mult, ALU.add))
                        src = tm[1]
                v_.tensor_tensor(oh16, oh[0], oh[1], ALU.add).then_inc(route_rdy, 1)
                v_.tensor_tensor(mx[2], mx[1], mx[0], ALU.subtract).then_inc(w2_rdy, 1)
                dve.wait_ge(pos_rdy, q + 1)
                link(v_.tensor_copy(cum[0], tP[1][:, 0:W]))
                a, b, d = 0, 1, 1
                while d < TG:
                    link(v_.tensor_copy(cum[b][:, 0:d * E], cum[a][:, 0:d * E]))
                    link(v_.tensor_tensor(cum[b][:, d * E:W], cum[a][:, d * E:W], cum[a][:, 0:W - d * E], ALU.add))
                    a, b, d = b, a, 2 * d
                tot = cum[a][:, W - E:W]
                link(v_.tensor_scalar(nb_i[:], tot, float(SPAN - 1), None, ALU.add))
                link(v_.tensor_scalar(nb_i[:], nb_i[:], SPAN.bit_length() - 1, None, ALU.arith_shift_right))
                blk = [small[:, 0:E], small[:, E:2 * E]]
                link(v_.tensor_copy(blk[0], nb_i[:]))
                s, r, d = 0, 1, 1
                while d < E:
                    link(v_.tensor_copy(blk[r][:, 0:d], blk[s][:, 0:d]))
                    link(v_.tensor_tensor(blk[r][:, d:E], blk[s][:, d:E], blk[s][:, 0:E - d], ALU.add))
                    s, r, d = r, s, 2 * d
                first = small[:, 2 * E:3 * E]
                link(v_.memset(first, 0.0))
                link(v_.tensor_scalar(first[:, 1:E], blk[s][:, 0:E - 1], float(SPAN), None, ALU.mult))
                link(v_.tensor_tensor(te(tm[0]), te(tP[0][:, 0:W]),
                                      first.rearrange("p (o e) -> p o e", o=1).to_broadcast([P, TG, E]), ALU.add))
                link(v_.tensor_tensor(tm[0][:, E:W], tm[0][:, E:W], cum[a][:, 0:W - E], ALU.add))
                slv = slf.rearrange("p (t c) -> p t c", c=2)
                for c in range(2):
                    link(v_.tensor_tensor(tm[1], tm[0], oh[c], ALU.mult))
                    link(v_.tensor_reduce(slv[:, :, c], te(tm[1]), AX.X, ALU.add))
                if q >= 1:
                    dve.wait_ge(slot_st, 16 * q)
                v_.tensor_copy(sl[:], slf).then_inc(tbl_rdy, 1)
                nbv = blockno[:].rearrange("p (n o) -> p n o", o=1).to_broadcast([P, NB, E])
                bv = blk[s].rearrange("p (o e) -> p o e", o=1).to_broadcast([P, NB, E])
                cv = cmpb.rearrange("p (n e) -> p n e", e=E)
                link(v_.tensor_tensor(cv, nbv, bv, ALU.is_ge))
                link(v_.tensor_reduce(bef, cv, AX.X, ALU.add))
                v_.tensor_scalar(be[g][:], bef[0:1, :], float(E - 1), None, ALU.min).then_inc(tbl_rdy, 1)
                dve.wait_ge(w2e_rdy, q + 1)
                wv = wgt[:, g * TG * 2:(g + 1) * TG * 2].rearrange("p (t c) -> p t c", c=2)
                link(v_.tensor_scalar(mx[0], mx[2], 1.0, None, ALU.add))
                link(v_.reciprocal(mx[1], mx[0]))
                link(v_.tensor_copy(wv[:, :, 0], mx[1]))
                link(v_.tensor_tensor(wv[:, :, 1], mx[1], mx[2], ALU.mult))

            def blocks(l, g):
                meet(dve, "blocks", l, g)
                q = q_of(l, g)
                dve.wait_ge(tbl_rdy, 2 * q + 2)

                def result(w, i):
                    u = R * w + i
                    e = expert_of(dve, g, u)
                    after(dve, yp_rdy, M0["blocks", l, g] + u + 1)
                    dve.wait_ge(ys_st[i], 16 * (1 + NRING[i] * q + w))
                    biased(i, b2b[l][:, ds(e * D, D)]).then_inc(y_out, 1)

                def step(w, i, has):
                    if has(0):
                        split(w, i, "blocks", l, g)
                    if has(-2):
                        result(*shifted(w, i, -2))
                    if combined and (not isinstance(w, int) or 1 <= w <= TG // R):
                        add_tile(*combined, w - 1, i)
                combined = COMBINED_IN.get(("blocks", l, g))
                each_unit(dve, NB, step, 0, 2)
                if combined:
                    after(dve, comb, TG * (q_of(*combined) + 1))
                for i in range(R):
                    dve.wait_ge(ys_st[i], 16 * (1 + NRING[i] * (q + 1)))

            def combine(l, g):
                if (l, g) in COMBINED_IN.values():
                    return
                with dve.Fori(0, TG // R) as w:
                    for i in range(R):
                        add_tile(l, g, w, i)
                after(dve, comb, TG * (q_of(l, g) + 1))

            order(project, gnn, relations, dense, blocks, combine)

        @block.tensor
        def _(pe):
            t_ = nc.tensor
            pe.wait_ge(c_ld, 16 * NC)
            pe.wait_ge(consts, NCONST)
            for l in range(2):
                n = NE[l] * C[l]
                t_.transpose(ps[0][:, 512 * l:512 * l + n], b1rows[l], ident[0:n, 0:n])
            t_.transpose(ps[1][:, 0:D], gw, ident[:])
            t_.matmul(ps[2][:, 0:2], gw, gacol[:], start=True, stop=True).then_inc(prep_pe, 1)

            def project(l, g):
                meet(pe, "project", l, g)
                q = q_of(l, g)
                if q == 0:
                    pe.wait_ge(prep_act, 4)
                    pe.wait_ge(prep_dve, 2)

                def turn(i, par):
                    n = q * QG + i
                    after(pe, xn4_rdy, n + 1)
                    after(pe, xT_rdy, n - 1)
                    for s in range(4):
                        last = t_.transpose(eP[:, 512 * par + s * P:512 * par + (s + 1) * P],
                                            xn4[par][:, s * D:(s + 1) * D], ident[:])
                    last.then_inc(xTp_rdy, 1)

                def multiply(i, par):
                    n = q * QG + i
                    after(pe, xT_rdy, n + 1)
                    after(pe, eb_used, n - 1)
                    after(pe, wh_used, n - 1)
                    t_.matmul(tP[par][:, 0:512], wa2b[:], xT4[par], start=True, stop=True).then_inc(ebP_rdy, 1)
                    for s in range(4):
                        t_.matmul(ps[3][:, 512 * par + s * D:512 * par + (s + 1) * D], xT4[par][:, s * P:(s + 1) * P],
                                  wcat[:], start=True, stop=True)
                        last = t_.matmul(tP[par][:, 512 + s:513 + s], xT4[par][:, s * P:(s + 1) * P],
                                         wa[:, 0:1], start=True, stop=True)
                    last.then_inc(whP_rdy, 1)
                with pe.Fori(0, QG // 2) as i:
                    turn(2 * i, 0)
                    turn(2 * i + 1, 1)
                    if l == 0:
                        multiply(2 * i, 0)
                        multiply(2 * i + 1, 1)

            def scores_of(bb, k):
                i0 = (bb * TB + k) * P
                for c in range(N // 512):
                    j0 = bb * N + c * 512
                    o = eP[:, c * 512:(c + 1) * 512]
                    hi_q, lo_q = qT[:, ds(i0, P)], qT[:, ds(TG * P + i0, P)]
                    hi_k, lo_k = kT[:, ds(j0, 512)], kT[:, ds(TG * P + j0, 512)]
                    t_.matmul(o, hi_q, hi_k, start=True, stop=False)
                    t_.matmul(o, hi_q, lo_k, start=False, stop=False)
                    last = t_.matmul(o, lo_q, hi_k, start=False, stop=True)
                return last

            def turn_of(par):
                for j in range(TB):
                    last = t_.transpose(tP[par][:, j * P:(j + 1) * P], pr[par][:, j * P:(j + 1) * P], ident[:])
                return last

            def sum_of(par, bb, bias):
                for j in range(TB):
                    last = t_.matmul(vP[par], pT[par][:, j * P:(j + 1) * P], vals[:, ds((bb * TB + j) * D, D)],
                                     start=(j == 0), stop=(j == TB - 1 and not bias))
                if bias:
                    last = t_.matmul(vP[par], ones_row[:], gbrow[:], start=False, stop=True)
                return last

            def gnn(l, g):
                meet(pe, "gnn", l, g)
                q = q_of(l, g)

                def similar(n, k, bb):
                    after(pe, y_rdy, n)
                    scores_of(bb, k).then_inc(e_rdy, 1)

                def turn(n, k):
                    after(pe, p_rdy, n + 1)
                    after(pe, t_used, n - 1)
                    turn_of(k % 2).then_inc(t_rdy, 1)

                def sum_up(n, k, bb):
                    after(pe, t_used, n + 1)
                    after(pe, v_used, n - 1)
                    sum_of(k % 2, bb, l == 1).then_inc(v_rdy, 1)

                def step(bb, k, has):
                    n = (q * BG + bb) * TB + k
                    if l == 1 and has(1):
                        b1_, k1 = shifted(bb, k, 1, TB)
                        similar(n + 1, k1, b1_)
                    if has(-1):
                        b1_, k1 = shifted(bb, k, -1, TB)
                        sum_up(n - 1, k1, b1_)
                    if has(0):
                        turn(n, k)
                if l == 1:
                    similar(q * TG, 0, 0)
                each_unit(pe, TG, step, l, 1, TB)

            def relations(l, g):
                pe.wait_ge(oth_rdy, g + 1)
                t_.matmul(tP[0][0:1, 512:513], other16[:], ones16[:, 0:1], start=True,
                          stop=True).then_inc(othP_rdy, 1)
                pe.wait_ge(flag_rdy, g + 1)
                flag = pe.value_load(others[g][0:1, 0:1], min_val=0, max_val=P)
                with pe.If(flag > 0):
                    with pe.Fori(1, 4) as r:
                        with pe.Fori(0, BG) as bb:
                            b = (r - 1) * BG + bb
                            with pe.Fori(0, TB) as k:
                                n = b * TB + k
                                after(pe, o_q[g], b + 1)
                                after(pe, o_s[g], n)
                                scores_of(bb, k).then_inc(o_e[g], 1)
                                after(pe, o_p[g], n + 1)
                                after(pe, o_c[g], n)
                                turn_of(0).then_inc(o_t[g], 1)
                                after(pe, o_c[g], n + 1)
                                after(pe, o_x[g], n)
                                sum_of(0, bb, False).then_inc(o_v[g], 1)

            def turn_unit(w, i, kind, l, g):
                q, u = q_of(l, g), R * w + i
                after(pe, xt_rdy, U0[kind, l, g] + u - 1)
                if kind == "dense":
                    after(pe, lg_rdy, q * US + u - 1)
                    after(pe, xb_made, q * US + u + 1)
                else:
                    pe.wait_ge(xb_ld[i], 16 * (NRING[i] * q + w + 1))
                xp = xtP[i % 2].rearrange("p (h s q) -> p h s q", h=2, s=ST)
                for s in range(ST):
                    for h in range(2):
                        last = t_.transpose(xp[:, h, s, :], xb[i][:, (2 * s + h) * D:(2 * s + h + 1) * D],
                                            ident16[:])
                last.then_inc(xtp_rdy, 1)

            def route_unit(w, i, l, g):
                u = R * w + i
                after(pe, xt_rdy, U0["dense", l, g] + u + 1)
                for s in range(ST):
                    hi, lo = xt[i][:, s * P:(s + 1) * P], xt[i][:, SPAN + s * P:SPAN + (s + 1) * P]
                    o = lgP[i % 2][:, s * E:(s + 1) * E]
                    t_.matmul(o, hi, wrs[:, l, 0, :], start=True, stop=False)
                    t_.matmul(o, hi, wrs[:, l, 1, :], start=False, stop=False)
                    last = t_.matmul(o, lo, wrs[:, l, 0, :], start=False, stop=True)
                last.then_inc(lgp_rdy, 1)

            def up(w, i, kind, l, g, e):
                u = R * w + i
                after(pe, xt_rdy, U0[kind, l, g] + u + 1)
                after(pe, hf_rdy, M0[kind, l, g] + u - 1)
                f = F[l]
                for c in range(C[l]):
                    o = hP[i % 2][:, c * SPAN:(c + 1) * SPAN]
                    hi = w1sp[l][:, ds(e * 2 * f + c * P, P)]
                    lo = w1sp[l][:, ds(e * 2 * f + f + c * P, P)]
                    t_.matmul(o, hi, xt[i][:, 0:SPAN], start=True, stop=False)
                    t_.matmul(o, hi, xt[i][:, SPAN:2 * SPAN], start=False, stop=False)
                    last = t_.matmul(o, lo, xt[i][:, 0:SPAN], start=False, stop=True)
                last.then_inc(hp_rdy, 1)

            def down(w, i, kind, l, g, e):
                u = R * w + i
                after(pe, hs_rdy, M0[kind, l, g] + u + 1)
                if kind == "dense":
                    after(pe, r_used, g * US + u - 1)
                else:
                    after(pe, y_out, BL0[kind, l, g] + u - 1)
                for s in range(ST):
                    o = yP[i % 2][:, s * D:(s + 1) * D]
                    for c in range(C[l]):
                        at_ = e * C[l] * 2 * D + c * 2 * D
                        hi = hs[i][:, c * SPAN + s * P:c * SPAN + (s + 1) * P]
                        lo = hs[i][:, (4 + c) * SPAN + s * P:(4 + c) * SPAN + (s + 1) * P]
                        whi, wlo = w2sp[l][:, ds(at_, D)], w2sp[l][:, ds(at_ + D, D)]
                        t_.matmul(o, hi, whi, start=(c == 0), stop=False)
                        t_.matmul(o, lo, whi, start=False, stop=False)
                        last = t_.matmul(o, hi, wlo, start=False, stop=(c == C[l] - 1))
                last.then_inc(yp_rdy, 1)

            def through_experts(kind, l, g, n, expert):
                known = {}

                def step(w, i, has):
                    if i == 0:
                        known.clear()
                    if has(0) and (kind == "blocks" or l == 0):
                        known[i] = expert(R * w + i)
                        up(w, i, kind, l, g, known[i])
                    if kind == "dense" and has(1):
                        route_unit(*shifted(w, i, 1), l, g)
                    if has(2):
                        turn_unit(*shifted(w, i, 2), kind, l, g)
                    if (kind == "blocks" or l == 0) and has(-2):
                        down(*shifted(w, i, -2), kind, l, g, known[i - 2] if i >= 2 else expert(R * w + i - 2))
                turn_unit(0, 0, kind, l, g)
                turn_unit(0, 1, kind, l, g)
                if kind == "dense":
                    route_unit(0, 0, l, g)
                each_unit(pe, n, step, 2, 2 if kind == "blocks" or l == 0 else 0)

            def dense(l, g):
                meet(pe, "dense", l, g)
                q = q_of(l, g)
                if q == 0:
                    pe.wait_ge(w_used, NPIECES)
                through_experts("dense", l, g, US, lambda u: SH)
                pe.wait_ge(route_rdy, q + 1)
                t_.matmul(tP[0][:, 0:TG * E], before[:], oh16, start=True, stop=True)
                t_.matmul(tP[1][:, 0:TG * E], ones16[:], oh16, start=True, stop=True).then_inc(pos_rdy, 1)

            def blocks(l, g):
                meet(pe, "blocks", l, g)
                pe.wait_ge(tbl_rdy, 2 * q_of(l, g) + 2)
                through_experts("blocks", l, g, NB,
                                lambda u: expert_of(pe, g, u))

            order(project, gnn, relations, dense, blocks, lambda l, g: None)


_INS = ["x", "adj", "L0_gnn_W", "L0_gnn_a", "L0_ffn_Wr", "L0_ffn_W1s", "L0_ffn_b1s", "L0_ffn_W2s", "L0_ffn_b2s",
        "L0_ffn_W1p", "L0_ffn_b1p", "L0_ffn_W2p", "L0_ffn_b2p", "L1_gnn_a0", "L1_gnn_a1", "L1_gnn_a2", "L1_gnn_a3",
        "L1_gnn_bias", "L1_ffn_Wg", "L1_ffn_bg", "L1_ffn_bias", "L1_ffn_W1", "L1_ffn_b1", "L1_ffn_W2", "L1_ffn_b2"]


def kernel(**inputs):
    import numpy as _np
    import concourse.bacc as _bacc
    from concourse import mybir as _mybir
    from concourse.bass_utils import run_bass_kernel_spmd as _run

    nc = _bacc.Bacc("TRN2", target_bir_lowering=False, num_devices=1)
    arrays, args = {}, []
    for name in _INS:
        a = _np.ascontiguousarray(inputs[name])
        arrays[f"in_{name}_dram"] = a
        args.append(nc.dram_tensor(f"in_{name}_dram", a.shape, _mybir.dt.from_np(a.dtype), kind="ExternalInput").ap())
    args.append(nc.dram_tensor("out_0_dram", inputs["x"].shape, _mybir.dt.float32, kind="ExternalOutput").ap())
    bass_two_layers_of_gnn_and_moe(nc, *args)
    r = _run(nc, [arrays], core_ids=[0])
    return r.results[0]["out_0_dram"]
```

```python
import concourse.bass as bass
from concourse import mybir
from contextlib import ExitStack


def bass_two_layers_of_gnn_and_moe(
    nc: bass.Bass, x_in, adj_in, gnn_w, gnn_a, wr0, w1s, b1s, w2s, b2s, w1p, b1p, w2p, b2p,
    a0, a1, a2, a3, gbias, wg1, bg1, bias1, w1e, b1e, w2e, b2e, out,
):
    f32, f16, i32 = mybir.dt.float32, mybir.dt.float16, mybir.dt.int32
    ALU = mybir.AluOpType
    ACT = mybir.ActivationFunctionType
    AX = mybir.AxisListType
    ds = bass.ds

    P = 128
    B, N, D = x_in.shape
    TB = N // P
    T = B * TB
    NG = 2
    BG = B // NG
    TG = BG * TB
    E = wr0.shape[1]
    F = [w1s.shape[1], w1e.shape[2]]
    C = [f // P for f in F]
    SH = E
    NE = [E + 1, E]
    SPAN = 256
    ST = SPAN // P
    US = TG // ST
    NB = (2 * TG * P - E) // SPAN + E
    ROWS = NB * SPAN
    R = 4
    NRING = [(NB - i + R - 1) // R for i in range(R)]
    QG = TG // 4
    LEAK = 0.2
    NEG = -1e30
    FLOOR = -1e20
    EPS = 1e-5
    assert US % R == 0
    NA = 4
    NCONST = 7
    NC = 17
    NPIECES = 2 * sum(NE)
    CR = NA

    ctx = ExitStack()
    with ctx:
        def sb(name, shape, dt):
            return ctx.enter_context(nc.sbuf_tensor(name, shape, dt))

        def sem(name):
            return ctx.enter_context(nc.semaphore(name))

        xn_d = nc.dram_tensor("xn_rows", (NG * TG * P, 2 * D), f16, kind="Internal").ap()
        xs_d = [nc.dram_tensor(f"block_in{g}", (ROWS, 2 * D), f16, kind="Internal").ap() for g in range(NG)]
        ys_d = [nc.dram_tensor(f"block_out{g}", (ROWS, D), f32, kind="Internal").ap() for g in range(NG)]
        slot_d = nc.dram_tensor("slots", (NG * P, TG * 2), i32, kind="Internal").ap()

        x = sb("x", [P, T * D], f32)
        ident = sb("ident", [P, P], f32)
        ident16 = sb("ident16", [P, P], f16)
        before = sb("before", [P, P], f16)
        ones16 = sb("ones16", [P, P], f16)
        zero16 = sb("zero16", [P, 256], f16)
        rank = sb("rank", [P, E], f32)
        blockno = sb("blockno", [P, NB], f32)
        wcat = sb("wcat", [P, D], f32)
        wa = sb("wa", [P, 2], f32)
        wa2b = sb("wa2b", [P, P], f32)
        gacol = sb("gacol", [P, 2], f32)
        akcol = sb("akcol", [P, 4], f32)
        gbsplit = sb("gbsplit", [3, D], f16)
        wrf = sb("wrf", [P, 2, E], f32)
        wrs = sb("wrs", [P, 2, 2, E], f16)
        gateb = sb("gateb", [P, 2, ST, E], f32)
        gtmp = sb("gtmp", [P, 2, E], f32)
        w1sp = [sb(f"w1sp{l}", [P, NE[l] * 2 * F[l]], f16) for l in range(2)]
        w2sp = [sb(f"w2sp{l}", [P, NE[l] * C[l] * 2 * D], f16) for l in range(2)]
        b1 = [sb(f"b1_{l}", [P, NE[l] * C[l]], f32) for l in range(2)]
        b2b = [sb(f"b2b{l}", [P, NE[l] * D], f32) for l in range(2)]
        adjb = [sb(f"adjb{i}", [P, N], i32) for i in range(NA)]
        mv = {k: sb(f"mv_{k}", [P, TG * 2], f32) for k in ("project0", "project1", "dense")}
        st8 = {k: sb(f"st8_{k}", [P, TB, 6], f32) for k in mv}
        ag8 = {k: sb(f"ag8_{k}", [P, TB * 2], f32) for k in mv}
        std = sb("std", [P, TG], f32)
        rstd = sb("rstd", [P, TG], f32)
        stage = [sb(f"stage{i}", [P, TB * 2 * D], f16) for i in range(2)]
        idx = [sb(f"idx{i}", [P, TB * 2], i32) for i in range(2)]
        got = [sb(f"got{i}", [P, 2 * D], f32) for i in range(R)]
        squares = sb("squares", [P, TG], f32)
        junk = sb("junk", [P, N], f32)

        KB = 256
        arena = sb("arena", [P, 75 * KB], f32)

        def at(kb, n, dt=f32):
            a = arena[:, int(kb * KB):int(kb * KB) + (n if dt == f32 else n // 2)]
            return a if dt == f32 else a.bitcast(dt)

        vals = at(0, TG * D)
        ejb = at(16, BG * N)
        kT = at(16, 2 * TG * P, f16)
        qT = at(32, 2 * TG * P, f16)
        ejc = at(32, N)
        zt = [at(48 + 4 * i, N) for i in range(2)]
        z4 = [at(36 + 4 * i, N) for i in range(4)]
        pr = [at(56 + 4 * i, N) for i in range(2)]
        pT = [at(64 + 4 * i, N) for i in range(2)]
        xn4 = [at(48 + 2 * i, 4 * D) for i in range(2)]
        xT4 = [at(52 + 2 * i, 4 * P) for i in range(2)]
        qf = [at(56 + 2 * i, 4 * P) for i in range(2)]
        ei = at(72, TG)
        mrow = at(72.5, 2)
        t1 = at(72.75, 1)
        umax = at(73.25, 1)
        shift1 = at(74, 2)
        shift2 = at(74.25, 2)
        rsum = at(73.5, 4)
        total = at(73.75, 2)
        gw = at(64, D)
        b1rows = [at(65 + l, P)[0:NE[l] * C[l], :] for l in range(2)]
        gb3 = at(67, D)[0:3, :]
        gbleft = at(67.5, D)[0:3, :]
        gbpart = [at(68 + 0.25 * i, D, f16)[0:3, :] for i in range(3)]
        xf = [at(54 + i, ST * D) for i in range(R)]
        xb = [at(2 + i, ST * 2 * D, f16) for i in range(R)]
        xt = [at(6 + i, 2 * SPAN, f16) for i in range(R)]
        ysb = [at(10 + i, ST * D) for i in range(R)]
        hf = [at(14 + 4 * i, 4 * SPAN) for i in range(2)]
        hs = [at(22 + 4 * i, 2 * 4 * SPAN, f16) for i in range(R)]
        lg = at(38, TG * E)
        oh = [at(39 + i, TG * E) for i in range(2)]
        tm = [at(41 + i, TG * E) for i in range(3)]
        oh16 = at(44, TG * E, f16)
        PAD = TG * E // 2
        cum = [at(45 + 1.5 * i, PAD + TG * E) for i in range(2)]
        mx = [at(48 + 0.25 * i, TG) for i in range(4)]
        blk = [at(49 + 0.25 * i, 2 * E) for i in range(2)]
        first = at(49.5, E)
        slf = at(50, 2 * TG)
        cmpb = at(51, NB * E)
        bef = at(53, NB)

        worst = sb("worst", [P, 1], f32)
        other16 = sb("other16", [P, 1], f16)
        others = [sb(f"others{g}", [1, 1], i32) for g in range(NG)]
        minus_half = sb("minus_half", [P, 1], f32)
        codes = sb("codes", [P, 4], f32)
        wgt = sb("wgt", [P, NG * TG * 2], f32)
        sl = sb("sl", [P, TG * 2], i32)
        be = [sb(f"be{g}", [1, NB], i32) for g in range(NG)]
        nb_i = sb("nb_i", [P, E], i32)

        ps = [ctx.enter_context(nc.psum_tensor(f"ps{i}", [P, 1024], f32)) for i in range(4)]
        eP = ps[0]
        tP = [ps[1], ps[2]]
        vP = [ps[3][:, 0:P], ps[3][:, 512:512 + P]]
        xtP = [ps[0][:, 512 * i:512 * i + SPAN].bitcast(f16) for i in range(2)]
        lgP = [ps[0][:, 512 * i + 384:512 * i + 384 + ST * E] for i in range(2)]
        hP = [ps[1], ps[2]]
        yP = [ps[3][:, 512 * i:512 * i + ST * D] for i in range(2)]

        x_ld = [sem(f"x_ld{i}") for i in range(BG + 1)]
        c_ld = sem("c_ld")
        w_ld = [sem(f"w_ld{i}") for i in range(2)]
        adj_ld = [sem(f"adj_ld{i}") for i in range(NA)]
        xs_zero = sem("xs_zero")
        xb_ld = [sem(f"xb_ld{i}") for i in range(R)]
        xb_st = [sem(f"xb_st{i}") for i in range(R)]
        ys_st = [sem(f"ys_st{i}") for i in range(R)]
        slot_st = sem("slot_st")
        st_ld = [sem(f"st_ld{i}") for i in range(2)]
        scat = [sem(f"scat{i}") for i in range(2)]
        gi_ld = [sem(f"gi_ld{i}") for i in range(2)]
        gath = [sem(f"gath{i}") for i in range(R)]
        o_st = sem("o_st")
        w_used, consts, pchain, chain = sem("w_used"), sem("consts"), sem("pchain"), sem("chain")
        prep_pe, prep_act, prep_dve = sem("prep_pe"), sem("prep_act"), sem("prep_dve")
        over, scat_all, blocks_out = sem("over"), sem("scat_all"), sem("blocks_out")
        var_rdy, std_rdy = sem("var_rdy"), sem("std_rdy")
        route_rdy, pos_rdy, w2_rdy, w2e_rdy, tbl_rdy = (sem("route_rdy"), sem("pos_rdy"), sem("w2_rdy"),
                                                        sem("w2e_rdy"), sem("tbl_rdy"))

        counted = []

        def unit(name):
            counted.append(sem(name))
            return counted[-1]

        xn4_rdy, xTp_rdy, xT_rdy, ebP_rdy, eb_used = (unit("xn4_rdy"), unit("xTp_rdy"), unit("xT_rdy"),
                                                      unit("ebP_rdy"), unit("eb_used"))
        whP_rdy, wh_used, qf_rdy, khi_rdy, kq_rdy, h_rdy = (unit("whP_rdy"), unit("wh_used"), unit("qf_rdy"),
                                                            unit("khi_rdy"), unit("kq_rdy"), unit("h_rdy"))
        ejc_rdy, mask_rdy, z_rdy, nm_step, nmax_rdy = (unit("ejc_rdy"), unit("mask_rdy"), unit("z_rdy"),
                                                       unit("nm_step"), unit("nmax_rdy"))
        e_rdy, y_rdy, s_rdy, p_rdy, t_rdy = (unit("e_rdy"), unit("y_rdy"), unit("s_rdy"), unit("p_rdy"),
                                             unit("t_rdy"))
        t_used, v_rdy, rc_step, v_used = unit("t_used"), unit("v_rdy"), unit("rc_step"), unit("v_used")
        xb_made, xtp_rdy, xt_rdy, lgp_rdy, lg_rdy = (unit("xb_made"), unit("xtp_rdy"), unit("xt_rdy"),
                                                     unit("lgp_rdy"), unit("lg_rdy"))
        hp_rdy, hf_rdy, hhi_rdy, hs_rdy, yp_rdy = (unit("hp_rdy"), unit("hf_rdy"), unit("hhi_rdy"),
                                                   unit("hs_rdy"), unit("yp_rdy"))
        norm_rdy, xhi_rdy = unit("norm_rdy"), unit("xhi_rdy")
        r_step, y_out = unit("r_step"), unit("y_out")
        first_in, comb = unit("first_in"), unit("comb")
        st_a, st_b, st_c = ({k: unit(f"{n}_{k}") for k in mv} for n in ("st_a", "st_b", "st_c"))

        seen, oth_rdy, othP_rdy, flag_rdy = unit("seen"), sem("oth_rdy"), sem("othP_rdy"), sem("flag_rdy")
        o_ld = [sem(f"o_ld{g}") for g in range(NG)]
        o_half, o_q, o_e, o_s, o_max, o_p, o_t, o_c, o_v, o_x, o_m = (
            [unit(f"{n}{g}") for g in range(NG)]
            for n in ("o_half", "o_q", "o_e", "o_s", "o_max", "o_p", "o_t", "o_c", "o_v", "o_x", "o_m"))

        def after(eng, semaphore, count):
            eng.wait_ge(semaphore, count + CR)

        ENGINES = 3

        def order(project, gnn, relations, dense, blocks, combine):
            for l in range(2):
                for g in range(NG):
                    project(l, g)
                    gnn(l, g)
                    if l == 1:
                        relations(l, g)
                    dense(l, g)
                for g in range(NG):
                    blocks(l, g)
            for g in range(NG):
                combine(1, g)

        COMBINED_IN = {("blocks", 0, 1): (0, 0), ("gnn", 1, 0): (0, 1), ("blocks", 1, 1): (1, 0)}

        MEASURED = {("dense", l, g): (l * NG + g + 1) * (TG // TB) for l in range(2) for g in range(NG)}
        for g in range(NG):
            MEASURED["project", 0, g] = TG // TB
        MEASURED["project", 1, 0] = TG // TB + TG // R
        MEASURED["project", 1, 1] = TG // TB + TG // TB

        MEET = {}

        def note(kind):
            def f(l, g):
                MEET[kind, l, g] = len(MEET) + 1
            return f
        order(note("project"), note("gnn"), lambda l, g: None, note("dense"), note("blocks"), lambda l, g: None)

        def meet(eng, kind, l, g):
            eng.drain().then_inc(over, 1)
            eng.wait_ge(over, ENGINES * MEET[kind, l, g])

        def q_of(l, g):
            return l * NG + g

        U0, M0, BL0 = {}, {}, {}
        u = m = bl = 0
        for l in range(2):
            for g in range(NG):
                U0["dense", l, g], M0["dense", l, g], BL0["dense", l, g] = u, m, bl
                u += US
                m += US if l == 0 else 0
            for g in range(NG):
                U0["blocks", l, g], M0["blocks", l, g], BL0["blocks", l, g] = u, m, bl
                u += NB
                m += NB
                bl += NB

        def shifted(w, i, by, ring=R):
            return w + (i + by) // ring, (i + by) % ring

        def each_unit(eng, n, step, ahead, lag, ring=R):
            rounds = (n - ring - ahead) // ring
            assert lag <= ring and rounds > 0

            def peeled(u):
                step(u // ring, u % ring, lambda by: 0 <= u + by < n)
            for u in range(ring):
                peeled(u)
            with eng.Fori(1, 1 + rounds) as w:
                for i in range(ring):
                    step(w, i, lambda by: True)
            for u in range(ring * (1 + rounds), n + lag):
                peeled(u)

        def expert_of(eng, g, u):
            return nc.values_load(be[g][0:1, ds(u, 1)], engines=[eng.engine], min_val=0, max_val=E - 1,
                                  skip_runtime_bounds_check_because="route() clamps it to E - 1, and it is a count")

        block = ctx.enter_context(nc.Block())

        @block.sync
        def _(sp):
            for c in counted:
                sp.sem_inc(c, CR)
            for c in (*xb_st, *ys_st):
                sp.sem_inc(c, 16)
            xv = x_in.rearrange("b (t p) d -> p (b t) d", p=P)
            ov = out.rearrange("b (t p) d -> p (b t) d", p=P)
            for b in range(BG):
                sp.dma_start(x[:, b * TB * D:(b + 1) * TB * D].rearrange("p (t d) -> p t d", d=D),
                             xv[:, b * TB:(b + 1) * TB, :]).then_inc(x_ld[b], 16)
            small_loads = [
                (gw, gnn_w), (gacol[:], gnn_a.rearrange("(k p) -> p k", p=P)),
                (gb3, gbias.partition_broadcast(3)),
                (wrf[:, 0, :], wr0), (wrf[:, 1, :], wg1),
                (b1rows[0][0:E * C[0], :], b1p.rearrange("e (c p) -> (e c) p", p=P)),
                (b1rows[0][E * C[0]:NE[0] * C[0], :], b1s.rearrange("(c p) -> c p", p=P)),
                (b1rows[1], b1e.rearrange("e (c p) -> (e c) p", p=P)),
                (b2b[0][:, 0:E * D], b2p.rearrange("e d -> (e d)").partition_broadcast(P)),
                (b2b[0][:, E * D:NE[0] * D], b2s.partition_broadcast(P)),
                (b2b[1][:, :], b2e.rearrange("e d -> (e d)").partition_broadcast(P)),
                (gtmp[:, 0, :], bg1.partition_broadcast(P)), (gtmp[:, 1, :], bias1.partition_broadcast(P)),
            ] + [(akcol[:, k:k + 1], a) for k, a in enumerate([a0, a1, a2, a3])]
            assert len(small_loads) == NC
            with nc.allow_non_contiguous_dma(reason="a few small vectors"):
                for dst, src in small_loads:
                    sp.dma_start(dst, src).then_inc(c_ld, 16)
            sp.dma_start(x[:, TG * D:T * D].rearrange("p (t d) -> p t d", d=D), xv[:, TG:T, :]).then_inc(x_ld[BG], 16)

            def project(l, g):
                pass

            def gnn(l, g):
                with sp.Fori(0, BG) as bb:
                    for k in range(TB):
                        n = (q_of(l, g) * BG + bb) * TB + k
                        if l == 0:
                            after(sp, mask_rdy, n - NA + 1)
                        else:
                            after(sp, p_rdy, n - NA + 1)
                            sp.nop(nofuse=True)
                            after(sp, seen, n - NG * TG - NA + 1)
                        sp.nop(nofuse=True)
                        sp.dma_start(adjb[k % NA][:], adj_in[ds(g * BG + bb, 1), k * P:(k + 1) * P, :]
                                     .rearrange("o p n -> (o p) n")).then_inc(adj_ld[k % NA], 16)
                if l == 0 and g == 0:
                    sp.wait_ge(consts, NCONST)
                    for gg in range(NG):
                        sp.dma_start(xs_d[gg].rearrange("(p r) c -> p (r c)", p=P)
                                     .rearrange("p (r c) -> p r c", c=256),
                                     zero16[:].rearrange("p (o c) -> p o c", o=1)
                                     .to_broadcast([P, ROWS * 2 * D // (P * 256), 256])).then_inc(xs_zero, 16)

            def relations(l, g):
                sp.wait_ge(flag_rdy, g + 1)
                flag = sp.value_load(others[g][0:1, 0:1], min_val=0, max_val=P)
                with sp.If(flag > 0):
                    after(sp, p_rdy, (q_of(l, g) + 1) * TG)
                    with sp.Fori(1, 4) as r:
                        with sp.Fori(0, BG) as bb:
                            with sp.Fori(0, TB) as k:
                                after(sp, o_p[g], ((r - 1) * BG + bb) * TB + k)
                                sp.dma_start(adjb[0][:], adj_in[ds(g * BG + bb, 1), ds(k * P, P), :]
                                             .rearrange("o p n -> (o p) n")).then_inc(o_ld[g], 16)

            def dense(l, g):
                q = q_of(l, g)
                if l == 1:
                    sp.wait_ge(scat_all, g + 1)

                with sp.Fori(0, US // R) as w:
                    for i in range(R):
                        u = R * w + i
                        after(sp, xb_made, q * US + u + 1)
                        sp.dma_start(xn_d[ds(g * TG * P + u * SPAN, SPAN), :].rearrange("(s p) c -> p s c", p=P),
                                     xb[i].rearrange("p (s c) -> p s c", s=ST)).then_inc(xb_st[i], 16)
                sp.wait_ge(tbl_rdy, 2 * q + 1)
                if l == 1:
                    after(sp, comb, TG * (g + 1))
                sp.dma_start(slot_d[g * P:(g + 1) * P, :], sl[:]).then_inc(slot_st, 16)

            def blocks(l, g):
                q = q_of(l, g)
                sp.wait_ge(over, ENGINES * MEET["blocks", l, g])
                sp.wait_ge(scat_all, q + 1)
                if l == 1:
                    after(sp, comb, TG * (g + 1))

                def load(w, i):
                    u = R * w + i
                    after(sp, xtp_rdy, U0["blocks", l, g] + u - R + 1)
                    sp.dma_start(xb[i].rearrange("p (s c) -> p s c", s=ST),
                                 xs_d[g][ds(u * SPAN, SPAN), :].rearrange("(s p) c -> p s c", p=P)
                                 ).then_inc(xb_ld[i], 16)

                def store(w, i):
                    u = R * w + i
                    after(sp, y_out, BL0["blocks", l, g] + u + 1)
                    sp.dma_start(ys_d[g][ds(u * SPAN, SPAN), :].rearrange("(s p) d -> p s d", p=P),
                                 ysb[i].rearrange("p (s d) -> p s d", s=ST)).then_inc(ys_st[i], 16)

                def step(w, i, has):
                    if has(R):
                        load(w + 1, i)
                    if has(-R):
                        store(w - 1, i)
                for i in range(R):
                    load(0, i)
                each_unit(sp, NB, step, R, R)
                for i in range(R):
                    sp.wait_ge(ys_st[i], 16 * (1 + NRING[i] * (q + 1)))
                sp.sem_inc(blocks_out, 1)

            def combine(l, g):
                if l == 1:
                    for bb in range(BG):
                        t = (g * BG + bb) * TB
                        after(sp, comb, (q_of(l, g) * BG + bb + 1) * TB)
                        sp.dma_start(ov[:, t:t + TB, :],
                                     x[:, t * D:(t + TB) * D].rearrange("p (t d) -> p t d", d=D)).then_inc(o_st, 16)
            order(project, gnn, relations, dense, blocks, combine)
            sp.wait_ge(o_st, 16 * B)

        @block.gpsimd
        def _(pool):
            n_link = [0]

            def link(ins):
                n_link[0] += 1
                ins.then_inc(pchain, 1)
                pool.wait_ge(pchain, n_link[0])

            g_ = nc.gpsimd
            link(g_.memset(ident[:], 0.0))
            link(g_.affine_select(out=ident[:], in_=ident[:], compare_op=ALU.not_equal, fill=1.0, base=0,
                                  pattern=[[-1, P]], channel_multiplier=1))
            g_.memset(zero16[:], 0.0).then_inc(consts, 1)
            g_.memset(ones16[:], 1.0).then_inc(consts, 1)
            link(g_.memset(before[:], 1.0))
            g_.affine_select(out=before[:], in_=before[:], compare_op=ALU.is_gt, fill=0.0, base=0,
                             pattern=[[1, P]], channel_multiplier=-1).then_inc(consts, 1)
            g_.iota(rank[:], pattern=[[-1, E]], base=E, channel_multiplier=0,
                    allow_small_or_imprecise_dtypes=True).then_inc(consts, 1)
            g_.iota(blockno[:], pattern=[[1, NB]], base=0, channel_multiplier=0,
                    allow_small_or_imprecise_dtypes=True).then_inc(consts, 1)
            g_.iota(codes[:], pattern=[[1, 4]], base=1, channel_multiplier=0,
                    allow_small_or_imprecise_dtypes=True).then_inc(consts, 1)
            g_.tensor_copy(ident16[:], ident[:]).then_inc(consts, 1)

            pieces = []
            for l in range(2):
                f, c = F[l], C[l]
                for e in range(NE[l]):
                    w1 = (w1s if e == SH else w1p[e]) if l == 0 else w1e[e]
                    w2 = (w2s if e == SH else w2p[e]) if l == 0 else w2e[e]
                    to1 = w1sp[l][:, e * 2 * f:(e + 1) * 2 * f].rearrange("p (h f) -> p h f", h=2)
                    to2 = (w2sp[l][:, e * c * 2 * D:(e + 1) * c * 2 * D]
                           .rearrange("p (c h d) -> p h c d", c=c, h=2))
                    pieces.append((w1, 0, to1[:, 0, :], to1[:, 1, :], f))
                    pieces.append((w2.rearrange("(c p) d -> p c d", p=P), c, to2[:, 0], to2[:, 1], f))
            assert len(pieces) == NPIECES

            def staged(i):
                c, f = pieces[i][1], pieces[i][4]
                w = stage[i % 2].bitcast(f32)[:, 0:f]
                return w.rearrange("p (c d) -> p c d", c=c) if c else w

            def fetch(i):
                if i >= 2:
                    pool.wait_ge(w_used, i - 1)
                pool.dma_start(staged(i), pieces[i][0]).then_inc(w_ld[i % 2], 16)

            def split_piece(i):
                _, _, hi, lo, _ = pieces[i]
                if i + 1 < len(pieces):
                    fetch(i + 1)
                pool.wait_ge(w_ld[i % 2], 16 * (i // 2 + 1))
                link(g_.tensor_copy(hi, staged(i)))
                g_.tensor_tensor(lo, staged(i), hi, ALU.subtract).then_inc(w_used, 1)

            fetch(0)
            for i in range(NPIECES):
                split_piece(i)

            h = BG // 2

            def slots_of(g, bb):
                return slot_d[g * P:(g + 1) * P, ds(bb * 2 * TB, 2 * TB)]

            def scatter(l, g):
                q = q_of(l, g)
                pool.wait_ge(slot_st, 16 * (q + 1))
                if q == 0:
                    pool.wait_ge(xs_zero, 16 * NG)
                if l == 1:
                    pool.wait_ge(blocks_out, g + 1)
                for i in range(R):
                    pool.wait_ge(xb_st[i], 16 * (1 + (q + 1) * US // R))

                def load(j, par):
                    pool.dma_start(idx[par][:], slots_of(g, 2 * j + par)).then_inc(st_ld[par], 16)
                    pool.dma_start(stage[par][:].rearrange("p (t c) -> p t c", t=TB),
                                   xn_d[ds((g * TG + (2 * j + par) * TB) * P, TB * P), :]
                                   .rearrange("(t p) c -> p t c", p=P)).then_inc(st_ld[par], 16)

                def rows_out(j, par):
                    pool.wait_ge(st_ld[par], 32 * (h * q + j + 1))
                    pool.nop(nofuse=True)
                    for k in range(TB):
                        for c in range(2):
                            pool.indirect_dma_start(
                                out=xs_d[g][:, :],
                                out_offset=bass.IndirectOffsetOnAxis(ap=idx[par][:, 2 * k + c:2 * k + c + 1], axis=0),
                                in_=stage[par][:, k * 2 * D:(k + 1) * 2 * D], in_offset=None).then_inc(scat[par], 16)

                def all_out(j, par):
                    pool.wait_ge(scat[par], 16 * 2 * TB * (h * q + j + 1))
                load(0, 0)
                load(0, 1)
                with pool.Fori(0, h - 1) as j:
                    rows_out(j, 0)
                    rows_out(j, 1)
                    for par in range(2):
                        all_out(j, par)
                        load(j + 1, par)
                rows_out(h - 1, 0)
                rows_out(h - 1, 1)
                all_out(h - 1, 0)
                all_out(h - 1, 1)
                pool.sem_inc(scat_all, 1)

            def gather(l, g):
                q = q_of(l, g)

                def load(j, par):
                    pool.dma_start(idx[par][:], slots_of(g, 2 * j + par)).then_inc(gi_ld[par], 16)

                def rows_in(j, par):
                    pool.wait_ge(gi_ld[par], 16 * (h * q + j + 1))
                    for k in range(TB):
                        after(pool, comb, (BG * q + 2 * j + par) * TB + k - R + 1)
                        pool.nop(nofuse=True)
                        for c in range(2):
                            pool.indirect_dma_start(
                                out=got[k % R][:, c * D:(c + 1) * D], out_offset=None, in_=ys_d[g][:, :],
                                in_offset=bass.IndirectOffsetOnAxis(ap=idx[par][:, 2 * k + c:2 * k + c + 1], axis=0),
                            ).then_inc(gath[k % R], 16)

                def all_in(j, par):
                    for i in range(R):
                        pool.wait_ge(gath[i], 32 * (BG * q + 2 * j + par + 1) * (TB // R))
                load(0, 0)
                load(0, 1)
                pool.wait_ge(blocks_out, q + 1)
                with pool.Fori(0, h - 1) as j:
                    rows_in(j, 0)
                    rows_in(j, 1)
                    for par in range(2):
                        all_in(j, par)
                        load(j + 1, par)
                rows_in(h - 1, 0)
                rows_in(h - 1, 1)
                all_in(h - 1, 0)
                all_in(h - 1, 1)

            for l in range(2):
                for g in range(NG):
                    scatter(l, g)
                for g in range(NG):
                    gather(l, g)

        @block.scalar
        def _(act):
            s_ = nc.scalar
            act.wait_ge(prep_pe, 1)
            act.wait_ge(prep_dve, 1)
            for l in range(2):
                s_.copy(b1[l][:], ps[0][:, 512 * l:512 * l + NE[l] * C[l]]).then_inc(prep_act, 1)
            s_.copy(wcat[:], ps[1][:, 0:D]).then_inc(prep_act, 1)
            s_.copy(wa[:], ps[2][:, 0:2]).then_inc(prep_act, 1)

            def deviation(n):
                act.wait_ge(var_rdy, n)
                s_.activation(std[:], std[:], ACT.Sqrt).then_inc(std_rdy, 1)

            def project(l, g):
                meet(act, "project", l, g)
                q = q_of(l, g)
                deviation(2 * q + 1)

                def turned(i, par):
                    n = q * QG + i
                    after(act, xTp_rdy, n + 1)
                    if l == 0:
                        after(act, whP_rdy, n - 1)
                    else:
                        after(act, kq_rdy, n - NG * QG - 1)
                    s_.copy(xT4[par], eP[:, 512 * par:512 * par + 512]).then_inc(xT_rdy, 1)

                def rest(i, par):
                    n = q * QG + i
                    if l == 0:
                        after(act, ebP_rdy, n + 1)
                        s_.copy(ejb[:, ds(i * 512, 512)], tP[par][:, 0:512]).then_inc(eb_used, 1)
                    else:
                        after(act, xT_rdy, n + 1)
                        after(act, kq_rdy, n - NG * QG - 1)
                        s_.activation(qf[par], xT4[par], ACT.Copy, scale=akcol[:, 0:1]).then_inc(qf_rdy, 1)
                        after(act, xn4_rdy, n + 1)
                        s_.copy(vals[:, ds(i * 4 * D, 4 * D)], xn4[par]).then_inc(h_rdy, 1)

                def step(w, par, has):
                    if has(1):
                        turned(2 * w + par + 1, 1 - par)
                    if l == 0 and has(0):
                        rest(2 * w + par, par)
                    if l == 1 and has(1):
                        rest(2 * w + par + 1, 1 - par)
                turned(0, 0)
                if l == 1:
                    rest(0, 0)
                each_unit(act, QG, step, 1, 0, 2)

            def gnn(l, g):
                meet(act, "gnn", l, g)
                q = q_of(l, g)

                def weights(n, k):
                    par = k % 2
                    after(act, t_rdy, n - 1)
                    if l == 0:
                        after(act, nmax_rdy, n + 1)
                        z = z4[k % 4]
                        s_.activation(pr[par], z, ACT.Exp, scale=LEAK, bias=shift2[:, par:par + 1])
                        s_.activation(z, z, ACT.Exp, bias=shift1[:, par:par + 1]).then_inc(y_rdy, 1)
                    else:
                        after(act, e_rdy, n - NG * TG + 1)
                        after(act, p_rdy, n - 1)
                        s_.activation(pr[par], eP[:, :], ACT.Sigmoid, scale=LEAK)
                        s_.activation(zt[par], eP[:, :], ACT.Sigmoid).then_inc(y_rdy, 1)

                def evacuate(n, k):
                    par = k % 2
                    after(act, t_rdy, n + 1)
                    after(act, v_rdy, n - 1)
                    s_.copy(pT[par], tP[par][:, :]).then_inc(t_used, 1)

                def look(n, bb, k):
                    act.wait_ge(adj_ld[k % NA], 16 * ((q * BG + bb) * (TB // NA) + k // NA + 1))
                    after(act, seen, n - NG * TG)
                    s_.activation(junk[:], adjb[k % NA][:], ACT.Square, bias=minus_half[:, 0:1],
                                  accum_out=squares[:, ds(bb * TB + k, 1)]).then_inc(seen, 1)

                def step(bb, k, has):
                    n = (q * BG + bb) * TB + k
                    if l == 0:
                        if has(0):
                            weights(n, k)
                        if has(-1):
                            evacuate(n - 1, (k - 1) % TB)
                    else:
                        if has(-1):
                            evacuate(n - 1, (k - 1) % TB)
                        if has(0):
                            look(n, bb, k)
                        if has(1):
                            weights(n + 1, (k + 1) % TB)
                if l == 1:
                    weights(q * TG, 0)
                each_unit(act, TG, step, l, 1, TB)

            def relations(l, g):
                act.wait_ge(flag_rdy, g + 1)
                flag = act.value_load(others[g][0:1, 0:1], min_val=0, max_val=P)
                with act.If(flag > 0):
                    with act.Fori(1, 4) as r:
                        with act.Fori(0, BG) as bb:
                            with act.Fori(0, TB) as k:
                                n = ((r - 1) * BG + bb) * TB + k
                                after(act, o_e[g], n + 1)
                                after(act, o_p[g], n)
                                after(act, o_t[g], n)
                                s_.activation(pr[0], eP[:, :], ACT.Sigmoid, scale=LEAK)
                                s_.activation(zt[0], eP[:, :], ACT.Sigmoid).then_inc(o_s[g], 1)

            def to_sbuf(w, i, kind, l, g):
                u = R * w + i
                after(act, xtp_rdy, U0[kind, l, g] + u + 1)
                if kind == "dense" and l == 1:
                    after(act, lgp_rdy, q_of(l, g) * US + u - R + 1)
                else:
                    after(act, hp_rdy, M0[kind, l, g] + u - R + 1)
                s_.copy(xt[i], xtP[i % 2]).then_inc(xt_rdy, 1)

            def hidden(w, i, kind, l, g, e):
                m = M0[kind, l, g] + R * w + i
                par = i % 2
                after(act, hp_rdy, m + 1)
                after(act, hs_rdy, m - 1)
                for c in range(C[l]):
                    last = s_.activation(hf[par][:, c * SPAN:(c + 1) * SPAN], hP[par][:, c * SPAN:(c + 1) * SPAN],
                                         ACT.Gelu if l == 0 else ACT.Relu, bias=b1[l][:, ds(e * C[l] + c, 1)])
                last.then_inc(hf_rdy, 1)

            def high(w, i, kind, l, g):
                m = M0[kind, l, g] + R * w + i
                n = C[l] * SPAN
                after(act, hf_rdy, m + 1)
                after(act, yp_rdy, m - R + 1)
                s_.copy(hs[i][:, 0:n], hf[i % 2][:, 0:n]).then_inc(hhi_rdy, 1)

            def rows_high(w, i, l, g):
                q, u = q_of(l, g), R * w + i
                after(act, norm_rdy, q * US + u + 1)
                after(act, xtp_rdy, U0["dense", l, g] + u - R + 1)
                act.wait_ge(xb_st[i], 16 * (1 + q * US // R + w))
                s_.copy(xb[i].rearrange("p (s c) -> p s c", s=ST)[:, :, 0:D],
                        xf[i].rearrange("p (s d) -> p s d", s=ST)).then_inc(xhi_rdy, 1)

            def through_experts(kind, l, g, n, expert):
                hid = kind == "blocks" or l == 0

                def step(w, i, has):
                    if hid and has(0):
                        hidden(w, i, kind, l, g, expert(R * w + i))
                    if has(2):
                        to_sbuf(*shifted(w, i, 2), kind, l, g)
                    if hid and has(0):
                        high(w, i, kind, l, g)
                    if kind == "dense" and has(4):
                        rows_high(*shifted(w, i, 4), l, g)
                if kind == "dense":
                    for i in range(4):
                        rows_high(0, i, l, g)
                to_sbuf(0, 0, kind, l, g)
                to_sbuf(0, 1, kind, l, g)
                each_unit(act, n, step, 4 if kind == "dense" else 2, 0)

            def dense(l, g):
                meet(act, "dense", l, g)
                deviation(2 * q_of(l, g) + 2)
                through_experts("dense", l, g, US, lambda u: SH)
                act.wait_ge(w2_rdy, q_of(l, g) + 1)
                s_.activation(mx[2], mx[2], ACT.Exp).then_inc(w2e_rdy, 1)

            def blocks(l, g):
                meet(act, "blocks", l, g)
                act.wait_ge(tbl_rdy, 2 * q_of(l, g) + 2)
                through_experts("blocks", l, g, NB,
                                lambda u: expert_of(act, g, u))

            order(project, gnn, relations, dense, blocks, lambda l, g: None)

        @block.vector
        def _(dve):
            v_ = nc.vector
            n_link = [0]

            def link(ins):
                n_link[0] += 1
                ins.then_inc(chain, 1)
                dve.wait_ge(chain, n_link[0])

            def add_choice(l, g, w, i, c):
                t = g * TG + R * w + i
                xt_ = x[:, ds(t * D, D)]
                return v_.scalar_tensor_tensor(xt_, got[i][:, c * D:(c + 1) * D], wgt[:, ds(t * 2 + c, 1)], xt_,
                                               ALU.mult, ALU.add)

            def add_first(l, g, w, i):
                dve.wait_ge(gath[i], 32 * (q_of(l, g) * (TG // R) + w + 1))
                add_choice(l, g, w, i, 0).then_inc(first_in, 1)

            def add_second(l, g, w, i):
                after(dve, first_in, q_of(l, g) * TG + R * w + i + 1)
                add_choice(l, g, w, i, 1).then_inc(comb, 1)

            def place(kind, g):
                return f"project{g}" if kind == "project" else kind

            def measure_a(kind, l, g, w, i, ring):
                t, at_ = ring * w + i, place(kind, g)
                if kind == "dense":
                    after(dve, v_used, q_of(l, g) * TG + t + 1)
                elif l == 1:
                    after(dve, comb, g * TG + t + 1)
                dve.nop(nofuse=True)
                v_.bn_stats(st8[at_][:, i, :], x[:, ds((g * TG + t) * D, D)]).then_inc(st_a[at_], 1)

            def measure_b(kind, l, g, w, i, ring):
                at_ = place(kind, g)
                n = (q_of(l, g) if kind == "dense" else l) * TG + ring * w + i
                after(dve, st_a[at_], n + 1)
                after(dve, st_c[at_], MEASURED[kind, l, g] - TG // ring + w)
                dve.nop(nofuse=True)
                v_.bn_aggr(ag8[at_][:, 2 * i:2 * i + 2], st8[at_][:, i, :]).then_inc(st_b[at_], 1)
                if i == ring - 1:
                    after(dve, st_b[at_], n + 1)
                    v_.tensor_copy(mv[at_][:, ds(2 * ring * w, 2 * ring)],
                                   ag8[at_][:, 0:2 * ring]).then_inc(st_c[at_], 1)

            for w in range(BG):
                dve.wait_ge(x_ld[w], 16)
                for i in range(TB + 1):
                    if i < TB:
                        measure_a("project", 0, 0, w, i, TB)
                    if i >= 1:
                        measure_b("project", 0, 0, w, i - 1, TB)

            dve.wait_ge(c_ld, 16 * NC)
            dve.wait_ge(consts, NCONST)
            link(v_.tensor_copy(wrs[:, :, 0, :], wrf[:]))
            v_.memset(gateb[:, 0], 0.0)
            v_.memset(minus_half[:], -0.5)
            for s in range(ST):
                v_.tensor_tensor(gateb[:, 1, s], gtmp[:, 0, :], gtmp[:, 1, :], ALU.add)
            v_.tensor_tensor(wrs[:, :, 1, :], wrf[:], wrs[:, :, 0, :], ALU.subtract).then_inc(prep_dve, 1)
            left = gb3
            for i in range(3):
                link(v_.tensor_copy(gbpart[i], left))
                if i < 2:
                    link(v_.tensor_tensor(gbleft, left, gbpart[i], ALU.subtract))
                    left = gbleft
            link(v_.tensor_scalar(gbsplit[:], gbpart[0], ident[0:3, 0:1], None, ALU.mult))
            for i in range(1, 3):
                link(v_.scalar_tensor_tensor(gbsplit[:], gbpart[i], ident[0:3, i:i + 1], gbsplit[:], ALU.mult,
                                             ALU.add))
            dve.wait_ge(prep_act, 4)
            v_.tensor_copy(wa2b[:], wa[:, 1:2].to_broadcast([P, P])).then_inc(prep_dve, 1)

            def scales(n, at_):
                v_.tensor_scalar(std[:], mv[at_][:].rearrange("p (t k) -> p t k", k=2)[:, :, 1], EPS, None,
                                 ALU.add).then_inc(var_rdy, 1)
                dve.wait_ge(std_rdy, n)
                link(v_.reciprocal(rstd[:], std[:]))

            def project(l, g):
                meet(dve, "project", l, g)
                q = q_of(l, g)
                after(dve, st_c[place("project", g)], MEASURED["project", l, g])
                scales(2 * q + 1, place("project", g))

                def normal(i, par):
                    n = q * QG + i
                    after(dve, xTp_rdy, n - 1)
                    if l == 1:
                        after(dve, h_rdy, n - NG * QG - 1)
                    for s in range(4):
                        t = 4 * i + s
                        last = v_.tensor_scalar(xn4[par][:, s * D:(s + 1) * D], x[:, ds((g * TG + t) * D, D)],
                                                mv[place("project", g)][:, ds(2 * t, 1)], rstd[:, ds(t, 1)],
                                                ALU.subtract, ALU.mult)
                    last.then_inc(xn4_rdy, 1)

                def collect(i, par):
                    n = q * QG + i
                    if l == 0:
                        after(dve, whP_rdy, n + 1)
                        v_.tensor_copy(vals[:, ds(i * 4 * D, 4 * D)], ps[3][:, 512 * par:512 * par + 512])
                        v_.tensor_copy(ei[:, ds(i * 4, 4)], tP[par][:, 512:516]).then_inc(wh_used, 1)
                    else:
                        m = n - NG * QG
                        after(dve, xT_rdy, n + 1)
                        v_.tensor_copy(kT[:, ds(i * 512, 512)], xT4[par]).then_inc(khi_rdy, 1)
                        after(dve, qf_rdy, m + 1)
                        v_.tensor_copy(qT[:, ds(i * 512, 512)], qf[par]).then_inc(khi_rdy, 1)
                        after(dve, khi_rdy, 2 * m + 1)
                        v_.tensor_tensor(kT[:, ds(TG * P + i * 512, 512)], xT4[par], kT[:, ds(i * 512, 512)],
                                         ALU.subtract)
                        after(dve, khi_rdy, 2 * m + 2)
                        v_.tensor_tensor(qT[:, ds(TG * P + i * 512, 512)], qf[par], qT[:, ds(i * 512, 512)],
                                         ALU.subtract).then_inc(kq_rdy, 1)

                def step(w, par, has):
                    if has(2):
                        normal(2 * w + par + 2, par)
                    if l == 0 and g == 0 and has(0):
                        half = range(par * TB // 2, (par + 1) * TB // 2)
                        for i in half:
                            measure_a("project", 0, 1, w, i, TB)
                        for i in half:
                            measure_b("project", 0, 1, w, i, TB)
                    if has(0):
                        collect(2 * w + par, par)
                normal(0, 0)
                normal(1, 1)
                if l == 0 and g == 0:
                    dve.wait_ge(x_ld[BG], 16)
                each_unit(dve, QG, step, 2, 0, 2)

            def gnn(l, g):
                meet(dve, "gnn", l, g)
                q = q_of(l, g)

                def adj_in_sbuf(bb, k):
                    dve.wait_ge(adj_ld[k % NA], 16 * ((q * BG + bb) * (TB // NA) + k // NA + 1))

                def own_batch(n, bb):
                    after(dve, z_rdy, n)
                    v_.tensor_copy(ejc, ejb[:, ds(bb * N, N)]).then_inc(ejc_rdy, 1)

                def masks(n, bb, k):
                    adj_in_sbuf(bb, k)
                    after(dve, p_rdy, n - 3)
                    v_.tensor_scalar(z4[k % 4], adjb[k % NA][:], 0.0, NEG, ALU.is_equal,
                                     ALU.mult).then_inc(mask_rdy, 1)

                def maximum(n, k, bb):
                    z = z4[k % 4]
                    after(dve, mask_rdy, n + 1)
                    after(dve, ejc_rdy, q * BG + bb + 1)
                    dve.nop(nofuse=True)
                    v_.tensor_tensor_reduce(out=z, in0=z, in1=ejc, scale=1.0, scalar=2 * NEG,
                                            op0=ALU.add, op1=ALU.max,
                                            accum_out=mrow[:, k % 2:k % 2 + 1]).then_inc(z_rdy, 1)

                def shift_a(n, k, bb):
                    after(dve, z_rdy, n + 1)
                    v_.tensor_scalar(t1, mrow[:, k % 2:k % 2 + 1], ei[:, ds(bb * TB + k, 1)], FLOOR,
                                     ALU.add, ALU.max).then_inc(nm_step, 1)

                def shift_b(n):
                    after(dve, nm_step, 2 * n + 1)
                    v_.scalar_tensor_tensor(umax, t1, LEAK, t1, ALU.mult, ALU.max).then_inc(nm_step, 1)

                def shift_c(n, k, bb):
                    par = k % 2
                    eik = ei[:, ds(bb * TB + k, 1)]
                    after(dve, nm_step, 2 * n + 2)
                    v_.tensor_tensor(shift1[:, par:par + 1], eik, umax, ALU.subtract)
                    v_.scalar_tensor_tensor(shift2[:, par:par + 1], eik, LEAK, umax, ALU.mult,
                                            ALU.subtract).then_inc(nmax_rdy, 1)

                def larger(n, k):
                    par = k % 2
                    after(dve, y_rdy, n + 1)
                    v_.scalar_tensor_tensor(pr[par], z4[k % 4], 1.0, pr[par], ALU.mult, ALU.max,
                                            accum_out=rsum[:, k % 4:k % 4 + 1]).then_inc(p_rdy, 1)

                def larger_a(n, k):
                    par = k % 2
                    after(dve, y_rdy, n + 1)
                    v_.tensor_tensor(zt[par], zt[par], pr[par], ALU.max).then_inc(s_rdy, 1)

                def larger_b(n, k, bb):
                    par = k % 2
                    after(dve, s_rdy, n - NG * TG + 1)
                    adj_in_sbuf(bb, k)
                    v_.scalar_tensor_tensor(pr[par], adjb[k % NA][:], 1.0, zt[par], ALU.is_equal,
                                            ALU.mult).then_inc(p_rdy, 1)

                def guard(n, k):
                    after(dve, p_rdy, n + 1)
                    v_.tensor_scalar(total[:, k % 2:k % 2 + 1], rsum[:, k % 4:k % 4 + 1], 1e-30, None,
                                     ALU.max).then_inc(rc_step, 1)

                def invert(n, k):
                    after(dve, rc_step, 2 * n + 1)
                    v_.reciprocal(total[:, k % 2:k % 2 + 1], total[:, k % 2:k % 2 + 1]).then_inc(rc_step, 1)

                def finish(n, bb, k):
                    xt_ = x[:, ds((g * TG + bb * TB + k) * D, D)]
                    after(dve, v_rdy, n + 1)
                    if l == 0:
                        after(dve, rc_step, 2 * n + 2)
                        last = v_.scalar_tensor_tensor(xt_, vP[k % 2], total[:, k % 2:k % 2 + 1], xt_, ALU.mult,
                                                       ALU.add)
                    else:
                        last = v_.tensor_tensor(xt_, vP[k % 2], xt_, ALU.add)
                    last.then_inc(v_used, 1)

                def step(bb, k, has):
                    n = (q * BG + bb) * TB + k
                    ahead1 = shifted(bb, k, 1, TB)
                    back2, back3, back4 = (shifted(bb, k, -by, TB) for by in (2, 3, 4))
                    if l == 0:
                        if has(0):
                            if k == 0:
                                own_batch(n, bb)
                            maximum(n, k, bb)
                        if has(1):
                            masks(n + 1, *ahead1)
                        if has(0):
                            shift_a(n, k, bb)
                        if has(-3):
                            guard(n - 3, back3[1])
                        if has(-4):
                            measure_a("dense", l, g, *back4, TB)
                        if has(0):
                            shift_b(n)
                        if has(-3):
                            invert(n - 3, back3[1])
                        if has(0):
                            shift_c(n, k, bb)
                        if has(-1):
                            larger(n - 1, (k - 1) % TB)
                        if has(-3):
                            finish(n - 3, *back3)
                        if has(-4):
                            measure_b("dense", l, g, *back4, TB)
                    else:
                        if has(0) and combined:
                            add_first(*combined, bb * (TB // R) + k // R, k % R)
                        if has(0):
                            larger_a(n, k)
                        if has(0) and combined:
                            add_second(*combined, bb * (TB // R) + k // R, k % R)
                        if has(-3):
                            measure_a("dense", l, g, *back3, TB)
                        if has(0):
                            larger_b(n, k, bb)
                        if has(0) and combined:
                            measure_a("project", 1, combined[1], bb, k, TB)
                        if has(-2):
                            finish(n - 2, *back2)
                        if has(-3):
                            measure_b("dense", l, g, *back3, TB)
                        if has(0) and combined:
                            measure_b("project", 1, combined[1], bb, k, TB)
                if l == 0:
                    masks(q * TG, 0, 0)
                combined = COMBINED_IN.get(("gnn", l, g))
                each_unit(dve, TG, step, 1 - l, 4 - l, TB)
                if combined:
                    after(dve, comb, TG * (q_of(*combined) + 1))

            def relations(l, g):
                q = q_of(l, g)
                after(dve, seen, (g + 1) * TG)
                link(v_.tensor_reduce(worst[:], squares[:], AX.X, ALU.max))
                v_.tensor_scalar(other16[:], worst[:], N / 4, None, ALU.is_gt).then_inc(oth_rdy, 1)
                dve.wait_ge(othP_rdy, g + 1)
                v_.tensor_copy(others[g][:], tP[0][0:1, 512:513]).then_inc(flag_rdy, 1)
                dve.wait_ge(flag_rdy, g + 1)
                flag = dve.value_load(others[g][0:1, 0:1], min_val=0, max_val=P)
                with dve.If(flag > 0):
                    after(dve, v_rdy, (q + 1) * TG)
                    after(dve, v_used, (q + 1) * TG)
                    after(dve, st_c["dense"], MEASURED["dense", l, g])
                    with dve.Fori(1, 4) as r:
                        with dve.Fori(0, BG) as bb:
                            b = (r - 1) * BG + bb
                            after(dve, o_v[g], b * TB)
                            hi_k, lo_k = kT[:, ds(bb * N, N)], kT[:, ds(TG * P + bb * N, N)]
                            hi_q, lo_q = qT[:, ds(bb * N, N)], qT[:, ds(TG * P + bb * N, N)]
                            v_.tensor_tensor(zt[0], hi_k, lo_k, ALU.add).then_inc(o_half[g], 1)
                            after(dve, o_half[g], 3 * b + 1)
                            v_.tensor_scalar(zt[0], zt[0], akcol[:, ds(r, 1)], None, ALU.mult).then_inc(o_half[g], 1)
                            after(dve, o_half[g], 3 * b + 2)
                            v_.tensor_copy(hi_q, zt[0]).then_inc(o_half[g], 1)
                            after(dve, o_half[g], 3 * b + 3)
                            v_.tensor_tensor(lo_q, zt[0], hi_q, ALU.subtract).then_inc(o_q[g], 1)
                            with dve.Fori(0, TB) as k:
                                n = b * TB + k
                                after(dve, o_s[g], n + 1)
                                v_.tensor_tensor(zt[0], zt[0], pr[0], ALU.max).then_inc(o_max[g], 1)
                                after(dve, o_max[g], n + 1)
                                dve.wait_ge(o_ld[g], 16 * (n + 1))
                                v_.scalar_tensor_tensor(pr[0], adjb[0][:], codes[:, ds(r, 1)], zt[0],
                                                        ALU.is_equal, ALU.mult).then_inc(o_p[g], 1)
                                after(dve, o_t[g], n + 1)
                                after(dve, o_v[g], n)
                                v_.tensor_copy(pT[0], tP[0][:, :]).then_inc(o_c[g], 1)
                                after(dve, o_v[g], n + 1)
                                xt_ = x[:, ds((g * TG + bb * TB + k) * D, D)]
                                v_.tensor_tensor(xt_, vP[0], xt_, ALU.add).then_inc(o_x[g], 1)
                    after(dve, o_x[g], 3 * TG)
                    with dve.Fori(0, BG) as w:
                        for i in range(TB):
                            v_.bn_stats(st8["dense"][:, i, :],
                                        x[:, ds((g * TG + TB * w + i) * D, D)]).then_inc(o_m[g], 1)
                        after(dve, o_m[g], (2 * TB + 1) * w + TB)
                        dve.nop(nofuse=True)
                        for i in range(TB):
                            v_.bn_aggr(ag8["dense"][:, 2 * i:2 * i + 2], st8["dense"][:, i, :]).then_inc(o_m[g], 1)
                        after(dve, o_m[g], (2 * TB + 1) * w + 2 * TB)
                        v_.tensor_copy(mv["dense"][:, ds(2 * TB * w, 2 * TB)], ag8["dense"][:]).then_inc(o_m[g], 1)
                        after(dve, o_m[g], (2 * TB + 1) * (w + 1))

            def low(w, i, kind, l, g):
                m = M0[kind, l, g] + R * w + i
                n = C[l] * SPAN
                after(dve, hhi_rdy, m + 1)
                v_.tensor_tensor(hs[i][:, 4 * SPAN:4 * SPAN + n], hf[i % 2][:, 0:n], hs[i][:, 0:n],
                                 ALU.subtract).then_inc(hs_rdy, 1)

            def biased(i, bias):
                return v_.tensor_tensor(ysb[i].rearrange("p (s d) -> p s d", s=ST),
                                        yP[i % 2].rearrange("p (s d) -> p s d", s=ST),
                                        bias.rearrange("p (o d) -> p o d", o=1).to_broadcast([P, ST, D]), ALU.add)

            def dense(l, g):
                meet(dve, "dense", l, g)
                q = q_of(l, g)
                after(dve, st_c["dense"], MEASURED["dense", l, g])
                scales(2 * q + 2, "dense")
                def normalised(w, i):
                    u = R * w + i
                    for s in range(ST):
                        t = ST * u + s
                        last = v_.tensor_scalar(xf[i][:, s * D:(s + 1) * D], x[:, ds((g * TG + t) * D, D)],
                                                mv["dense"][:, ds(2 * t, 1)], rstd[:, ds(t, 1)], ALU.subtract,
                                                ALU.mult)
                    last.then_inc(norm_rdy, 1)

                def rows_low(w, i):
                    after(dve, xhi_rdy, q * US + R * w + i + 1)
                    f3 = xf[i].rearrange("p (s d) -> p s d", s=ST)
                    b3 = xb[i].rearrange("p (s c) -> p s c", s=ST)
                    v_.tensor_tensor(b3[:, :, D:2 * D], f3, b3[:, :, 0:D], ALU.subtract).then_inc(xb_made, 1)

                def scores(w, i):
                    u = R * w + i
                    after(dve, lgp_rdy, q * US + u + 1)
                    v_.tensor_tensor(lg[:, ds(u * ST * E, ST * E)], lgP[i % 2],
                                     gateb[:, l].rearrange("p s e -> p (s e)"), ALU.add).then_inc(lg_rdy, 1)

                def residual(w, i):
                    u = R * w + i
                    r = g * US + u
                    after(dve, yp_rdy, M0["dense", l, g] + u + 1)
                    biased(i, b2b[0][:, SH * D:(SH + 1) * D]).then_inc(r_step, 1)
                    after(dve, r_step, r + 1)
                    xu = x[:, ds((g * TG + ST * u) * D, ST * D)]
                    v_.tensor_tensor(xu, xu, ysb[i], ALU.add)

                def step(w, i, has):
                    if l == 0 and has(-1):
                        low(*shifted(w, i, -1), "dense", l, g)
                    if has(1):
                        scores(*shifted(w, i, 1))
                    if has(4):
                        normalised(*shifted(w, i, 4))
                    if has(3):
                        rows_low(*shifted(w, i, 3))
                    if l == 0 and has(-2):
                        residual(*shifted(w, i, -2))
                for z in cum:
                    v_.memset(z[:, 0:PAD], 0.0)
                for z in blk:
                    v_.memset(z[:, 0:E], 0.0)
                for i in range(4):
                    normalised(0, i)
                for i in range(3):
                    rows_low(0, i)
                scores(0, 0)
                each_unit(dve, US, step, 4, 2 if l == 0 else 0)
                after(dve, lg_rdy, US * (q + 1))
                route(l, g)
                for i in range(R):
                    dve.wait_ge(xb_st[i], 16 * (1 + (q + 1) * US // R))

            def route(l, g):
                q = q_of(l, g)
                W = TG * E

                def te(a):
                    return a.rearrange("p (t e) -> p t e", e=E)

                def bc(a):
                    return a.rearrange("p (t o) -> p t o", o=1).to_broadcast([P, TG, E])
                rk = rank[:].rearrange("p (o e) -> p o e", o=1).to_broadcast([P, TG, E])
                src = lg
                for c in range(2):
                    link(v_.tensor_reduce(mx[c], te(src), AX.X, ALU.max))
                    link(v_.tensor_tensor(te(tm[0]), te(src), bc(mx[c]), ALU.is_equal))
                    link(v_.tensor_tensor(te(tm[0]), te(tm[0]), rk, ALU.mult))
                    link(v_.tensor_reduce(mx[3], te(tm[0]), AX.X, ALU.max))
                    link(v_.tensor_tensor(te(oh[c]), te(tm[0]), bc(mx[3]), ALU.is_equal))
                    if c == 0:
                        link(v_.scalar_tensor_tensor(tm[1], oh[0], NEG, lg, ALU.mult, ALU.add))
                        src = tm[1]
                v_.tensor_tensor(oh16, oh[0], oh[1], ALU.add).then_inc(route_rdy, 1)
                v_.tensor_tensor(mx[2], mx[1], mx[0], ALU.subtract).then_inc(w2_rdy, 1)
                dve.wait_ge(pos_rdy, q + 1)
                link(v_.tensor_copy(cum[0][:, PAD:], tP[1][:, 0:W]))
                a, b, d = 0, 1, E
                while d < W:
                    link(v_.tensor_tensor(cum[b][:, PAD:], cum[a][:, PAD:], cum[a][:, PAD - d:PAD + W - d],
                                          ALU.add))
                    a, b, d = b, a, 2 * d
                link(v_.tensor_scalar(nb_i[:], cum[a][:, PAD + W - E:], float(SPAN - 1), None, ALU.add))
                link(v_.tensor_scalar(nb_i[:], nb_i[:], SPAN.bit_length() - 1, None, ALU.arith_shift_right))
                link(v_.tensor_copy(blk[0][:, E:], nb_i[:]))
                s, r, d = 0, 1, 1
                while d < E:
                    link(v_.tensor_tensor(blk[r][:, E:], blk[s][:, E:], blk[s][:, E - d:2 * E - d], ALU.add))
                    s, r, d = r, s, 2 * d
                link(v_.tensor_scalar(first, blk[s][:, E - 1:2 * E - 1], float(SPAN), None, ALU.mult))
                link(v_.tensor_tensor(te(tm[0]), te(tP[0][:, 0:W]),
                                      first.rearrange("p (o e) -> p o e", o=1).to_broadcast([P, TG, E]), ALU.add))
                link(v_.tensor_tensor(tm[0], tm[0], cum[a][:, PAD - E:PAD + W - E], ALU.add))
                slv = slf.rearrange("p (t c) -> p t c", c=2)
                for c in range(2):
                    link(v_.tensor_tensor(tm[1], tm[0], oh[c], ALU.mult))
                    link(v_.tensor_reduce(slv[:, :, c], te(tm[1]), AX.X, ALU.add))
                if q >= 1:
                    dve.wait_ge(slot_st, 16 * q)
                v_.tensor_copy(sl[:], slf).then_inc(tbl_rdy, 1)
                nbv = blockno[:].rearrange("p (n o) -> p n o", o=1).to_broadcast([P, NB, E])
                bv = blk[s][:, E:].rearrange("p (o e) -> p o e", o=1).to_broadcast([P, NB, E])
                cv = cmpb.rearrange("p (n e) -> p n e", e=E)
                link(v_.tensor_tensor(cv, nbv, bv, ALU.is_ge))
                link(v_.tensor_reduce(bef, cv, AX.X, ALU.add))
                v_.tensor_scalar(be[g][:], bef[0:1, :], float(E - 1), None, ALU.min).then_inc(tbl_rdy, 1)
                dve.wait_ge(w2e_rdy, q + 1)
                wv = wgt[:, g * TG * 2:(g + 1) * TG * 2].rearrange("p (t c) -> p t c", c=2)
                link(v_.tensor_scalar(mx[0], mx[2], 1.0, None, ALU.add))
                link(v_.reciprocal(mx[1], mx[0]))
                link(v_.tensor_copy(wv[:, :, 0], mx[1]))
                link(v_.tensor_tensor(wv[:, :, 1], mx[1], mx[2], ALU.mult))

            def blocks(l, g):
                meet(dve, "blocks", l, g)
                q = q_of(l, g)
                dve.wait_ge(tbl_rdy, 2 * q + 2)

                def result(w, i):
                    u = R * w + i
                    e = expert_of(dve, g, u)
                    after(dve, yp_rdy, M0["blocks", l, g] + u + 1)
                    dve.wait_ge(ys_st[i], 16 * (1 + NRING[i] * q + w))
                    biased(i, b2b[l][:, ds(e * D, D)]).then_inc(y_out, 1)

                def step(w, i, has):
                    adding = combined and (not isinstance(w, int) or 1 <= w <= TG // R)
                    if adding:
                        add_first(*combined, w - 1, i)
                    if has(-1):
                        low(*shifted(w, i, -1), "blocks", l, g)
                    if adding:
                        add_second(*combined, w - 1, i)
                    if has(-2):
                        result(*shifted(w, i, -2))
                    if adding and l == 0:
                        measure_a("project", 1, combined[1], w - 1, i, R)
                        measure_b("project", 1, combined[1], w - 1, i, R)
                combined = COMBINED_IN.get(("blocks", l, g))
                each_unit(dve, NB, step, 0, 2)
                if combined:
                    after(dve, comb, TG * (q_of(*combined) + 1))
                for i in range(R):
                    dve.wait_ge(ys_st[i], 16 * (1 + NRING[i] * (q + 1)))

            def combine(l, g):
                if (l, g) in COMBINED_IN.values():
                    return
                with dve.Fori(0, TG // R) as w:
                    for i in range(R):
                        add_first(l, g, w, i)
                        add_second(l, g, w, i)
                after(dve, comb, TG * (q_of(l, g) + 1))

            order(project, gnn, relations, dense, blocks, combine)

        @block.tensor
        def _(pe):
            t_ = nc.tensor
            pe.wait_ge(c_ld, 16 * NC)
            pe.wait_ge(consts, NCONST)
            for l in range(2):
                n = NE[l] * C[l]
                t_.transpose(ps[0][:, 512 * l:512 * l + n], b1rows[l], ident[0:n, 0:n])
            t_.transpose(ps[1][:, 0:D], gw, ident[:])
            t_.matmul(ps[2][:, 0:2], gw, gacol[:], start=True, stop=True).then_inc(prep_pe, 1)

            def project(l, g):
                meet(pe, "project", l, g)
                q = q_of(l, g)
                if q == 0:
                    pe.wait_ge(prep_act, 4)
                    pe.wait_ge(prep_dve, 2)

                def turn(i, par):
                    n = q * QG + i
                    after(pe, xn4_rdy, n + 1)
                    after(pe, xT_rdy, n - 1)
                    for s in range(4):
                        last = t_.transpose(eP[:, 512 * par + s * P:512 * par + (s + 1) * P],
                                            xn4[par][:, s * D:(s + 1) * D], ident[:])
                    last.then_inc(xTp_rdy, 1)

                def multiply(i, par):
                    n = q * QG + i
                    after(pe, xT_rdy, n + 1)
                    after(pe, eb_used, n - 1)
                    after(pe, wh_used, n - 1)
                    t_.matmul(tP[par][:, 0:512], wa2b[:], xT4[par], start=True, stop=True).then_inc(ebP_rdy, 1)
                    for s in range(4):
                        t_.matmul(ps[3][:, 512 * par + s * D:512 * par + (s + 1) * D], xT4[par][:, s * P:(s + 1) * P],
                                  wcat[:], start=True, stop=True)
                        last = t_.matmul(tP[par][:, 512 + s:513 + s], xT4[par][:, s * P:(s + 1) * P],
                                         wa[:, 0:1], start=True, stop=True)
                    last.then_inc(whP_rdy, 1)
                def step(w, par, has):
                    if has(1):
                        turn(2 * w + par + 1, 1 - par)
                    if l == 0 and has(0):
                        multiply(2 * w + par, par)
                turn(0, 0)
                each_unit(pe, QG, step, 1, 0, 2)

            def scores_of(bb, k):
                i0 = (bb * TB + k) * P
                for c in range(N // 512):
                    j0 = bb * N + c * 512
                    o = eP[:, c * 512:(c + 1) * 512]
                    hi_q, lo_q = qT[:, ds(i0, P)], qT[:, ds(TG * P + i0, P)]
                    hi_k, lo_k = kT[:, ds(j0, 512)], kT[:, ds(TG * P + j0, 512)]
                    t_.matmul(o, hi_q, hi_k, start=True, stop=False)
                    t_.matmul(o, hi_q, lo_k, start=False, stop=False)
                    last = t_.matmul(o, lo_q, hi_k, start=False, stop=True)
                return last

            def turn_of(par):
                for j in range(TB):
                    last = t_.transpose(tP[par][:, j * P:(j + 1) * P], pr[par][:, j * P:(j + 1) * P], ident[:])
                return last

            def sum_of(par, bb, bias):
                for j in range(TB):
                    last = t_.matmul(vP[par], pT[par][:, j * P:(j + 1) * P], vals[:, ds((bb * TB + j) * D, D)],
                                     start=(j == 0), stop=(j == TB - 1 and not bias))
                if bias:
                    last = t_.matmul(vP[par], ones16[0:3, :], gbsplit[:], start=False, stop=True)
                return last

            def gnn(l, g):
                meet(pe, "gnn", l, g)
                q = q_of(l, g)

                def similar(n, bb, k):
                    after(pe, y_rdy, n)
                    scores_of(bb, k).then_inc(e_rdy, 1)

                def turn(n, k):
                    after(pe, p_rdy, n + 1)
                    after(pe, t_used, n - 1)
                    turn_of(k % 2).then_inc(t_rdy, 1)

                def sum_up(n, bb, k):
                    after(pe, t_used, n + 1)
                    after(pe, v_used, n - 1)
                    sum_of(k % 2, bb, l == 1).then_inc(v_rdy, 1)

                def step(bb, k, has):
                    n = (q * BG + bb) * TB + k
                    if l == 1 and has(1):
                        similar(n + 1, *shifted(bb, k, 1, TB))
                    if has(-1):
                        sum_up(n - 1, *shifted(bb, k, -1, TB))
                    if has(0):
                        turn(n, k)
                if l == 1:
                    similar(q * TG, 0, 0)
                each_unit(pe, TG, step, l, 1, TB)

            def relations(l, g):
                pe.wait_ge(oth_rdy, g + 1)
                t_.matmul(tP[0][0:1, 512:513], other16[:], ones16[:, 0:1], start=True,
                          stop=True).then_inc(othP_rdy, 1)
                pe.wait_ge(flag_rdy, g + 1)
                flag = pe.value_load(others[g][0:1, 0:1], min_val=0, max_val=P)
                with pe.If(flag > 0):
                    with pe.Fori(1, 4) as r:
                        with pe.Fori(0, BG) as bb:
                            b = (r - 1) * BG + bb
                            with pe.Fori(0, TB) as k:
                                n = b * TB + k
                                after(pe, o_q[g], b + 1)
                                after(pe, o_s[g], n)
                                scores_of(bb, k).then_inc(o_e[g], 1)
                                after(pe, o_p[g], n + 1)
                                after(pe, o_c[g], n)
                                turn_of(0).then_inc(o_t[g], 1)
                                after(pe, o_c[g], n + 1)
                                after(pe, o_x[g], n)
                                sum_of(0, bb, False).then_inc(o_v[g], 1)

            def turn_unit(w, i, kind, l, g):
                q, u = q_of(l, g), R * w + i
                if kind == "dense":
                    after(pe, lg_rdy, q * US + u - 1)
                    after(pe, xb_made, q * US + u + 1)
                else:
                    pe.wait_ge(xb_ld[i], 16 * (NRING[i] * q + w + 1))
                xp = xtP[i % 2].rearrange("p (h s q) -> p h s q", h=2, s=ST)
                for s in range(ST):
                    for h in range(2):
                        last = t_.transpose(xp[:, h, s, :], xb[i][:, (2 * s + h) * D:(2 * s + h + 1) * D],
                                            ident16[:])
                last.then_inc(xtp_rdy, 1)

            def route_unit(w, i, l, g):
                u = R * w + i
                after(pe, xt_rdy, U0["dense", l, g] + u + 1)
                for s in range(ST):
                    hi, lo = xt[i][:, s * P:(s + 1) * P], xt[i][:, SPAN + s * P:SPAN + (s + 1) * P]
                    o = lgP[i % 2][:, s * E:(s + 1) * E]
                    t_.matmul(o, hi, wrs[:, l, 0, :], start=True, stop=False)
                    t_.matmul(o, hi, wrs[:, l, 1, :], start=False, stop=False)
                    last = t_.matmul(o, lo, wrs[:, l, 0, :], start=False, stop=True)
                last.then_inc(lgp_rdy, 1)

            def up(w, i, kind, l, g, e):
                u = R * w + i
                after(pe, xt_rdy, U0[kind, l, g] + u + 1)
                f = F[l]
                for c in range(C[l]):
                    o = hP[i % 2][:, c * SPAN:(c + 1) * SPAN]
                    hi = w1sp[l][:, ds(e * 2 * f + c * P, P)]
                    lo = w1sp[l][:, ds(e * 2 * f + f + c * P, P)]
                    t_.matmul(o, hi, xt[i][:, 0:SPAN], start=True, stop=False)
                    t_.matmul(o, hi, xt[i][:, SPAN:2 * SPAN], start=False, stop=False)
                    last = t_.matmul(o, lo, xt[i][:, 0:SPAN], start=False, stop=True)
                last.then_inc(hp_rdy, 1)

            def down(w, i, kind, l, g, e):
                u = R * w + i
                after(pe, hs_rdy, M0[kind, l, g] + u + 1)
                for s in range(ST):
                    o = yP[i % 2][:, s * D:(s + 1) * D]
                    for c in range(C[l]):
                        at_ = e * C[l] * 2 * D + c * 2 * D
                        hi = hs[i][:, c * SPAN + s * P:c * SPAN + (s + 1) * P]
                        lo = hs[i][:, (4 + c) * SPAN + s * P:(4 + c) * SPAN + (s + 1) * P]
                        whi, wlo = w2sp[l][:, ds(at_, D)], w2sp[l][:, ds(at_ + D, D)]
                        t_.matmul(o, hi, whi, start=(c == 0), stop=False)
                        t_.matmul(o, lo, whi, start=False, stop=False)
                        last = t_.matmul(o, hi, wlo, start=False, stop=(c == C[l] - 1))
                last.then_inc(yp_rdy, 1)

            def through_experts(kind, l, g, n, expert):
                known = {}
                long = 2 * R if kind == "blocks" else R

                def step(w, i, has):
                    if i == 0:
                        known.clear()
                    own = w * (long // R) + i // R, i % R
                    if has(0) and (kind == "blocks" or l == 0):
                        known[i] = expert(long * w + i)
                        up(*own, kind, l, g, known[i])
                    if kind == "dense" and has(1):
                        route_unit(*shifted(*own, 1), l, g)
                    if has(2):
                        turn_unit(*shifted(*own, 2), kind, l, g)
                    if (kind == "blocks" or l == 0) and has(-2):
                        down(*shifted(*own, -2), kind, l, g,
                             known[i - 2] if i >= 2 else expert(long * w + i - 2))
                turn_unit(0, 0, kind, l, g)
                turn_unit(0, 1, kind, l, g)
                if kind == "dense":
                    route_unit(0, 0, l, g)
                each_unit(pe, n, step, 2, 2 if kind == "blocks" or l == 0 else 0, long)

            def dense(l, g):
                meet(pe, "dense", l, g)
                q = q_of(l, g)
                if q == 0:
                    pe.wait_ge(w_used, NPIECES)
                through_experts("dense", l, g, US, lambda u: SH)
                pe.wait_ge(route_rdy, q + 1)
                t_.matmul(tP[0][:, 0:TG * E], before[:], oh16, start=True, stop=True)
                t_.matmul(tP[1][:, 0:TG * E], ones16[:], oh16, start=True, stop=True).then_inc(pos_rdy, 1)

            def blocks(l, g):
                meet(pe, "blocks", l, g)
                pe.wait_ge(tbl_rdy, 2 * q_of(l, g) + 2)
                through_experts("blocks", l, g, NB,
                                lambda u: expert_of(pe, g, u))

            order(project, gnn, relations, dense, blocks, lambda l, g: None)


_INS = ["x", "adj", "L0_gnn_W", "L0_gnn_a", "L0_ffn_Wr", "L0_ffn_W1s", "L0_ffn_b1s", "L0_ffn_W2s", "L0_ffn_b2s",
        "L0_ffn_W1p", "L0_ffn_b1p", "L0_ffn_W2p", "L0_ffn_b2p", "L1_gnn_a0", "L1_gnn_a1", "L1_gnn_a2", "L1_gnn_a3",
        "L1_gnn_bias", "L1_ffn_Wg", "L1_ffn_bg", "L1_ffn_bias", "L1_ffn_W1", "L1_ffn_b1", "L1_ffn_W2", "L1_ffn_b2"]


def kernel(**inputs):
    import numpy as _np
    import concourse.bacc as _bacc
    from concourse import mybir as _mybir
    from concourse.bass_utils import run_bass_kernel_spmd as _run

    nc = _bacc.Bacc("TRN2", target_bir_lowering=False, num_devices=1)
    arrays, args = {}, []
    for name in _INS:
        a = _np.ascontiguousarray(inputs[name])
        arrays[f"in_{name}_dram"] = a
        args.append(nc.dram_tensor(f"in_{name}_dram", a.shape, _mybir.dt.from_np(a.dtype), kind="ExternalInput").ap())
    args.append(nc.dram_tensor("out_0_dram", inputs["x"].shape, _mybir.dt.float32, kind="ExternalOutput").ap())
    bass_two_layers_of_gnn_and_moe(nc, *args)
    r = _run(nc, [arrays], core_ids=[0])
    return r.results[0]["out_0_dram"]
```
